# Optimizing a Trainium2 kernel written in Bass

```python
import numpy as np
import jax
import jax.numpy as jnp

def _softmax(x, axis=-1):
    return jax.nn.softmax(x, axis=axis)

def _gelu(x):
    return jax.nn.gelu(x, approximate=True)

def _silu(x):
    return jax.nn.silu(x)

def _sigmoid(x):
    return jax.nn.sigmoid(x)

def _layernorm(x, axis=-1, eps=1e-05):
    m = jnp.mean(x, axis=axis, keepdims=True)
    v = jnp.var(x, axis=axis, keepdims=True)
    return (x - m) / jnp.sqrt(v + eps)

def _scatter_add(tgt, idx, src, axis=0):
    return tgt.at[idx].add(src)

def _segment_sum(src, seg, n):
    return jax.ops.segment_sum(src, seg, n)
kernel_name = 'mk_hybrid_d1_jaxref_r8_212249'

def setup_inputs(seed: int=0):
    np.random.seed(seed)
    _w = jnp.asarray

    def _L0_attn_a_setup():
        import jax, jax.numpy as jnp
        import numpy as np
        B, S, H = (1, 256, 128)
        INTER, K, DST, DTR = (256, 4, 16, 64)

        def _ssm(dA, dBu, C):
            xs = (jnp.moveaxis(dA, 1, 0), jnp.moveaxis(dBu, 1, 0), jnp.moveaxis(C, 1, 0))
            state0 = jnp.zeros(dA.shape[:1] + dA.shape[2:], dA.dtype)

            def step(state, inp):
                Ai, dBui, Ci = inp
                state = Ai * state + dBui
                y = jnp.einsum('bhd,bd->bh', state, Ci)
                return (state, y)
            _, ys = jax.lax.scan(step, state0, xs)
            return jnp.moveaxis(ys, 0, 1)
        key = jax.random.key(seed)
        ks = jax.random.split(key, 10)
        sc = 0.02
        return {'x': jax.random.normal(ks[0], (B, S, H), jnp.float32), 'W_in': jax.random.normal(ks[1], (H, 2 * INTER), jnp.float32) * sc, 'conv_w': jax.random.normal(ks[2], (K, 1, INTER), jnp.float32) * sc, 'conv_b': jax.random.normal(ks[3], (INTER,), jnp.float32) * sc, 'W_x': jax.random.normal(ks[4], (INTER, DTR + 2 * DST), jnp.float32) * sc, 'W_dt': jax.random.normal(ks[5], (DTR, INTER), jnp.float32) * sc, 'b_dt': jax.random.normal(ks[6], (INTER,), jnp.float32) * sc, 'A_log': jax.random.normal(ks[7], (INTER, DST), jnp.float32) * sc, 'D': jax.random.normal(ks[8], (INTER,), jnp.float32) * sc, 'W_out': jax.random.normal(ks[9], (INTER, H), jnp.float32) * sc}
    _L0_attn_a_in = _L0_attn_a_setup()

    def _L0_attn_b_setup():
        import jax, jax.numpy as jnp
        import numpy as np
        DIM = 128
        H = 8
        N = 32
        EXP = 2.0
        DC = 4
        KD = H * N
        VD = int(H * N * EXP)
        HV = VD // H
        B, T = (2, 256)
        EPS_NORM = 1e-06
        EPS_RMS = 1e-05

        def _xavier(key, shape):
            fan_out, fan_in = shape
            limit = float(np.sqrt(6.0 / (fan_in + fan_out)))
            return jax.random.uniform(key, shape, jnp.float32, -limit, limit)

        def _dwconv_causal(u, w):
            y = jax.lax.conv_general_dilated(u.transpose(0, 2, 1), w, window_strides=(1,), padding=[(w.shape[-1] - 1, 0)], feature_group_count=w.shape[0], dimension_numbers=('NCH', 'OIH', 'NCH'))
            return y.transpose(0, 2, 1)

        def _e88_forward(x, Wq, Wk, Wv, Wa, A_log, dt_bias, q_conv_w, k_conv_w, v_conv_w, Wg, Wo, o_norm_w):
            b, t, d = x.shape
            h = A_log.shape[0]
            n = Wq.shape[0] // h
            hv = Wv.shape[0] // h
            silu = jax.nn.silu
            q = silu(_dwconv_causal(x @ Wq.T, q_conv_w))
            k = silu(_dwconv_causal(x @ Wk.T, k_conv_w))
            v = silu(_dwconv_causal(x @ Wv.T, v_conv_w))
            g_dec = -jnp.exp(A_log) * jax.nn.softplus(x @ Wa.T + dt_bias)
            decay = jnp.exp(g_dec)
            q = q.reshape(b, t, h, n)
            k = k.reshape(b, t, h, n)
            v = v.reshape(b, t, h, hv)
            kT = k.transpose(1, 0, 2, 3)
            qT = q.transpose(1, 0, 2, 3)
            vT = v.transpose(1, 0, 2, 3)
            dT = decay.transpose(1, 0, 2)

            def step(S, inp):
                k_t, v_t, q_t, d_t = inp
                kn = k_t / (jnp.linalg.norm(k_t, axis=-1, keepdims=True) + EPS_NORM)
                qn = q_t / (jnp.linalg.norm(q_t, axis=-1, keepdims=True) + EPS_NORM)
                retrieved = jnp.einsum('bhnv,bhn->bhv', S, kn)
                delta = v_t - retrieved
                S = jnp.tanh(d_t[..., None, None] * S + kn[..., None] * delta[..., None, :])
                Sq = jnp.einsum('bhnv,bhn->bhv', S, qn)
                out = Sq * (Sq * jax.nn.sigmoid(Sq))
                return (S, out)
            S0 = jnp.zeros((b, h, n, hv), x.dtype)
            S_final, outs = jax.lax.scan(step, S0, (kT, vT, qT, dT))
            out = outs.transpose(1, 0, 2, 3)
            gate = (x @ Wg.T).reshape(b, t, h, hv)
            rms = jax.lax.rsqrt(jnp.mean(out * out, axis=-1, keepdims=True) + EPS_RMS)
            out = out * rms * o_norm_w * jax.nn.sigmoid(gate)
            y = out.reshape(b, t, h * hv) @ Wo.T
            return (y, S_final)

        def _reference_tuple_inner(x, Wq, Wk, Wv, Wa, A_log, dt_bias, q_conv_w, k_conv_w, v_conv_w, Wg, Wo, o_norm_w):
            return _e88_forward(x, Wq, Wk, Wv, Wa, A_log, dt_bias, q_conv_w, k_conv_w, v_conv_w, Wg, Wo, o_norm_w)
        key = jax.random.key(seed)
        ks = jax.random.split(key, 14)
        x = jax.random.normal(ks[0], (B, T, DIM), jnp.float32)
        Wq = _xavier(ks[1], (KD, DIM))
        Wk = _xavier(ks[2], (KD, DIM))
        Wv = _xavier(ks[3], (VD, DIM))
        Wa = _xavier(ks[4], (H, DIM))
        Wg = _xavier(ks[5], (VD, DIM))
        Wo = _xavier(ks[6], (DIM, VD))
        A = jax.random.uniform(ks[7], (H,), jnp.float32, 0.01, 16.0)
        A_log = jnp.log(A)
        dt = jnp.exp(jax.random.uniform(ks[8], (H,), jnp.float32) * (np.log(0.1) - np.log(0.001)) + np.log(0.001))
        dt = jnp.clip(dt, 0.0001)
        dt_bias = dt + jnp.log(-jnp.expm1(-dt))
        q_conv_w = jax.random.normal(ks[9], (KD, 1, DC), jnp.float32) * 0.1
        k_conv_w = jax.random.normal(ks[10], (KD, 1, DC), jnp.float32) * 0.1
        v_conv_w = jax.random.normal(ks[11], (VD, 1, DC), jnp.float32) * 0.1
        o_norm_w = jnp.ones((HV,), jnp.float32)
        return {'x': x, 'Wq': Wq, 'Wk': Wk, 'Wv': Wv, 'Wa': Wa, 'A_log': A_log, 'dt_bias': dt_bias, 'q_conv_w': q_conv_w, 'k_conv_w': k_conv_w, 'v_conv_w': v_conv_w, 'Wg': Wg, 'Wo': Wo, 'o_norm_w': o_norm_w}
    _L0_attn_b_in = _L0_attn_b_setup()

    def _L0_ffn_setup():
        import jax, jax.numpy as jnp
        import numpy as np
        D = 128
        H = 16
        HD = D // H
        L = 64
        E = 8
        B, T = (4, 256)
        EPS = 1e-06

        def _glorot(k, shape):
            fan_in, fan_out = (shape[-2], shape[-1])
            lim = np.sqrt(6.0 / (fan_in + fan_out)).astype(np.float32)
            return jax.random.uniform(k, shape, jnp.float32, -lim, lim)

        def _rmsnorm(x, gamma):
            return gamma * x * jax.lax.rsqrt(jnp.mean(x * x, axis=-1, keepdims=True) + EPS)
        key = jax.random.key(seed)
        ks = jax.random.split(key, 8)
        return {'x': jax.random.normal(ks[0], (B, T, D), jnp.float32), 'gamma1': jnp.ones((D,), jnp.float32), 'Wq': _glorot(ks[1], (D, D)), 'bq': jnp.zeros((D,), jnp.float32), 'Wdown': _glorot(ks[2], (D, L)), 'bdown': jnp.zeros((L,), jnp.float32), 'Wup': _glorot(ks[3], (L, 2 * D)), 'bup': jnp.zeros((2 * D,), jnp.float32), 'Wo': _glorot(ks[4], (D, D)), 'bo': jnp.zeros((D,), jnp.float32), 'gamma2': jnp.ones((D,), jnp.float32), 'Wg': _glorot(ks[5], (D, E)), 'bg': jnp.zeros((E,), jnp.float32), 'We': _glorot(ks[6], (E, D, D))}
    _L0_ffn_in = _L0_ffn_setup()
    _d = {'L0_attn_a_x': _L0_attn_a_in['x'], 'L0_attn_a_W_in': _L0_attn_a_in['W_in'], 'L0_attn_a_conv_w': _L0_attn_a_in['conv_w'], 'L0_attn_a_conv_b': _L0_attn_a_in['conv_b'], 'L0_attn_a_W_x': _L0_attn_a_in['W_x'], 'L0_attn_a_W_dt': _L0_attn_a_in['W_dt'], 'L0_attn_a_b_dt': _L0_attn_a_in['b_dt'], 'L0_attn_a_A_log': _L0_attn_a_in['A_log'], 'L0_attn_a_D': _L0_attn_a_in['D'], 'L0_attn_a_W_out': _L0_attn_a_in['W_out'], 'L0_attn_b_Wq': _L0_attn_b_in['Wq'], 'L0_attn_b_Wk': _L0_attn_b_in['Wk'], 'L0_attn_b_Wv': _L0_attn_b_in['Wv'], 'L0_attn_b_Wa': _L0_attn_b_in['Wa'], 'L0_attn_b_A_log': _L0_attn_b_in['A_log'], 'L0_attn_b_dt_bias': _L0_attn_b_in['dt_bias'], 'L0_attn_b_q_conv_w': _L0_attn_b_in['q_conv_w'], 'L0_attn_b_k_conv_w': _L0_attn_b_in['k_conv_w'], 'L0_attn_b_v_conv_w': _L0_attn_b_in['v_conv_w'], 'L0_attn_b_Wg': _L0_attn_b_in['Wg'], 'L0_attn_b_Wo': _L0_attn_b_in['Wo'], 'L0_attn_b_o_norm_w': _L0_attn_b_in['o_norm_w'], 'L0_ffn_gamma1': _L0_ffn_in['gamma1'], 'L0_ffn_Wq': _L0_ffn_in['Wq'], 'L0_ffn_bq': _L0_ffn_in['bq'], 'L0_ffn_Wdown': _L0_ffn_in['Wdown'], 'L0_ffn_bdown': _L0_ffn_in['bdown'], 'L0_ffn_Wup': _L0_ffn_in['Wup'], 'L0_ffn_bup': _L0_ffn_in['bup'], 'L0_ffn_Wo': _L0_ffn_in['Wo'], 'L0_ffn_bo': _L0_ffn_in['bo'], 'L0_ffn_gamma2': _L0_ffn_in['gamma2'], 'L0_ffn_Wg': _L0_ffn_in['Wg'], 'L0_ffn_bg': _L0_ffn_in['bg'], 'L0_ffn_We': _L0_ffn_in['We']}
    _x0 = _d['L0_attn_a_x']
    _d['L0_attn_a_x'] = jax.random.normal(jax.random.fold_in(jax.random.key(seed), 1), (16, 512, 128), dtype=_x0.dtype)
    del _x0
    return _d

def reference(L0_attn_a_x, L0_attn_a_W_in, L0_attn_a_conv_w, L0_attn_a_conv_b, L0_attn_a_W_x, L0_attn_a_W_dt, L0_attn_a_b_dt, L0_attn_a_A_log, L0_attn_a_D, L0_attn_a_W_out, L0_attn_b_Wq, L0_attn_b_Wk, L0_attn_b_Wv, L0_attn_b_Wa, L0_attn_b_A_log, L0_attn_b_dt_bias, L0_attn_b_q_conv_w, L0_attn_b_k_conv_w, L0_attn_b_v_conv_w, L0_attn_b_Wg, L0_attn_b_Wo, L0_attn_b_o_norm_w, L0_ffn_gamma1, L0_ffn_Wq, L0_ffn_bq, L0_ffn_Wdown, L0_ffn_bdown, L0_ffn_Wup, L0_ffn_bup, L0_ffn_Wo, L0_ffn_bo, L0_ffn_gamma2, L0_ffn_Wg, L0_ffn_bg, L0_ffn_We):

    def _L0_attn_a_ref(x, W_in, conv_w, conv_b, W_x, W_dt, b_dt, A_log, D, W_out):
        import jax, jax.numpy as jnp
        import numpy as np
        B, S, H = (1, 256, 128)
        INTER, K, DST, DTR = (256, 4, 16, 64)

        def _ssm(dA, dBu, C):
            xs = (jnp.moveaxis(dA, 1, 0), jnp.moveaxis(dBu, 1, 0), jnp.moveaxis(C, 1, 0))
            state0 = jnp.zeros(dA.shape[:1] + dA.shape[2:], dA.dtype)

            def step(state, inp):
                Ai, dBui, Ci = inp
                state = Ai * state + dBui
                y = jnp.einsum('bhd,bd->bh', state, Ci)
                return (state, y)
            _, ys = jax.lax.scan(step, state0, xs)
            return jnp.moveaxis(ys, 0, 1)
        proj = x @ W_in
        raw, gate = jnp.split(proj, 2, axis=-1)
        conv = jax.lax.conv_general_dilated(raw, conv_w, window_strides=(1,), padding=[(K - 1, 0)], dimension_numbers=('NWC', 'WIO', 'NWC'), feature_group_count=INTER)
        h = jax.nn.silu(conv + conv_b)
        ssm_p = h @ W_x
        ts, Bmat, C = jnp.split(ssm_p, [DTR, DTR + DST], axis=-1)
        dt = jax.nn.softplus(ts @ W_dt + b_dt)
        A = -jnp.exp(A_log)
        dA = jnp.exp(dt[..., None] * A)
        dBu = dt[..., None] * Bmat[:, :, None, :] * h[..., None]
        y = _ssm(dA, dBu, C)
        y = y + h * D
        y = y * jax.nn.silu(gate)
        return y @ W_out

    def _L0_attn_b_ref(x, Wq, Wk, Wv, Wa, A_log, dt_bias, q_conv_w, k_conv_w, v_conv_w, Wg, Wo, o_norm_w):
        import jax, jax.numpy as jnp
        import numpy as np
        DIM = 128
        H = 8
        N = 32
        EXP = 2.0
        DC = 4
        KD = H * N
        VD = int(H * N * EXP)
        HV = VD // H
        B, T = (2, 256)
        EPS_NORM = 1e-06
        EPS_RMS = 1e-05

        def _xavier(key, shape):
            fan_out, fan_in = shape
            limit = float(np.sqrt(6.0 / (fan_in + fan_out)))
            return jax.random.uniform(key, shape, jnp.float32, -limit, limit)

        def _dwconv_causal(u, w):
            y = jax.lax.conv_general_dilated(u.transpose(0, 2, 1), w, window_strides=(1,), padding=[(w.shape[-1] - 1, 0)], feature_group_count=w.shape[0], dimension_numbers=('NCH', 'OIH', 'NCH'))
            return y.transpose(0, 2, 1)

        def _e88_forward(x, Wq, Wk, Wv, Wa, A_log, dt_bias, q_conv_w, k_conv_w, v_conv_w, Wg, Wo, o_norm_w):
            b, t, d = x.shape
            h = A_log.shape[0]
            n = Wq.shape[0] // h
            hv = Wv.shape[0] // h
            silu = jax.nn.silu
            q = silu(_dwconv_causal(x @ Wq.T, q_conv_w))
            k = silu(_dwconv_causal(x @ Wk.T, k_conv_w))
            v = silu(_dwconv_causal(x @ Wv.T, v_conv_w))
            g_dec = -jnp.exp(A_log) * jax.nn.softplus(x @ Wa.T + dt_bias)
            decay = jnp.exp(g_dec)
            q = q.reshape(b, t, h, n)
            k = k.reshape(b, t, h, n)
            v = v.reshape(b, t, h, hv)
            kT = k.transpose(1, 0, 2, 3)
            qT = q.transpose(1, 0, 2, 3)
            vT = v.transpose(1, 0, 2, 3)
            dT = decay.transpose(1, 0, 2)

            def step(S, inp):
                k_t, v_t, q_t, d_t = inp
                kn = k_t / (jnp.linalg.norm(k_t, axis=-1, keepdims=True) + EPS_NORM)
                qn = q_t / (jnp.linalg.norm(q_t, axis=-1, keepdims=True) + EPS_NORM)
                retrieved = jnp.einsum('bhnv,bhn->bhv', S, kn)
                delta = v_t - retrieved
                S = jnp.tanh(d_t[..., None, None] * S + kn[..., None] * delta[..., None, :])
                Sq = jnp.einsum('bhnv,bhn->bhv', S, qn)
                out = Sq * (Sq * jax.nn.sigmoid(Sq))
                return (S, out)
            S0 = jnp.zeros((b, h, n, hv), x.dtype)
            S_final, outs = jax.lax.scan(step, S0, (kT, vT, qT, dT))
            out = outs.transpose(1, 0, 2, 3)
            gate = (x @ Wg.T).reshape(b, t, h, hv)
            rms = jax.lax.rsqrt(jnp.mean(out * out, axis=-1, keepdims=True) + EPS_RMS)
            out = out * rms * o_norm_w * jax.nn.sigmoid(gate)
            y = out.reshape(b, t, h * hv) @ Wo.T
            return (y, S_final)

        def _reference_tuple_inner(x, Wq, Wk, Wv, Wa, A_log, dt_bias, q_conv_w, k_conv_w, v_conv_w, Wg, Wo, o_norm_w):
            return _e88_forward(x, Wq, Wk, Wv, Wa, A_log, dt_bias, q_conv_w, k_conv_w, v_conv_w, Wg, Wo, o_norm_w)
        return _reference_tuple_inner(x, Wq, Wk, Wv, Wa, A_log, dt_bias, q_conv_w, k_conv_w, v_conv_w, Wg, Wo, o_norm_w)[0]

    def _L0_ffn_ref(x, gamma1, Wq, bq, Wdown, bdown, Wup, bup, Wo, bo, gamma2, Wg, bg, We):
        import jax, jax.numpy as jnp
        import numpy as np
        D = 128
        H = 16
        HD = D // H
        L = 64
        E = 8
        B, T = (4, 256)
        EPS = 1e-06

        def _glorot(k, shape):
            fan_in, fan_out = (shape[-2], shape[-1])
            lim = np.sqrt(6.0 / (fan_in + fan_out)).astype(np.float32)
            return jax.random.uniform(k, shape, jnp.float32, -lim, lim)

        def _rmsnorm(x, gamma):
            return gamma * x * jax.lax.rsqrt(jnp.mean(x * x, axis=-1, keepdims=True) + EPS)
        b, t = (x.shape[0], x.shape[1])
        h = _rmsnorm(x, gamma1)
        q = (h @ Wq + bq).reshape(b, t, H, HD)
        kv = ((h @ Wdown + bdown) @ Wup + bup).reshape(b, t, H, 2 * HD)
        k, v = jnp.split(kv, 2, axis=-1)
        att = jnp.einsum('bthd,btgd->bthg', q, k) / np.sqrt(HD).astype(np.float32)
        att = jax.nn.softmax(att, axis=-1)
        out = jnp.einsum('bthg,btgd->bthd', att, v).reshape(b, t, D)
        x = x + (out @ Wo + bo)
        h2 = _rmsnorm(x, gamma2)
        gate = jax.nn.softmax(h2 @ Wg + bg, axis=-1)
        combined = jnp.einsum('btd,edf,bte->btf', h2, We, gate)
        return x + combined
    x = L0_attn_a_x
    x = x + _L0_attn_a_ref(_layernorm(x, axis=-1), L0_attn_a_W_in, L0_attn_a_conv_w, L0_attn_a_conv_b, L0_attn_a_W_x, L0_attn_a_W_dt, L0_attn_a_b_dt, L0_attn_a_A_log, L0_attn_a_D, L0_attn_a_W_out)
    x = x + _L0_ffn_ref(_layernorm(x, axis=-1), L0_ffn_gamma1, L0_ffn_Wq, L0_ffn_bq, L0_ffn_Wdown, L0_ffn_bdown, L0_ffn_Wup, L0_ffn_bup, L0_ffn_Wo, L0_ffn_bo, L0_ffn_gamma2, L0_ffn_Wg, L0_ffn_bg, L0_ffn_We)
    x = x + _L0_attn_b_ref(_layernorm(x, axis=-1), L0_attn_b_Wq, L0_attn_b_Wk, L0_attn_b_Wv, L0_attn_b_Wa, L0_attn_b_A_log, L0_attn_b_dt_bias, L0_attn_b_q_conv_w, L0_attn_b_k_conv_w, L0_attn_b_v_conv_w, L0_attn_b_Wg, L0_attn_b_Wo, L0_attn_b_o_norm_w)
    x = x + _L0_ffn_ref(_layernorm(x, axis=-1), L0_ffn_gamma1, L0_ffn_Wq, L0_ffn_bq, L0_ffn_Wdown, L0_ffn_bdown, L0_ffn_Wup, L0_ffn_bup, L0_ffn_Wo, L0_ffn_bo, L0_ffn_gamma2, L0_ffn_Wg, L0_ffn_bg, L0_ffn_We)
    return x

_drawn_inputs = setup_inputs


def setup_inputs(seed=0):
    import zlib

    import numpy as np

    out = dict(_drawn_inputs(seed))
    spreads = {'L0_attn_b_o_norm_w': (1.0, 0.6),
     'L0_ffn_gamma1': (1.0, 0.2),
     'L0_ffn_bq': (0.0, 0.452),
     'L0_ffn_bdown': (0.0, 0.363),
     'L0_ffn_bup': (0.0, 0.357),
     'L0_ffn_bo': (0.0, 0.1),
     'L0_ffn_gamma2': (1.0, 0.2),
     'L0_ffn_bg': (0.0, 0.442)}
    factors = {'L0_attn_a_W_in': 8.0,
     'L0_attn_a_conv_w': 8.0,
     'L0_attn_a_conv_b': 8.0,
     'L0_attn_a_W_x': 8.0,
     'L0_attn_a_W_dt': 8.0,
     'L0_attn_a_b_dt': 8.0,
     'L0_attn_a_A_log': 8.0,
     'L0_attn_a_D': 8.0,
     'L0_attn_a_W_out': 8.0,
     'L0_attn_b_Wa': 3.727,
     'L0_attn_b_A_log': 2.96,
     'L0_attn_b_dt_bias': 3.193,
     'L0_attn_b_Wg': 4.874}
    for name, (base, spread) in spreads.items():
        noise = np.random.default_rng([zlib.crc32(name.encode()), seed]).standard_normal(out[name].shape)
        drawn = base * np.exp(spread * noise) if base else spread * noise
        out[name] = jnp.asarray(drawn.astype(out[name].dtype))
    for name, factor in factors.items():
        out[name] = (out[name] * factor).astype(out[name].dtype)
    return out
```

```python
import concourse.bass as bass
from concourse import mybir
from contextlib import ExitStack, contextmanager

F32 = mybir.dt.float32
BF16 = mybir.dt.bfloat16
ALU = mybir.AluOpType
ACT = mybir.ActivationFunctionType
AXX = mybir.AxisListType.X

P = 128
B = 16
T = 512
DM = 128
NT = T // P
LN_EPS = 1e-5

CH = 256
CT = CH // P
ST = 16
RK = 64
TAPS = 4
PAD = TAPS - 1

FH = 16
HD = DM // FH
LAT = 64
EX = 8
RMS_EPS = 1e-6

RH = 8
RN = 32
RV = 64
HH = 2
J = RH // HH
G = HH * B
NC = 4
CG = G // NC
CW = CG * RV
TCH = 16
PCH = 32
BLK = 8
GRP = 4


class Chain:

    def __init__(self, eng, sem, per=0):
        self.eng, self.sem, self.per, self.i, self.n = eng, sem, per, 0, 0

    def round(self, i):
        self.i, self.n = i, 0

    def __call__(self, ins):
        self.n += 1
        ins.then_inc(self.sem, 1)
        self.eng.wait_ge(self.sem, self.i * self.per + self.n)

    def end(self):
        assert self.n == self.per, self.n


def alloc(nc, ctx, tag=""):
    def sb(name, shape, dt=F32):
        return ctx.enter_context(nc.sbuf_tensor(tag + name, shape, dt))

    def sem(name):
        return nc.alloc_semaphore(tag + name)
    return sb, sem


@contextmanager
def layer_scope(nc):
    with nc.cleanup_on_exit(), ExitStack() as ctx:
        yield ctx


def bc(ap, *shape):
    return ap.broadcast_to(list(shape))


def diagonal(pool, chain, m, base=0, pattern=None, fill=1.0):
    chain(pool.affine_select(out=m, in_=m, compare_op=ALU.not_equal, fill=fill, base=base,
                             pattern=pattern, channel_multiplier=1))


def norm_statistics(nc, link, src, stats, mv):
    for tb in range(NT):
        last = nc.vector.bn_stats(stats[:, tb, :], src[:, tb, :])
    link(last)
    nc.vector.memset(stats[:, NT, :], 0.0)
    for tb in range(NT):
        last = nc.vector.bn_aggr(mv[:, tb, :], stats[:, tb, :])
    link(last)


def power(pool, dst, src, exponent):
    return pool.tensor_tensor(dst, src, exponent, ALU.pow)


def normalise(nc, src, dst, mv, rstd):
    for tb in range(NT):
        last = nc.vector.tensor_scalar(dst[:, tb, :], src[:, tb, :], mv[:, tb, 0:1], rstd[:, tb:tb + 1],
                                       ALU.subtract, ALU.mult)
    return last


def rows(x, b):
    return x[b].rearrange("(n p) d -> p n d", p=P)


def state_space(nc, x_in, x_out, w):
    RA, RB, RS, RP, RC = 4, 3, 4, 4, 3
    NK = ST * CT
    with layer_scope(nc) as ctx:
        sb, sem = alloc(nc, ctx)
        w_in = sb("ss_w_in", [P, 2 * CH])
        conv_w = sb("ss_conv_w", [P, TAPS, CH])
        w_tap = sb("ss_w_tap", [P, TAPS, CH])
        conv_b = sb("ss_conv_b", [P, CT])
        w_x = sb("ss_w_x", [P, CT, RK + 2 * ST])
        w_bc = sb("ss_w_bc", [P, CT, 3, 2 * ST])
        w_dt = sb("ss_w_dt", [RK, CH])
        b_dt = sb("ss_b_dt", [P, CT])
        a_log = sb("ss_a_log", [P, CT, ST])
        a_neg = sb("ss_a_neg", [P, CT, ST])
        d_skip = sb("ss_d", [P, CT])
        w_out = sb("ss_w_out", [P, CT, DM])
        ident = sb("ss_ident", [P, P])
        pick = sb("ss_pick", [96, 2 * ST, P], BF16)
        xt = sb("ss_xt", [P, NT, DM])
        xn = sb("ss_xn", [P, NT, DM])
        z = sb("ss_z", [P, NT, DM])
        stats = sb("ss_stats", [P, NT + 1, 6])
        mv = sb("ss_mv", [P, NT, 2])
        rstd = sb("ss_rstd", [P, NT])
        var = sb("ss_var", [P, NT])
        minus_half = sb("ss_minus_half", [P, NT])
        zT = sb("ss_zT", [P, PAD + T])
        u = sb("ss_u", [P, CT, T])
        e = sb("ss_e", [P, CT, T])
        h = sb("ss_h", [P, CT, T])
        eg = sb("ss_eg", [P, CT, T])
        gate = sb("ss_gate", [P, CT, T])
        ts = sb("ss_ts", [RK, T])
        dt = sb("ss_dt", [P, CT, T])
        dth = sb("ss_dth", [P, CT, T])
        bc_hi = sb("ss_bc_hi", [96, T], BF16)
        bc_mid = sb("ss_bc_mid", [96, T], BF16)
        bc_r1 = sb("ss_bc_r1", [96, T])
        bc3 = sb("ss_bc3", [96, T], BF16)
        dA = sb("ss_dA", [P, RA, T])
        dBu = sb("ss_dBu", [P, RB, T])
        state = sb("ss_state", [P, RS, T])
        c_all = sb("ss_c_all", [P, RC, T])
        prod = sb("ss_prod", [P, RP, T])
        yT = sb("ss_yT", [P, CT, T])
        ps = ctx.enter_context(nc.psum_tensor("ss_ps", [P, 8, 512], F32))

        weights_in, ident_ready, taps_ready = sem("ss_weights_in"), sem("ss_ident_ready"), sem("ss_taps_ready")
        a_exp, pool_step, dve_step = sem("ss_a_exp"), sem("ss_pool_step"), sem("ss_dve_step")
        x_loaded, z_ready, zT_ps, zT_ready = sem("ss_x_loaded"), sem("ss_z_ready"), sem("ss_zT_ps"), sem("ss_zT_ready")
        h_ps, gate_ps, u_ready, eh_ready = sem("ss_h_ps"), sem("ss_gate_ps"), sem("ss_u_ready"), sem("ss_eh_ready")
        eg_ready, h_ready, gate_ready = sem("ss_eg_ready"), sem("ss_h_ready"), sem("ss_gate_ready")
        ts_ps, bc_ps, ts_ready, bc_ready = sem("ss_ts_ps"), sem("ss_bc_ps"), sem("ss_ts_ready"), sem("ss_bc_ready")
        dt_ps, dtu_ready, dte_ready, ln_ready = sem("ss_dt_ps"), sem("ss_dtu_ready"), sem("ss_dte_ready"), sem("ss_ln_ready")
        dt_ready = sem("ss_dt_ready")
        b_ps, c_ps, c_copied, dA_ready = sem("ss_b_ps"), sem("ss_c_ps"), sem("ss_c_copied"), sem("ss_dA_ready")
        dBu_done, scan_done, prod_ready, y_acc = sem("ss_dBu_done"), sem("ss_scan_done"), sem("ss_prod_ready"), sem("ss_y_acc")
        yT_ready, out_ps, xn_ready, stored = sem("ss_yT_ready"), sem("ss_out_ps"), sem("ss_xn_ready"), sem("ss_stored")
        var_ready, rstd_ready = sem("ss_var_ready"), sem("ss_rstd_ready")
        NW = 9

        block = ctx.enter_context(nc.Block())

        @block.sync
        def _(sp):
            for dst, src in ((w_in[:, :], w["W_in"]),
                             (conv_w[:, :, :], bc(w["conv_w"].rearrange("k a c -> a k c"), P, TAPS, CH)),
                             (conv_b[:, :], w["conv_b"]),
                             (w_x[:, :, :], w["W_x"].rearrange("(c p) n -> p c n", p=P)),
                             (w_dt[:, :], w["W_dt"]),
                             (b_dt[:, :], w["b_dt"]),
                             (a_log[:, :, :], w["A_log"].rearrange("(c p) n -> p c n", p=P)),
                             (d_skip[:, :], w["D"]),
                             (w_out[:, :, :], w["W_out"].rearrange("(c p) n -> p c n", p=P))):
                sp.dma_start(dst, src).then_inc(weights_in, 16)
            with sp.Fori(0, B) as i:
                sp.wait_ge(xn_ready, i)
                sp.dma_start(xt[:, :, :], rows(x_in, i)).then_inc(x_loaded, 16)
                sp.wait_ge(xn_ready, i + 1)
                sp.dma_start(rows(x_out, i), xn[:, :, :]).then_inc(stored, 16)
            sp.wait_ge(stored, B * 16)

        @block.gpsimd
        def _(pool):
            link = Chain(pool, pool_step)
            link(pool.memset(ident[:, :], 0.0))
            diagonal(pool, link, ident[:, :], 0, [[-1, P]])
            link(pool.memset(pick[:, :, :], 0.0))
            for part in range(3):
                diagonal(pool, link, pick[:, :, :], -2 * ST * part, [[-1, 2 * ST], [0, P]])
            link(pool.memset(minus_half[:, :], -0.5))
            pool.memset(zT[:, 0:PAD], 0.0).then_inc(ident_ready, 1)
            with pool.Fori(0, B) as i:
                pool.wait_ge(var_ready, i + 1)
                power(pool, rstd[:, :], var[:, :], minus_half[:, :]).then_inc(rstd_ready, 1)
                for k in range(NK):
                    n, ct = k // CT, k % CT
                    pool.wait_ge(scan_done, i * NK + k + 1)
                    pool.wait_ge(c_copied, i * ST + n + 1)
                    if k >= RP:
                        pool.wait_ge(y_acc, i * NK + k - RP + 1)
                    pool.tensor_tensor(prod[:, k % RP, :], state[:, k % RS, :], c_all[:, n % RC, :],
                                       ALU.mult).then_inc(prod_ready, 1)

        @block.scalar
        def _(act):
            act.wait_ge(weights_in, NW * 16)
            act.activation(a_neg[:, :, :], a_log[:, :, :], ACT.Exp).then_inc(a_exp, 1)
            with act.Fori(0, B) as i:
                act.wait_ge(zT_ps, i + 1)
                act.activation(zT[:, PAD:PAD + T], ps[:, 0, :], ACT.Copy).then_inc(zT_ready, 1)
                act.wait_ge(u_ready, i + 1)
                act.activation(e[:, :, :], u[:, :, :], ACT.Exp, scale=-1.0).then_inc(eh_ready, 1)
                act.wait_ge(gate_ps, i + 1)
                act.activation(eg[:, :, :], ps[:, 3:5, :], ACT.Exp, scale=-1.0).then_inc(eg_ready, 1)
                act.wait_ge(ts_ps, i + 1)
                act.activation(ts[:, :], ps[0:RK, 7, :], ACT.Copy).then_inc(ts_ready, 1)
                act.wait_ge(dtu_ready, i + 1)
                act.activation(e[:, :, :], eg[:, :, :], ACT.Exp, scale=-1.0).then_inc(dte_ready, 1)
                act.wait_ge(dte_ready, i + 1)
                act.activation(e[:, :, :], e[:, :, :], ACT.Ln, bias=1.0).then_inc(ln_ready, 1)
                act.wait_ge(dt_ready, i + 1)
                for n in range(ST):
                    for ct in range(CT):
                        k = n * CT + ct
                        if k >= RA:
                            act.wait_ge(scan_done, i * NK + k - RA + 1)
                        act.activation(dA[:, k % RA, :], dt[:, ct, :], ACT.Exp,
                                       scale=a_neg[:, ct, n:n + 1]).then_inc(dA_ready, 1)
                    act.wait_ge(c_ps, i * ST + n + 1)
                    if n >= RC:
                        act.wait_ge(prod_ready, i * NK + (n - RC + 1) * CT)
                    act.activation(c_all[:, n % RC, :], ps[:, 5 + n % 2, :], ACT.Copy).then_inc(c_copied, 1)

        @block.vector
        def _(dve):
            dve.wait_ge(weights_in, NW * 16)
            nc.vector.tensor_tensor(w_tap[:, :, :], bc(w_in[:, 0:CH].unsqueeze(1), P, TAPS, CH), conv_w[:, :, :], ALU.mult)
            for rep in range(3):
                nc.vector.tensor_copy(w_bc[:, :, rep, :], w_x[:, :, RK:RK + 2 * ST])
            dve.wait_ge(a_exp, 1)
            nc.vector.tensor_scalar(a_neg[:, :, :], a_neg[:, :, :], -1.0, None, ALU.mult).then_inc(taps_ready, 1)
            link = Chain(dve, dve_step, 12)
            with dve.Fori(0, B) as i:
                link.round(i)
                dve.wait_ge(x_loaded, i * 16 + 16)
                norm_statistics(nc, link, xt, stats, mv)
                nc.vector.tensor_scalar(var[:, :], mv[:, :, 1], LN_EPS, None, ALU.add).then_inc(var_ready, 1)
                dve.wait_ge(rstd_ready, i + 1)
                normalise(nc, xt, z, mv, rstd).then_inc(z_ready, 1)
                dve.wait_ge(h_ps, i + 1)
                for ct in range(CT):
                    last = nc.vector.tensor_scalar(u[:, ct, :], ps[:, 1 + ct, :], conv_b[:, ct:ct + 1], None, ALU.add)
                last.then_inc(u_ready, 1)
                dve.wait_ge(eh_ready, i + 1)
                link(nc.vector.tensor_scalar(h[:, :, :], e[:, :, :], 1.0, None, ALU.add))
                link(nc.vector.reciprocal(h[:, :, :], h[:, :, :]))
                nc.vector.tensor_tensor(h[:, :, :], h[:, :, :], u[:, :, :], ALU.mult).then_inc(h_ready, 1)
                dve.wait_ge(eg_ready, i + 1)
                link(nc.vector.tensor_scalar(gate[:, :, :], eg[:, :, :], 1.0, None, ALU.add))
                link(nc.vector.reciprocal(gate[:, :, :], gate[:, :, :]))
                nc.vector.tensor_tensor(gate[:, :, :], gate[:, :, :], ps[:, 3:5, :], ALU.mult).then_inc(gate_ready, 1)
                dve.wait_ge(bc_ps, i + 1)
                link(nc.vector.tensor_copy(bc_hi[:, :], ps[0:96, 0, :]))
                link(nc.vector.tensor_tensor(bc_r1[:, :], ps[0:96, 0, :], bc_hi[:, :], ALU.subtract))
                link(nc.vector.tensor_copy(bc_mid[:, :], bc_r1[:, :]))
                nc.vector.tensor_copy(bc3[0:32, :], bc_hi[0:32, :])
                nc.vector.tensor_copy(bc3[32:64, :], bc_mid[32:64, :])
                nc.vector.tensor_tensor(bc3[64:96, :], bc_r1[64:96, :], bc_mid[64:96, :],
                                        ALU.subtract).then_inc(bc_ready, 1)
                dve.wait_ge(dt_ps, i + 1)
                for ct in range(CT):
                    last = nc.vector.tensor_scalar(u[:, ct, :], ps[:, 5 + ct, :], b_dt[:, ct:ct + 1], None, ALU.add)
                link(last)
                nc.vector.scalar_tensor_tensor(out=eg[:, :, :], in0=u[:, :, :], scalar=-1.0, in1=u[:, :, :],
                                               op0=ALU.mult, op1=ALU.max).then_inc(dtu_ready, 1)
                dve.wait_ge(ln_ready, i + 1)
                link(nc.vector.scalar_tensor_tensor(out=dt[:, :, :], in0=u[:, :, :], scalar=0.0, in1=e[:, :, :],
                                                    op0=ALU.max, op1=ALU.add))
                dve.wait_ge(h_ready, i + 1)
                nc.vector.tensor_tensor(dth[:, :, :], dt[:, :, :], h[:, :, :], ALU.mult).then_inc(dt_ready, 1)
                dve.wait_ge(dt_ready, i + 1)

                def inflow(k):
                    n, ct = k // CT, k % CT
                    dve.wait_ge(b_ps, i * ST + n + 1)
                    if k >= RB:
                        dve.wait_ge(scan_done, i * NK + k - RB + 1)
                    nc.vector.tensor_tensor(dBu[:, k % RB, :], dth[:, ct, :], ps[:, 3 + n % 2, :],
                                            ALU.mult).then_inc(dBu_done, 1)

                inflow(0)
                for k in range(NK):
                    if k + 1 < NK:
                        inflow(k + 1)
                    dve.wait_ge(dBu_done, i * NK + k + 1)
                    dve.wait_ge(dA_ready, i * NK + k + 1)
                    if k >= RS:
                        dve.wait_ge(prod_ready, i * NK + k - RS + 1)
                    nc.vector.tensor_tensor_scan(state[:, k % RS, :], dA[:, k % RA, :], dBu[:, k % RB, :], 0.0,
                                                 ALU.mult, ALU.add).then_inc(scan_done, 1)
                dve.wait_ge(y_acc, i * NK + NK)
                for ct in range(CT):
                    last = nc.vector.scalar_tensor_tensor(out=u[:, ct, :], in0=h[:, ct, :], scalar=d_skip[:, ct:ct + 1],
                                                          in1=ps[:, 1 + ct, :], op0=ALU.mult, op1=ALU.add)
                link(last)
                dve.wait_ge(gate_ready, i + 1)
                nc.vector.tensor_tensor(yT[:, :, :], u[:, :, :], gate[:, :, :], ALU.mult).then_inc(yT_ready, 1)
                dve.wait_ge(out_ps, i + 1)
                dve.wait_ge(stored, i * 16)
                nc.vector.tensor_tensor(xn[:, :, :], xt[:, :, :],
                                        ps[:, 0, :].rearrange("p (n d) -> p n d", n=NT), ALU.add).then_inc(xn_ready, 1)
                link.end()

        @block.tensor
        def _(pe):
            pe.wait_ge(ident_ready, 1)
            pe.wait_ge(taps_ready, 1)
            pe.wait_ge(weights_in, NW * 16)
            with pe.Fori(0, B) as i:
                pe.wait_ge(z_ready, i + 1)
                pe.wait_ge(xn_ready, i)
                for tb in range(NT):
                    last = nc.tensor.transpose(ps[:, 0, tb * P:(tb + 1) * P], z[:, tb, :], ident[:, :])
                last.then_inc(zT_ps, 1)
                pe.wait_ge(zT_ready, i + 1)
                for ct in range(CT):
                    for tap in range(TAPS):
                        last = nc.tensor.matmul(ps[:, 1 + ct, :], w_tap[:, tap, ct * P:(ct + 1) * P],
                                                zT[:, tap:tap + T], start=(tap == 0), stop=(tap == TAPS - 1))
                last.then_inc(h_ps, 1)
                for ct in range(CT):
                    last = nc.tensor.matmul(ps[:, 3 + ct, :], w_in[:, CH + ct * P:CH + (ct + 1) * P],
                                            zT[:, PAD:PAD + T], start=True, stop=True)
                last.then_inc(gate_ps, 1)
                pe.wait_ge(h_ready, i + 1)
                for ct in range(CT):
                    last = nc.tensor.matmul(ps[0:RK, 7, :], w_x[:, ct, 0:RK], h[:, ct, :],
                                            start=(ct == 0), stop=(ct == CT - 1))
                last.then_inc(ts_ps, 1)
                for ct in range(CT):
                    last = nc.tensor.matmul(ps[0:96, 0, :], w_bc[:, ct, :, :].rearrange("p r n -> p (r n)"),
                                            h[:, ct, :], start=(ct == 0), stop=(ct == CT - 1))
                last.then_inc(bc_ps, 1)
                pe.wait_ge(ts_ready, i + 1)
                for ct in range(CT):
                    last = nc.tensor.matmul(ps[:, 5 + ct, :], w_dt[:, ct * P:(ct + 1) * P], ts[:, :],
                                            start=True, stop=True)
                last.then_inc(dt_ps, 1)
                pe.wait_ge(bc_ready, i + 1)
                pe.wait_ge(gate_ready, i + 1)
                pe.wait_ge(dtu_ready, i + 1)

                def add_state(n):
                    for ct in range(CT):
                        k = n * CT + ct
                        pe.wait_ge(prod_ready, i * NK + k + 1)
                        nc.tensor.matmul(ps[:, 1 + ct, :], ident[:, :], prod[:, k % RP, :],
                                         start=(n == 0), stop=(n == ST - 1)).then_inc(y_acc, 1)

                for n in range(ST):
                    if n >= 2:
                        pe.wait_ge(dBu_done, i * NK + (n - 1) * CT)
                    nc.tensor.matmul(ps[:, 3 + n % 2, :], pick[:, n, :], bc3[:, :],
                                     start=True, stop=True).then_inc(b_ps, 1)
                    if n >= 2:
                        pe.wait_ge(c_copied, i * ST + n - 1)
                    nc.tensor.matmul(ps[:, 5 + n % 2, :], pick[:, ST + n, :], bc3[:, :],
                                     start=True, stop=True).then_inc(c_ps, 1)
                    if n >= 2:
                        add_state(n - 2)
                add_state(ST - 2)
                add_state(ST - 1)
                pe.wait_ge(yT_ready, i + 1)
                for tb in range(NT):
                    for ct in range(CT):
                        last = nc.tensor.matmul(ps[:, 0, tb * P:(tb + 1) * P], yT[:, ct, tb * P:(tb + 1) * P],
                                                w_out[:, ct, :], start=(ct == 0), stop=(ct == CT - 1))
                last.then_inc(out_ps, 1)


def feed_forward(nc, tag, x_in, x_out, w):
    SCALE = 1.0 / float(HD) ** 0.5
    with layer_scope(nc) as ctx:
        sb, sem = alloc(nc, ctx, tag)
        ident = sb("ident", [P, P])
        wq, wdown = sb("wq", [P, DM]), sb("wdown", [P, LAT])
        wup = sb("wup", [LAT, 2 * DM])
        wo, wg, we = sb("wo", [P, DM]), sb("wg", [P, EX]), sb("we", [P, EX, DM])
        g1, g2, bdown = sb("g1", [P, 1]), sb("g2", [P, 1]), sb("bdown", [LAT, 1])
        b_q, b_up, bo, bg = sb("b_q", [P, DM]), sb("b_up", [P, 2 * DM]), sb("bo", [P, DM]), sb("bg", [P, EX])
        minus_half = sb("minus_half", [P, NT])
        xt, z, hn, xn = sb("xt", [P, NT, DM]), sb("z", [P, NT, DM]), sb("hn", [P, NT, DM]), sb("xn", [P, NT, DM])
        stats, mv = sb("stats", [P, NT + 1, 6]), sb("mv", [P, NT, 2])
        var, rstd, ms, r1 = sb("var", [P, NT]), sb("rstd", [P, NT]), sb("ms", [P, NT]), sb("r1", [P, NT])
        hT, down = sb("hT", [P, T]), sb("down", [LAT, T])
        q, kk, v = sb("q", [P, NT, DM]), sb("k", [P, NT, DM]), sb("v", [P, NT, DM])
        qk = sb("qk", [P, 2, HD, FH * FH])
        pv = sb("pv", [P, 2, FH, DM])
        top, s, tot = sb("top", [P, NT, FH]), sb("s", [P, NT, FH, FH]), sb("tot", [P, NT, FH])
        attn, attnT = sb("attn", [P, NT, DM]), sb("attnT", [P, T])
        x1, h2T = sb("x1", [P, NT, DM]), sb("h2T", [P, T])
        lg, lmax, gsum = sb("lg", [P, NT, EX]), sb("lmax", [P, NT]), sb("gsum", [P, NT])
        mix, comb = sb("mix", [P, EX, DM]), sb("comb", [P, NT, DM])
        ps = ctx.enter_context(nc.psum_tensor(tag + "ps", [P, 8, 512], F32))

        weights_in, pool_step, consts_ready = sem("weights_in"), sem("pool_step"), sem("consts_ready")
        dve_step = sem("dve_step")
        x_loaded, var_ready, rstd_ready = sem("x_loaded"), sem("var_ready"), sem("rstd_ready")
        h_ready, hT_ps, hT_ready = sem("h_ready"), sem("hT_ps"), sem("hT_ready")
        qd_ps, down_ready, kv_ps, qkv_ready = sem("qd_ps"), sem("down_ready"), sem("kv_ps"), sem("qkv_ready")
        qk_ready, s_ps, s_ready, p_ready, pv_ready, attn_ready = sem("qk_ready"), sem("s_ps"), sem("s_ready"), sem("p_ready"), sem("pv_ready"), sem("attn_ready")
        o_done, attnT_ps, attnT_ready = sem("o_done"), sem("attnT_ps"), sem("attnT_ready")
        wo_ps, h2_ready, h2T_ps, h2T_ready = sem("wo_ps"), sem("h2_ready"), sem("h2T_ps"), sem("h2T_ready")
        lg_ps, lg_ready, eg_ready, ex_ps, mixed, xn_ready, stored = sem("lg_ps"), sem("lg_ready"), sem("eg_ready"), sem("ex_ps"), sem("mixed"), sem("xn_ready"), sem("stored")

        block = ctx.enter_context(nc.Block())
        loads = [(wq[:, :], w["Wq"]), (wdown[:, :], w["Wdown"]), (wup[:, :], w["Wup"]), (wo[:, :], w["Wo"]),
                 (wg[:, :], w["Wg"]), (we[:, :, :], w["We"].rearrange("e d f -> d e f")),
                 (g1[:, :], w["gamma1"]), (g2[:, :], w["gamma2"]), (bdown[:, :], w["bdown"]),
                 (b_q[:, :], bc(w["bq"], P, DM)), (b_up[:, :], bc(w["bup"], P, 2 * DM)),
                 (bo[:, :], bc(w["bo"], P, DM)), (bg[:, :], bc(w["bg"], P, EX))]
        NW = len(loads)

        def heads(ap):
            return ap.rearrange("p (h d) -> p h d", d=HD)

        @block.sync
        def _(sp):
            for dst, src in loads:
                sp.dma_start(dst, src).then_inc(weights_in, 16)
            with sp.Fori(0, B) as i:
                sp.wait_ge(xn_ready, i)
                sp.dma_start(xt[:, :, :], rows(x_in, i)).then_inc(x_loaded, 16)
                sp.wait_ge(xn_ready, i + 1)
                sp.dma_start(rows(x_out, i), xn[:, :, :]).then_inc(stored, 16)
            sp.wait_ge(stored, B * 16)

        @block.gpsimd
        def _(pool):
            link = Chain(pool, pool_step)
            link(pool.memset(ident[:, :], 0.0))
            diagonal(pool, link, ident[:, :], 0, [[-1, P]])
            pool.memset(minus_half[:, :], -0.5).then_inc(consts_ready, 1)
            pool.wait_ge(consts_ready, 1)
            with pool.Fori(0, B) as i:
                pool.wait_ge(var_ready, i * 3 + 1)
                power(pool, rstd[:, :], var[:, :], minus_half[:, :]).then_inc(rstd_ready, 1)
                pool.wait_ge(var_ready, i * 3 + 2)
                power(pool, r1[:, :], ms[:, :], minus_half[:, :]).then_inc(rstd_ready, 1)
                pool.wait_ge(qkv_ready, i + 1)
                for tb in range(NT):
                    pool.wait_ge(p_ready, i * NT + tb + 1)
                    if tb >= 2:
                        pool.wait_ge(o_done, i * NT + tb - 1)
                    pool.tensor_tensor(pv[:, tb % 2, :, :].rearrange("p g (h d) -> p g h d", d=HD),
                                       bc(s[:, tb, :, :].rearrange("p h g -> p g h").unsqueeze(3), P, FH, FH, HD),
                                       bc(heads(v[:, tb, :]).unsqueeze(2), P, FH, FH, HD),
                                       ALU.mult).then_inc(pv_ready, 1)
                pool.wait_ge(var_ready, i * 3 + 3)
                power(pool, r1[:, :], ms[:, :], minus_half[:, :]).then_inc(rstd_ready, 1)

        @block.scalar
        def _(act):
            act.wait_ge(weights_in, NW * 16)
            with act.Fori(0, B) as i:
                act.wait_ge(hT_ps, i + 1)
                act.activation(hT[:, :], ps[:, 4, :], ACT.Copy, scale=g1[:, :]).then_inc(hT_ready, 1)
                act.wait_ge(qd_ps, i + 1)
                act.activation(down[:, :], ps[0:LAT, 0, :], ACT.Identity, bias=bdown[:, :]).then_inc(down_ready, 1)
                for tb in range(NT):
                    act.wait_ge(s_ready, i * NT + tb + 1)
                    act.activation(s[:, tb, :, :], s[:, tb, :, :], ACT.Exp, scale=SCALE).then_inc(p_ready, 1)
                act.wait_ge(attnT_ps, i + 1)
                act.activation(attnT[:, :], ps[:, 3, :], ACT.Copy).then_inc(attnT_ready, 1)
                act.wait_ge(h2T_ps, i + 1)
                act.activation(h2T[:, :], ps[:, 5, :], ACT.Copy, scale=g2[:, :]).then_inc(h2T_ready, 1)
                act.wait_ge(lg_ready, i + 1)
                act.activation(lg[:, :, :], lg[:, :, :], ACT.Exp).then_inc(eg_ready, 1)

        @block.vector
        def _(dve):
            dve.wait_ge(weights_in, NW * 16)
            link = Chain(dve, dve_step, 33)
            with dve.Fori(0, B) as i:
                link.round(i)
                dve.wait_ge(x_loaded, i * 16 + 16)
                norm_statistics(nc, link, xt, stats, mv)
                nc.vector.tensor_scalar(var[:, :], mv[:, :, 1], LN_EPS, None, ALU.add).then_inc(var_ready, 1)
                dve.wait_ge(rstd_ready, i * 3 + 1)
                link(normalise(nc, xt, z, mv, rstd))
                link(nc.vector.tensor_tensor(ms[:, :], rstd[:, :], rstd[:, :], ALU.mult))
                link(nc.vector.tensor_tensor(ms[:, :], ms[:, :], mv[:, :, 1], ALU.mult))
                nc.vector.tensor_scalar(ms[:, :], ms[:, :], RMS_EPS, None, ALU.add).then_inc(var_ready, 1)
                dve.wait_ge(rstd_ready, i * 3 + 2)
                nc.vector.tensor_tensor(hn[:, :, :], z[:, :, :], bc(r1[:, :].unsqueeze(2), P, NT, DM),
                                        ALU.mult).then_inc(h_ready, 1)
                dve.wait_ge(qd_ps, i + 1)
                nc.vector.tensor_tensor(q[:, :, :], ps[:, 5, :].rearrange("p (n d) -> p n d", n=NT),
                                        bc(b_q[:, :].unsqueeze(1), P, NT, DM), ALU.add)
                dve.wait_ge(kv_ps, i + 1)
                for a, dst in enumerate((kk, v)):
                    last = nc.vector.tensor_tensor(
                        dst[:, :, :].rearrange("p n (h d) -> p n h d", d=HD),
                        ps[:, 6:8, :].rearrange("p a (m h e d) -> p (a m) h e d", h=FH, e=2, d=HD)[:, :, :, a, :],
                        bc(b_up[:, :].rearrange("p (h e d) -> p h e d", e=2, d=HD)[:, :, a, :].unsqueeze(1), P, NT, FH, HD),
                        ALU.add)
                last.then_inc(qkv_ready, 1)
                dve.wait_ge(qkv_ready, i + 1)

                def scores(tb):
                    if tb >= 2:
                        dve.wait_ge(s_ps, i * NT + tb - 1)
                    nc.vector.tensor_tensor(qk[:, tb % 2, :, :].rearrange("p d (h g) -> p d h g", g=FH),
                                            bc(heads(q[:, tb, :]).rearrange("p h d -> p d h").unsqueeze(3), P, HD, FH, FH),
                                            bc(heads(kk[:, tb, :]).rearrange("p g d -> p d g").unsqueeze(2), P, HD, FH, FH),
                                            ALU.mult).then_inc(qk_ready, 1)

                def less_maximum(tb):
                    dve.wait_ge(s_ps, i * NT + tb + 1)
                    sc = ps[:, 1 + tb % 2, 0:256].rearrange("p (h g) -> p h g", g=FH)
                    link(nc.vector.tensor_reduce(out=top[:, tb, :], in_=sc, op=ALU.max, axis=AXX))
                    nc.vector.tensor_tensor(s[:, tb, :, :], sc, bc(top[:, tb, :].unsqueeze(2), P, FH, FH),
                                            ALU.subtract).then_inc(s_ready, 1)

                def weighted(tb):
                    dve.wait_ge(p_ready, i * NT + tb + 1)
                    link(nc.vector.tensor_reduce(out=tot[:, tb, :], in_=s[:, tb, :, :], op=ALU.add, axis=AXX))
                    link(nc.vector.reciprocal(tot[:, tb, :], tot[:, tb, :]))
                    dve.wait_ge(pv_ready, i * NT + tb + 1)
                    nc.vector.tensor_reduce(out=attn[:, tb, :], in_=pv[:, tb % 2, :, :].rearrange("p g c -> p c g"),
                                            op=ALU.add, axis=AXX).then_inc(o_done, 1)
                    dve.wait_ge(o_done, i * NT + tb + 1)
                    nc.vector.tensor_tensor(heads(attn[:, tb, :]), heads(attn[:, tb, :]),
                                            bc(tot[:, tb, :].unsqueeze(2), P, FH, HD), ALU.mult).then_inc(attn_ready, 1)

                scores(0)
                scores(1)
                less_maximum(0)
                for tb in range(NT):
                    if tb + 2 < NT:
                        scores(tb + 2)
                    if tb + 1 < NT:
                        less_maximum(tb + 1)
                    weighted(tb)
                dve.wait_ge(wo_ps, i + 1)
                link(nc.vector.tensor_tensor(x1[:, :, :], ps[:, 4, :].rearrange("p (n d) -> p n d", n=NT),
                                             z[:, :, :], ALU.add))
                link(nc.vector.tensor_tensor(x1[:, :, :], x1[:, :, :], bc(bo[:, :].unsqueeze(1), P, NT, DM), ALU.add))
                norm_statistics(nc, link, x1, stats, mv)
                link(nc.vector.tensor_tensor(ms[:, :], mv[:, :, 0], mv[:, :, 0], ALU.mult))
                link(nc.vector.tensor_tensor(ms[:, :], ms[:, :], mv[:, :, 1], ALU.add))
                nc.vector.tensor_scalar(ms[:, :], ms[:, :], RMS_EPS, None, ALU.add).then_inc(var_ready, 1)
                dve.wait_ge(rstd_ready, i * 3 + 3)
                nc.vector.tensor_tensor(hn[:, :, :], x1[:, :, :], bc(r1[:, :].unsqueeze(2), P, NT, DM),
                                        ALU.mult).then_inc(h2_ready, 1)
                dve.wait_ge(lg_ps, i + 1)
                link(nc.vector.tensor_tensor(lg[:, :, :], ps[:, 6, 0:NT * EX].rearrange("p (n e) -> p n e", n=NT),
                                             bc(bg[:, :].unsqueeze(1), P, NT, EX), ALU.add))
                link(nc.vector.tensor_reduce(out=lmax[:, :], in_=lg[:, :, :], op=ALU.max, axis=AXX))
                nc.vector.tensor_tensor(lg[:, :, :], lg[:, :, :], bc(lmax[:, :].unsqueeze(2), P, NT, EX),
                                        ALU.subtract).then_inc(lg_ready, 1)
                dve.wait_ge(eg_ready, i + 1)
                link(nc.vector.tensor_reduce(out=gsum[:, :], in_=lg[:, :, :], op=ALU.add, axis=AXX))
                link(nc.vector.reciprocal(gsum[:, :], gsum[:, :]))
                link(nc.vector.tensor_tensor(lg[:, :, :], lg[:, :, :], bc(gsum[:, :].unsqueeze(2), P, NT, EX), ALU.mult))
                link(nc.vector.tensor_tensor(x1[:, :, :], x1[:, :, :], xt[:, :, :], ALU.add))
                for tb in range(NT):
                    dve.wait_ge(ex_ps, i * NT + tb + 1)
                    nc.vector.tensor_tensor(mix[:, :, :], ps[:, 2 * (tb % 2):2 * (tb % 2) + 2, :].rearrange("p a (e f) -> p (a e) f", f=DM),
                                            bc(lg[:, tb, :].unsqueeze(2), P, EX, DM), ALU.mult).then_inc(mixed, 1)
                    dve.wait_ge(mixed, i * NT + tb + 1)
                    link(nc.vector.tensor_reduce(out=comb[:, tb, :], in_=mix[:, :, :].rearrange("p e f -> p f e"),
                                                 op=ALU.add, axis=AXX))
                dve.wait_ge(stored, i * 16)
                nc.vector.tensor_tensor(xn[:, :, :], x1[:, :, :], comb[:, :, :], ALU.add).then_inc(xn_ready, 1)
                link.end()

        @block.tensor
        def _(pe):
            pe.wait_ge(weights_in, NW * 16)
            pe.wait_ge(consts_ready, 1)
            with pe.Fori(0, B) as i:
                pe.wait_ge(h_ready, i + 1)
                for tb in range(NT):
                    last = nc.tensor.transpose(ps[:, 4, tb * P:(tb + 1) * P], hn[:, tb, :], ident[:, :])
                last.then_inc(hT_ps, 1)
                pe.wait_ge(hT_ready, i + 1)
                pe.wait_ge(mixed, i * NT)
                nc.tensor.matmul(ps[0:LAT, 0, :], wdown[:, :], hT[:, :], start=True, stop=True)
                for tb in range(NT):
                    last = nc.tensor.matmul(ps[:, 5, tb * P:(tb + 1) * P], hT[:, tb * P:(tb + 1) * P], wq[:, :],
                                            start=True, stop=True)
                last.then_inc(qd_ps, 1)
                pe.wait_ge(down_ready, i + 1)
                for tb in range(NT):
                    last = nc.tensor.matmul(ps[:, 6 + tb // 2, (tb % 2) * 256:(tb % 2) * 256 + 256],
                                            down[:, tb * P:(tb + 1) * P], wup[:, :], start=True, stop=True)
                last.then_inc(kv_ps, 1)
                for tb in range(NT):
                    pe.wait_ge(qk_ready, i * NT + tb + 1)
                    if tb >= 2:
                        pe.wait_ge(s_ready, i * NT + tb - 1)
                    for d in range(HD):
                        last = nc.tensor.matmul(ps[:, 1 + tb % 2, 0:256], ident[:, :],
                                                qk[:, tb % 2, d, :], start=(d == 0), stop=(d == HD - 1))
                    last.then_inc(s_ps, 1)
                pe.wait_ge(attn_ready, i * NT + NT)
                for tb in range(NT):
                    last = nc.tensor.transpose(ps[:, 3, tb * P:(tb + 1) * P], attn[:, tb, :], ident[:, :])
                last.then_inc(attnT_ps, 1)
                pe.wait_ge(attnT_ready, i + 1)
                for tb in range(NT):
                    last = nc.tensor.matmul(ps[:, 4, tb * P:(tb + 1) * P], attnT[:, tb * P:(tb + 1) * P], wo[:, :],
                                            start=True, stop=True)
                last.then_inc(wo_ps, 1)
                pe.wait_ge(h2_ready, i + 1)
                for tb in range(NT):
                    last = nc.tensor.transpose(ps[:, 5, tb * P:(tb + 1) * P], hn[:, tb, :], ident[:, :])
                last.then_inc(h2T_ps, 1)
                pe.wait_ge(h2T_ready, i + 1)
                for tb in range(NT):
                    last = nc.tensor.matmul(ps[:, 6, tb * EX:(tb + 1) * EX], h2T[:, tb * P:(tb + 1) * P], wg[:, :],
                                            start=True, stop=True)
                last.then_inc(lg_ps, 1)
                for tb in range(NT):
                    if tb >= 2:
                        pe.wait_ge(mixed, i * NT + tb - 1)
                    for j in range(2):
                        last = nc.tensor.matmul(ps[:, 2 * (tb % 2) + j, :], h2T[:, tb * P:(tb + 1) * P],
                                                we[:, 4 * j:4 * j + 4, :].rearrange("p e f -> p (e f)"),
                                                start=True, stop=True)
                    last.then_inc(ex_ps, 1)


def normalised_columns(nc, x_in, zt_d):
    with layer_scope(nc) as ctx:
        sb, sem = alloc(nc, ctx)
        ident, minus_half = sb("nz_ident", [P, P]), sb("nz_minus_half", [P, NT])
        xt, z, zT = sb("nz_xt", [P, 2, NT, DM]), sb("nz_z", [P, NT, DM]), sb("nz_zT", [P, 2, PAD + T])
        stats, mv = sb("nz_stats", [P, NT + 1, 6]), sb("nz_mv", [P, NT, 2])
        var, rstd = sb("nz_var", [P, NT]), sb("nz_rstd", [P, NT])
        ps = ctx.enter_context(nc.psum_tensor("nz_ps", [P, 2, 512], F32))
        pool_step, consts_ready, dve_step = sem("nz_pool_step"), sem("nz_consts_ready"), sem("nz_dve_step")
        x_loaded = [sem("nz_x_loaded0"), sem("nz_x_loaded1")]
        stored = [sem("nz_stored0"), sem("nz_stored1")]
        var_ready, rstd_ready, z_ready = sem("nz_var_ready"), sem("nz_rstd_ready"), sem("nz_z_ready")
        zT_ps, zT_ready = sem("nz_zT_ps"), sem("nz_zT_ready")
        block = ctx.enter_context(nc.Block())

        @block.sync
        def _(sp):
            for a in range(2):
                sp.dma_start(xt[:, a, :, :], rows(x_in, a)).then_inc(x_loaded[a], 16)
            with sp.Fori(0, B // 2 - 1) as i:
                for a in range(2):
                    sp.wait_ge(z_ready, i * 2 + a + 1)
                    sp.dma_start(xt[:, a, :, :], rows(x_in, i * 2 + 2 + a)).then_inc(x_loaded[a], 16)

        @block.gpsimd
        def _(pool):
            link = Chain(pool, pool_step)
            link(pool.memset(ident[:, :], 0.0))
            diagonal(pool, link, ident[:, :], 0, [[-1, P]])
            link(pool.memset(zT[:, :, 0:PAD], 0.0))
            pool.memset(minus_half[:, :], -0.5).then_inc(consts_ready, 1)
            pool.wait_ge(consts_ready, 1)
            with pool.Fori(0, B) as i:
                pool.wait_ge(var_ready, i + 1)
                power(pool, rstd[:, :], var[:, :], minus_half[:, :]).then_inc(rstd_ready, 1)

        @block.vector
        def _(dve):
            link = Chain(dve, dve_step, 4)
            with dve.Fori(0, B // 2) as i:
                link.round(i)
                for a in range(2):
                    dve.wait_ge(x_loaded[a], i * 16 + 16)
                    norm_statistics(nc, link, xt[:, a, :, :], stats, mv)
                    nc.vector.tensor_scalar(var[:, :], mv[:, :, 1], LN_EPS, None, ALU.add).then_inc(var_ready, 1)
                    dve.wait_ge(rstd_ready, i * 2 + a + 1)
                    dve.wait_ge(zT_ps, i * 2 + a)
                    normalise(nc, xt[:, a, :, :], z, mv, rstd).then_inc(z_ready, 1)
                link.end()

        @block.tensor
        def _(pe):
            pe.wait_ge(consts_ready, 1)
            with pe.Fori(0, B // 2) as i:
                for a in range(2):
                    pe.wait_ge(z_ready, i * 2 + a + 1)
                    pe.wait_ge(zT_ready, i * 2 + a)
                    for tb in range(NT):
                        last = nc.tensor.transpose(ps[:, 0, tb * P:(tb + 1) * P], z[:, tb, :], ident[:, :])
                    last.then_inc(zT_ps, 1)

        @block.scalar
        def _(act):
            act.wait_ge(consts_ready, 1)
            with act.Fori(0, B // 2) as i:
                for a in range(2):
                    act.wait_ge(zT_ps, i * 2 + a + 1)
                    act.wait_ge(stored[a], i * 16)
                    act.activation(zT[:, a, PAD:PAD + T], ps[:, 0, :], ACT.Copy).then_inc(zT_ready, 1)
                    act.wait_ge(zT_ready, i * 2 + a + 1)
                    act.dma_start(zt_d[:, i * 2 + a, :], zT[:, a, :]).then_inc(stored[a], 16)
            for a in range(2):
                act.wait_ge(stored[a], B // 2 * 16)


def projections(nc, zt_d, k_d, q_d, d_d, v_d, w):
    NP = T // PCH
    KD, VD = RH * RN, RH * RV
    VT = P // B
    NV = PCH // VT
    with layer_scope(nc) as ctx:
        sb, sem = alloc(nc, ctx)
        wq, wk, wv = sb("pr_wq", [P, KD]), sb("pr_wk", [P, KD]), sb("pr_wv", [P, VD])
        cq, ck, cv = sb("pr_cq", [P, TAPS, KD]), sb("pr_ck", [P, TAPS, KD]), sb("pr_cv", [P, TAPS, VD])
        wa, wa_rep = sb("pr_wa", [P, RH]), sb("pr_wa_rep", [P, HH, J, RN])
        a_log, dt_b, a_exp = sb("pr_a_log", [P, HH]), sb("pr_dt_b", [P, HH]), sb("pr_a_exp", [P, HH])
        head_sum = sb("pr_head_sum", [P, P])
        zb = sb("pr_zb", [P, B, PAD + PCH])
        zc = sb("pr_zc", [P, (PAD + PCH) * B])
        ex = sb("pr_ex", [P, 4, 512])
        act_kq = sb("pr_act_kq", [P, 4, 512])
        sq = sb("pr_sq", [P, 4, 512])
        kq = sb("pr_kq", [P, 2, 2, HH, B, TCH])
        du, de = sb("pr_du", [P, HH, 512]), sb("pr_de", [P, HH, 512])
        dec = sb("pr_dec", [P, 2, HH, B, TCH])
        vv, ve = sb("pr_vv", [P, NV, VD]), sb("pr_ve", [P, NV, VD])
        ps = ctx.enter_context(nc.psum_tensor("pr_ps", [P, 8, 512], F32))

        weights_in, pool_step, consts_ready, a_ready, taps_ready = sem("pr_weights_in"), sem("pr_pool_step"), sem("pr_consts_ready"), sem("pr_a_ready"), sem("pr_taps_ready")
        dve_step = sem("pr_dve_step")
        z_in, z_ready = sem("pr_z_in"), sem("pr_z_ready")
        kq_ps, kq_exp, kq_silu, kq_sq, ss_ps, kq_root, kq_ready = sem("pr_kq_ps"), sem("pr_kq_exp"), sem("pr_kq_silu"), sem("pr_kq_sq"), sem("pr_ss_ps"), sem("pr_kq_root"), sem("pr_kq_ready")
        d_ps, du_ready, de_ready, ln_ready, dl_ready, d_ready = sem("pr_d_ps"), sem("pr_du_ready"), sem("pr_de_ready"), sem("pr_ln_ready"), sem("pr_dl_ready"), sem("pr_d_ready")
        v_ps, v_exp, v_ready, stored = sem("pr_v_ps"), sem("pr_v_exp"), sem("pr_v_ready"), sem("pr_stored")
        block = ctx.enter_context(nc.Block())
        NST = 2 * 3 + NV * HH
        NW = 7 + 2 * J

        @block.sync
        def _(sp):
            for dst, src in ((wq[:, :], w["Wq"]), (wk[:, :], w["Wk"]), (wv[:, :], w["Wv"]), (wa[:, :], w["Wa"])):
                sp.dma_start(dst, src).then_inc(weights_in, 16)
            for dst, src, n in ((cq, w["q_conv_w"], KD), (ck, w["k_conv_w"], KD), (cv, w["v_conv_w"], VD)):
                sp.dma_start(dst[:, :, :], bc(src.unsqueeze(0), P, TAPS, n)).then_inc(weights_in, 16)
            for j in range(J):
                sp.dma_start(a_log[RN * j:RN * (j + 1), :], bc(w["A_log"][j:j + 1, :], RN, HH)).then_inc(weights_in, 16)
                sp.dma_start(dt_b[RN * j:RN * (j + 1), :], bc(w["dt_bias"][j:j + 1, :], RN, HH)).then_inc(weights_in, 16)
            with sp.Fori(0, NP) as i:
                sp.wait_ge(z_ready, i)
                sp.dma_start(zb[:, :, :], zt_d[:, :, bass.ds(i * PCH, PAD + PCH)]).then_inc(z_in, 16)
                sp.wait_ge(d_ready, i + 1)
                for c in range(2):
                    sp.dma_start(d_d[i * 2 + c], dec[:, c, :, :, :].rearrange("p h b t -> p (h b t)")).then_inc(stored, 16)
                sp.wait_ge(kq_ready, i * 4 + 4)
                for c in range(2):
                    for a, dst in enumerate((q_d, k_d)):
                        sp.dma_start(dst[i * 2 + c], kq[:, a, c, :, :, :].rearrange("p h b t -> p (h b t)")).then_inc(stored, 16)
                sp.wait_ge(v_ready, i * NV + NV)
                for m in range(NV):
                    for h in range(HH):
                        sp.dma_start(v_d[h, bass.ds(i * PCH + m * VT, VT)].rearrange("t (b j) v -> (t b) (j v)", j=J),
                                     vv[:, m, h * J * RV:(h + 1) * J * RV]).then_inc(stored, 16)
            sp.wait_ge(stored, NP * NST * 16)
            for dst in (k_d, q_d, d_d):
                sp.dma_start(dst[2 * NP:2 * NP + 2], dst[0:2]).then_inc(stored, 16)
            sp.dma_start(v_d[:, T:T + PCH], v_d[:, 0:PCH]).then_inc(stored, 16)
            sp.wait_ge(stored, (NP * NST + 4) * 16)

        @block.gpsimd
        def _(pool):
            link = Chain(pool, pool_step)
            link(pool.memset(head_sum[:, :], 1.0))
            blocks = head_sum[:, :].rearrange("p (a r) -> p a r", r=RN)
            link(pool.affine_select(out=blocks, in_=blocks, compare_op=ALU.is_ge, fill=0.0, base=0,
                                    pattern=[[-RN, J], [0, RN]], channel_multiplier=1))
            pool.affine_select(out=blocks, in_=blocks, compare_op=ALU.is_ge, fill=0.0, base=RN - 1,
                               pattern=[[RN, J], [0, RN]], channel_multiplier=-1).then_inc(consts_ready, 1)

        @block.scalar
        def _(act):
            act.wait_ge(weights_in, NW * 16)
            act.activation(a_exp[:, :], a_log[:, :], ACT.Exp).then_inc(a_ready, 1)
            act.wait_ge(a_ready, 1)
            with act.Fori(0, NP) as i:
                act.wait_ge(z_in, i * 16 + 16)
                act.wait_ge(v_ps, i * NV)
                act.activation(zc[:, :].rearrange("p (t b) -> p b t", b=B), zb[:, :, :], ACT.Copy).then_inc(z_ready, 1)
                act.wait_ge(kq_ps, i + 1)
                act.activation(ex[:, :, :], ps[:, 0:4, :], ACT.Exp, scale=-1.0).then_inc(kq_exp, 1)
                act.wait_ge(du_ready, i + 1)
                act.activation(de[:, :, :], de[:, :, :], ACT.Exp, scale=-1.0).then_inc(de_ready, 1)
                for m in range(NV):
                    act.wait_ge(v_ps, i * NV + m + 1)
                    act.activation(ve[:, m, :], ps[:, 6 + m % 2, :], ACT.Exp, scale=-1.0).then_inc(v_exp, 1)
                act.wait_ge(kq_silu, i + 1)
                act.activation(sq[:, :, :], act_kq[:, :, :], ACT.Square).then_inc(kq_sq, 1)
                act.wait_ge(de_ready, i + 1)
                act.activation(de[:, :, :], de[:, :, :], ACT.Ln, bias=1.0).then_inc(ln_ready, 1)
                act.wait_ge(dl_ready, i + 1)
                act.wait_ge(stored, i * NST * 16)
                for h in range(HH):
                    last = act.activation(dec[:, :, h, :, :].rearrange("p c b t -> p c t b"),
                                          du[:, h, :].rearrange("p (c t b) -> p c t b", b=B, c=2), ACT.Exp,
                                          scale=-1.0)
                last.then_inc(d_ready, 1)
                act.wait_ge(ss_ps, i + 1)
                act.activation(sq[:, :, :], ps[:, 0:4, :], ACT.Sqrt).then_inc(kq_root, 1)

        @block.vector
        def _(dve):
            dve.wait_ge(weights_in, NW * 16)
            for c, m, n in ((cq, wq, KD), (ck, wk, KD), (cv, wv, VD)):
                nc.vector.tensor_tensor(c[:, :, :], c[:, :, :], bc(m[:, :].unsqueeze(1), P, TAPS, n), ALU.mult)
            nc.vector.tensor_copy(wa_rep[:, :, :, :], bc(wa[:, :].rearrange("p (h j) -> p h j", h=HH).unsqueeze(3), P, HH, J, RN)).then_inc(taps_ready, 1)
            dve.wait_ge(a_ready, 1)
            PER = 6 + 2 * NV
            link = Chain(dve, dve_step, PER)
            with dve.Fori(0, NP) as i:
                link.round(i)
                dve.wait_ge(d_ps, i + 1)
                for h in range(HH):
                    last = nc.vector.tensor_scalar(du[:, h, :], ps[:, 4 + h, :], dt_b[:, h:h + 1], None, ALU.add)
                link(last)
                nc.vector.scalar_tensor_tensor(out=de[:, :, :], in0=du[:, :, :], scalar=-1.0, in1=du[:, :, :],
                                               op0=ALU.mult, op1=ALU.max).then_inc(du_ready, 1)
                dve.wait_ge(kq_exp, i + 1)
                link(nc.vector.tensor_scalar(act_kq[:, :, :], ex[:, :, :], 1.0, None, ALU.add))
                link(nc.vector.reciprocal(act_kq[:, :, :], act_kq[:, :, :]))
                nc.vector.tensor_tensor(act_kq[:, :, :], act_kq[:, :, :], ps[:, 0:4, :], ALU.mult).then_inc(kq_silu, 1)
                for m in range(NV):
                    dve.wait_ge(v_exp, i * NV + m + 1)
                    link(nc.vector.tensor_scalar(ve[:, m, :], ve[:, m, :], 1.0, None, ALU.add))
                    link(nc.vector.reciprocal(ve[:, m, :], ve[:, m, :]))
                    if m == 0:
                        dve.wait_ge(stored, i * NST * 16)
                    nc.vector.tensor_tensor(vv[:, m, :], ve[:, m, :], ps[:, 6 + m % 2, :], ALU.mult).then_inc(v_ready, 1)
                dve.wait_ge(ln_ready, i + 1)
                link(nc.vector.scalar_tensor_tensor(out=du[:, :, :], in0=du[:, :, :], scalar=0.0, in1=de[:, :, :],
                                                    op0=ALU.max, op1=ALU.add))
                for h in range(HH):
                    last = nc.vector.tensor_scalar(du[:, h, :], du[:, h, :], a_exp[:, h:h + 1], None, ALU.mult)
                last.then_inc(dl_ready, 1)
                dve.wait_ge(kq_root, i + 1)
                link(nc.vector.tensor_scalar(sq[:, :, :], sq[:, :, :], 1e-6, None, ALU.add))
                link(nc.vector.reciprocal(sq[:, :, :], sq[:, :, :]))
                dve.wait_ge(kq_silu, i + 1)
                for a in range(2):
                    for h in range(HH):
                        def by_chunk(t):
                            return t[:, a * HH + h, :].rearrange("p (c t b) -> p c t b", b=B, c=2)
                        nc.vector.tensor_tensor(kq[:, a, :, h, :, :].rearrange("p c b t -> p c t b"),
                                                by_chunk(act_kq), by_chunk(sq), ALU.mult).then_inc(kq_ready, 1)
                dve.wait_ge(kq_ready, i * 4 + 4)
                link.end()

        @block.tensor
        def _(pe):
            pe.wait_ge(taps_ready, 1)
            pe.wait_ge(consts_ready, 1)
            pe.wait_ge(weights_in, NW * 16)
            with pe.Fori(0, NP) as i:
                pe.wait_ge(z_ready, i + 1)
                pe.wait_ge(kq_root, i)
                for n, (c, h) in enumerate(((cq, 0), (cq, 1), (ck, 0), (ck, 1))):
                    for tap in range(TAPS):
                        last = nc.tensor.matmul(ps[:, n, :], c[:, tap, h * P:(h + 1) * P], zc[:, tap * B:(tap + PCH) * B],
                                                start=(tap == 0), stop=(tap == TAPS - 1))
                last.then_inc(kq_ps, 1)
                for h in range(HH):
                    last = nc.tensor.matmul(ps[:, 4 + h, :], wa_rep[:, h, :, :].rearrange("p j n -> p (j n)"),
                                            zc[:, PAD * B:(PAD + PCH) * B], start=True, stop=True)
                last.then_inc(d_ps, 1)
                for m in range(NV):
                    if m >= 2:
                        pe.wait_ge(v_ready, i * NV + m - 1)
                    for tap in range(TAPS):
                        last = nc.tensor.matmul(ps[:, 6 + m % 2, :], zc[:, (tap + VT * m) * B:(tap + VT * (m + 1)) * B],
                                                cv[:, tap, :], start=(tap == 0), stop=(tap == TAPS - 1))
                    last.then_inc(v_ps, 1)
                pe.wait_ge(kq_sq, i + 1)
                for n in range(4):
                    last = nc.tensor.matmul(ps[:, n, :], head_sum[:, :], sq[:, n, :], start=True, stop=True)
                last.then_inc(ss_ps, 1)


def recurrence(nc, k_d, q_d, d_d, v_d, sq_d):
    SR = 2 * TCH
    NB = SR // BLK
    LD = 16 * (3 + HH)
    with layer_scope(nc) as ctx:
        sb, sem = alloc(nc, ctx)
        kc, qc, dc = sb("rc_kc", [P, 2, G, TCH]), sb("rc_qc", [P, 2, G, TCH]), sb("rc_dc", [P, 2, G, TCH])
        vc = sb("rc_vc", [P, 2, TCH, RV])
        kb, qb = sb("rc_kb", [P, 2, BLK, P]), sb("rc_qb", [P, 2, BLK, P])
        kt = sb("rc_kt", [P, 2, GRP, NC, P])
        state = sb("rc_state", [P, 2, G * RV])
        faded, arg = sb("rc_faded", [P, G * RV]), sb("rc_arg", [P, G * RV])
        delta = sb("rc_delta", [P, 2, CW])
        ring = sb("rc_ring", [P, 2, BLK, CW])
        ident = sb("rc_ident", [P, P])
        neg_head, one_head = sb("rc_neg_head", [P, J]), sb("rc_one_head", [P, J])
        own4, neg_own = sb("rc_own4", [P, NC, CG]), sb("rc_neg_own", [P, CG])
        ps = ctx.enter_context(nc.psum_tensor("rc_ps", [P, 8, 512], F32))
        RB, QB, TB = 4, 6, 7

        pool_step, consts_ready, own_ready = sem("rc_pool_step"), sem("rc_consts_ready"), sem("rc_own_ready")
        chunk_in = [sem("rc_chunk_in0"), sem("rc_chunk_in1")]
        k_built, q_built = sem("rc_k_built"), sem("rc_q_built")
        kt_ps, kt_copied = sem("rc_kt_ps"), sem("rc_kt_copied")
        state_ready = sem("rc_state_ready")
        r_ps, delta_ready, up_ps, faded_ready, arg_ready = sem("rc_r_ps"), sem("rc_delta_ready"), sem("rc_up_ps"), sem("rc_faded_ready"), sem("rc_arg_ready")
        q_ps, q_copied = sem("rc_q_ps"), sem("rc_q_copied")
        ring_out = [sem("rc_ring_out0"), sem("rc_ring_out1")]
        block = ctx.enter_context(nc.Block())

        def cols(c):
            return slice(c * CW, (c + 1) * CW)

        @block.sync
        def _(sp):
            def load(par, chunk, t0):
                for dst, src in ((kc, k_d), (qc, q_d), (dc, d_d)):
                    sp.dma_start(dst[:, par, :, :].rearrange("p g t -> p (g t)"), src[chunk]).then_inc(chunk_in[par], 16)
                for h in range(HH):
                    sp.dma_start(vc[h * B * J:(h + 1) * B * J, par, :, :],
                                 v_d[h, bass.ds(t0, TCH)].rearrange("t r v -> r t v")).then_inc(chunk_in[par], 16)

            for par in range(2):
                load(par, par, par * TCH)
            with sp.Fori(0, T // SR) as i:
                for blk in range(NB):
                    sp.wait_ge(q_copied, i * SR + (blk + 1) * BLK)
                    for c in range(NC):
                        for g in range(CG):
                            p0 = 32 * c + J * g
                            sp.dma_start(sq_d[p0:p0 + J, bass.ds(i * SR + blk * BLK, BLK), :],
                                         ring[p0:p0 + J, blk % 2, :, g * RV:(g + 1) * RV]).then_inc(ring_out[blk % 2], 16)
                    if blk % 2 == 1:
                        par = blk // 2
                        sp.wait_ge(arg_ready, i * SR * NC + NC * TCH * (par + 1))
                        load(par, i * 2 + 2 + par, i * SR + SR + par * TCH)
            for par in range(2):
                sp.wait_ge(ring_out[par], T // SR * NB // 2 * 32 * 16)
                sp.wait_ge(chunk_in[par], (T // SR + 1) * LD)

        @block.gpsimd
        def _(pool):
            link = Chain(pool, pool_step)
            link(pool.memset(ident[:, :], 0.0))
            diagonal(pool, link, ident[:, :], 0, [[-1, P]])
            for m, value in ((neg_head, -1.0), (one_head, 1.0)):
                link(pool.memset(m[:, :], value))
                link(pool.affine_select(out=m[:, :], in_=m[:, :], compare_op=ALU.is_ge, fill=0.0, base=0,
                                        pattern=[[-RN, J]], channel_multiplier=1))
                link(pool.affine_select(out=m[:, :], in_=m[:, :], compare_op=ALU.is_ge, fill=0.0, base=RN - 1,
                                        pattern=[[RN, J]], channel_multiplier=-1))
            link(pool.memset(own4[:, :, :], -1.0))
            link(pool.affine_select(out=own4[:, :, :], in_=own4[:, :, :], compare_op=ALU.is_ge, fill=0.0, base=0,
                                    pattern=[[-32, NC], [-J, CG]], channel_multiplier=1))
            link(pool.affine_select(out=own4[:, :, :], in_=own4[:, :, :], compare_op=ALU.is_ge, fill=0.0, base=J - 1,
                                    pattern=[[32, NC], [J, CG]], channel_multiplier=-1))
            pool.memset(kt[:, :, :, :, :], 0.0).then_inc(consts_ready, 1)
            with pool.Fori(0, T // SR) as i:
                for s in range(SR):
                    par = s // TCH
                    if s % TCH == 0:
                        pool.wait_ge(chunk_in[par], i * LD + LD)
                    for c in range(NC):
                        pool.wait_ge(state_ready, i * SR * NC + NC * s + c + 1)
                        pool.tensor_tensor(faded[:, cols(c)].rearrange("p (g v) -> p g v", v=RV),
                                           state[:, (s + 1) % 2, cols(c)].rearrange("p (g v) -> p g v", v=RV),
                                           bc(dc[:, par, c * CG:(c + 1) * CG, s % TCH].unsqueeze(2), P, CG, RV),
                                           ALU.mult).then_inc(faded_ready, 1)

        @block.vector
        def _(dve):
            dve.wait_ge(consts_ready, 1)
            nc.vector.tensor_reduce(out=neg_own[:, :], in_=own4[:, :, :].rearrange("p c g -> p g c"), op=ALU.add,
                                    axis=AXX).then_inc(own_ready, 1)
            for c in range(NC):
                nc.vector.memset(state[:, 1, cols(c)], 0.0).then_inc(state_ready, 1)
            dve.wait_ge(own_ready, 1)

            def build(dst, slot, src, half, par, head, done):
                nc.vector.tensor_tensor(
                    dst[:, slot, :, :].rearrange("p t (g j) -> p t g j", j=J),
                    bc(src[:, par, :, half * BLK:(half + 1) * BLK].rearrange("p g t -> p t g").unsqueeze(3), P, BLK, G, J),
                    bc(head[:, :].unsqueeze(1).unsqueeze(1), P, BLK, G, J), ALU.mult).then_inc(done, 1)

            dve.wait_ge(chunk_in[0], LD)
            build(kb, 0, kc, 0, 0, neg_head, k_built)
            build(qb, 0, qc, 0, 0, one_head, q_built)
            with dve.Fori(0, T // SR) as i:
                for s in range(SR):
                    dve.wait_ge(r_ps, i * SR + s + 1)
                    nc.vector.tensor_tensor(delta[:, s % 2, :].rearrange("p (g v) -> p g v", v=RV),
                                            ps[:, RB + s % 2, :].rearrange("p (g v) -> p g v", v=RV),
                                            bc(neg_own[:, :].unsqueeze(2), P, CG, RV), ALU.mult).then_inc(delta_ready, 1)
                    for c in range(NC):
                        dve.wait_ge(up_ps, i * SR * NC + NC * s + c + 1)
                        dve.wait_ge(faded_ready, i * SR * NC + NC * s + c + 1)
                        nc.vector.tensor_tensor(arg[:, cols(c)], faded[:, cols(c)], ps[:, c, :],
                                                ALU.add).then_inc(arg_ready, 1)
                    nb = s // BLK + 1
                    par = nb // 2 % 2
                    if s % BLK == 1:
                        dve.wait_ge(q_ps, i * SR + s)
                        if nb % 2 == 0:
                            dve.wait_ge(chunk_in[par], i * LD + (2 * LD if nb == NB else LD))
                        build(kb, nb % 2, kc, nb % 2, par, neg_head, k_built)
                    if s % BLK == 2:
                        build(qb, nb % 2, qc, nb % 2, par, one_head, q_built)

        @block.scalar
        def _(act):
            def copy_turned(slot, c0, n):
                for c in range(c0, c0 + n):
                    act.activation(kt[32 * c:32 * c + 32, slot, :, c, :],
                                   ps[32 * c:32 * c + 32, TB, :].rearrange("p (t m) -> p t m", t=GRP),
                                   ACT.Copy).then_inc(kt_copied, 1)

            def copy_answer(i, s):
                act.wait_ge(q_ps, i * SR + s + 1)
                if s % BLK == 0:
                    act.wait_ge(ring_out[s // BLK % 2], (i * (NB // 2) + s // BLK // 2) * 512)
                act.activation(ring[:, s // BLK % 2, s % BLK, :], ps[:, QB, :], ACT.Copy).then_inc(q_copied, 1)

            act.wait_ge(consts_ready, 1)
            act.wait_ge(kt_ps, 1)
            copy_turned(0, 0, NC)
            with act.Fori(0, T // SR) as i:
                for s in range(SR):
                    if s > 0:
                        copy_answer(i, s - 1)
                    for c in range(NC):
                        act.wait_ge(arg_ready, i * SR * NC + NC * s + c + 1)
                        if s == 0 and c == 0:
                            act.wait_ge(q_ps, i * SR)
                        act.activation(state[:, s % 2, cols(c)], arg[:, cols(c)], ACT.Tanh).then_inc(state_ready, 1)
                    grp = s // GRP
                    if s % GRP == 1:
                        act.wait_ge(kt_ps, i * (SR // GRP) + grp + 2)
                        copy_turned((grp + 1) % 2, 0, 2)
                    if s % GRP == 2:
                        copy_turned((grp + 1) % 2, 2, 2)
                copy_answer(i, SR - 1)

        @block.tensor
        def _(pe):
            def place_values(bank, par, t):
                for c in range(NC):
                    last = nc.tensor.matmul(ps[32 * c:32 * c + 32, bank, :].rearrange("p (g v) -> p g v", v=RV),
                                            ident[:, 32 * c:32 * c + 32], bc(vc[:, par, t, :].unsqueeze(1), P, CG, RV),
                                            start=True, stop=False, skip_group_check=True)

            def turn_keys(slot, first):
                for t in range(GRP):
                    last = nc.tensor.transpose(ps[:, TB, t * P:(t + 1) * P], kb[:, slot, first + t, :], ident[:, :])
                last.then_inc(kt_ps, 1)

            def answer(i, s):
                for c in range(NC):
                    pe.wait_ge(state_ready, i * SR * NC + NC * (s + 1) + c + 1)
                    if c == 0:
                        pe.wait_ge(q_copied, i * SR + s)
                    last = nc.tensor.matmul(ps[32 * c:32 * c + 32, QB, :], qb[:, s // BLK % 2, s % BLK, 32 * c:32 * c + 32],
                                            state[:, s % 2, cols(c)], start=True, stop=True)
                last.then_inc(q_ps, 1)

            pe.wait_ge(consts_ready, 1)
            pe.wait_ge(k_built, 1)
            turn_keys(0, 0)
            pe.wait_ge(chunk_in[0], LD)
            place_values(RB, 0, 0)
            with pe.Fori(0, T // SR) as i:
                for s in range(SR):
                    blk, grp = s // BLK, s // GRP
                    if s % BLK == 0:
                        pe.wait_ge(k_built, i * NB + blk + 1)
                        pe.wait_ge(q_built, i * NB + blk + 1)
                    for c in range(NC):
                        pe.wait_ge(state_ready, i * SR * NC + NC * s + c + 1)
                        last = nc.tensor.matmul(ps[32 * c:32 * c + 32, RB + s % 2, :],
                                                kb[:, blk % 2, s % BLK, 32 * c:32 * c + 32],
                                                state[:, (s + 1) % 2, cols(c)], start=False, stop=True,
                                                skip_group_check=True)
                    last.then_inc(r_ps, 1)
                    if s > 0:
                        answer(i, s - 1)
                    pe.wait_ge(delta_ready, i * SR + s + 1)
                    if s % GRP == 0:
                        pe.wait_ge(kt_copied, (i * (SR // GRP) + grp + 1) * NC)
                    for c in range(NC):
                        nc.tensor.matmul(ps[:, c, :], kt[:, grp % 2, s % GRP, c, :], delta[:, s % 2, :],
                                         start=True, stop=True).then_inc(up_ps, 1)
                    if s % GRP == 0:
                        n = grp + 1
                        if n % 2 == 0:
                            pe.wait_ge(k_built, i * NB + n // 2 + 1)
                        turn_keys(n // 2 % 2, (n % 2) * GRP)
                    if (s + 1) % TCH == 0:
                        par = (s + 1) // TCH % 2
                        pe.wait_ge(chunk_in[par], i * LD + (2 * LD if par == 0 else LD))
                    place_values(RB + (s + 1) % 2, (s + 1) // TCH % 2, (s + 1) % TCH)
                answer(i, SR - 1)


def outputs(nc, x_in, x_out, zt_d, sq_d, w):
    VD = RH * RV
    NVT = VD // P
    with layer_scope(nc) as ctx:
        sb, sem = alloc(nc, ctx)
        ident, minus_half = sb("po_ident", [P, P]), sb("po_minus_half", [P, NT, RH])
        wg, wo, onorm = sb("po_wg", [P, VD]), sb("po_wo", [P, NVT, DM]), sb("po_onorm", [P, RV])
        xt, xn, zT = sb("po_xt", [P, NT, DM]), sb("po_xn", [P, NT, DM]), sb("po_zT", [P, T])
        s = sb("po_s", [P, NT, VD])
        e, eg, o, o2 = sb("po_e", [P, NT, VD]), sb("po_eg", [P, NT, VD]), sb("po_o", [P, NT, VD]), sb("po_o2", [P, NT, VD])
        ssum, rms = sb("po_ssum", [P, NT, RH]), sb("po_rms", [P, NT, RH])
        oT = sb("po_oT", [P, 2, VD])
        ps = ctx.enter_context(nc.psum_tensor("po_ps", [P, 8, 512], F32))
        weights_in, pool_step, consts_ready, dve_step = sem("po_weights_in"), sem("po_pool_step"), sem("po_consts_ready"), sem("po_dve_step")
        loaded, g_ps, eg_ready, es_ready = sem("po_loaded"), sem("po_g_ps"), sem("po_eg_ready"), sem("po_es_ready")
        o_ready, sq_ready, ss_ready, rms_ready, y_ready = sem("po_o_ready"), sem("po_sq_ready"), sem("po_ss_ready"), sem("po_rms_ready"), sem("po_y_ready")
        oT_ps, oT_ready, wo_ps, xn_ready, stored = sem("po_oT_ps"), sem("po_oT_ready"), sem("po_wo_ps"), sem("po_xn_ready"), sem("po_stored")
        block = ctx.enter_context(nc.Block())
        NL = 2 + NT * HH
        sq_v = sq_d.rearrange("(h b j) t v -> b h t j v", h=HH, j=J)

        @block.sync
        def _(sp):
            for dst, src in ((wg[:, :], w["Wg"]), (wo[:, :, :], w["Wo"].rearrange("(c p) n -> p c n", p=P)),
                             (onorm[:, :], bc(w["o_norm_w"], P, RV))):
                sp.dma_start(dst, src).then_inc(weights_in, 16)
            with sp.Fori(0, B) as i:
                sp.wait_ge(xn_ready, i)
                sp.dma_start(xt[:, :, :], rows(x_in, i)).then_inc(loaded, 16)
                sp.dma_start(zT[:, :], zt_d[:, i, PAD:PAD + T]).then_inc(loaded, 16)
                for tb in range(NT):
                    for h in range(HH):
                        sp.dma_start(s[:, tb, h * J * RV:(h + 1) * J * RV].rearrange("p (j v) -> p j v", j=J),
                                     sq_v[i, h, tb * P:(tb + 1) * P]).then_inc(loaded, 16)
                sp.wait_ge(xn_ready, i + 1)
                sp.dma_start(rows(x_out, i), xn[:, :, :]).then_inc(stored, 16)
            sp.wait_ge(stored, B * 16)

        @block.gpsimd
        def _(pool):
            link = Chain(pool, pool_step)
            link(pool.memset(ident[:, :], 0.0))
            diagonal(pool, link, ident[:, :], 0, [[-1, P]])
            pool.memset(minus_half[:, :, :], -0.5).then_inc(consts_ready, 1)
            pool.wait_ge(consts_ready, 1)
            with pool.Fori(0, B) as i:
                pool.wait_ge(ss_ready, i + 1)
                power(pool, rms[:, :, :], ssum[:, :, :], minus_half[:, :, :]).then_inc(rms_ready, 1)

        @block.scalar
        def _(act):
            with act.Fori(0, B) as i:
                act.wait_ge(loaded, (i * NL + NL) * 16)
                act.activation(e[:, :, :], s[:, :, :], ACT.Exp, scale=-1.0).then_inc(es_ready, 1)
                act.wait_ge(g_ps, i + 1)
                act.activation(eg[:, :, :], ps[:, 0:NT, :], ACT.Exp, scale=-1.0).then_inc(eg_ready, 1)
                act.wait_ge(o_ready, i + 1)
                act.activation(o2[:, :, :], o[:, :, :], ACT.Square).then_inc(sq_ready, 1)
                for tb in range(NT):
                    act.wait_ge(oT_ps, i * NT + tb + 1)
                    act.activation(oT[:, tb % 2, :], ps[:, 4 + tb % 2, :], ACT.Copy).then_inc(oT_ready, 1)

        @block.vector
        def _(dve):
            dve.wait_ge(weights_in, 3 * 16)
            link = Chain(dve, dve_step, 8)
            with dve.Fori(0, B) as i:
                link.round(i)
                dve.wait_ge(es_ready, i + 1)
                link(nc.vector.tensor_scalar(e[:, :, :], e[:, :, :], 1.0, None, ALU.add))
                link(nc.vector.reciprocal(e[:, :, :], e[:, :, :]))
                link(nc.vector.tensor_tensor(o[:, :, :], s[:, :, :], s[:, :, :], ALU.mult))
                nc.vector.tensor_tensor(o[:, :, :], o[:, :, :], e[:, :, :], ALU.mult).then_inc(o_ready, 1)
                dve.wait_ge(eg_ready, i + 1)
                link(nc.vector.tensor_scalar(eg[:, :, :], eg[:, :, :], 1.0, None, ALU.add))
                link(nc.vector.reciprocal(eg[:, :, :], eg[:, :, :]))
                link(nc.vector.tensor_tensor(eg[:, :, :].rearrange("p n (h v) -> p (n h) v", v=RV),
                                             eg[:, :, :].rearrange("p n (h v) -> p (n h) v", v=RV),
                                             bc(onorm[:, :].unsqueeze(1), P, NT * RH, RV), ALU.mult))
                dve.wait_ge(sq_ready, i + 1)
                link(nc.vector.tensor_reduce(out=ssum[:, :, :], in_=o2[:, :, :].rearrange("p n (h v) -> p n h v", v=RV),
                                             op=ALU.add, axis=AXX))
                nc.vector.tensor_scalar(ssum[:, :, :], ssum[:, :, :], 1.0 / RV, 1e-5, ALU.mult, ALU.add).then_inc(ss_ready, 1)
                dve.wait_ge(o_ready, i + 1)
                link(nc.vector.tensor_tensor(eg[:, :, :], eg[:, :, :], o[:, :, :], ALU.mult))
                dve.wait_ge(rms_ready, i + 1)
                nc.vector.tensor_tensor(o[:, :, :].rearrange("p n (h v) -> p (n h) v", v=RV),
                                        eg[:, :, :].rearrange("p n (h v) -> p (n h) v", v=RV),
                                        bc(rms[:, :, :].rearrange("p n h -> p (n h)").unsqueeze(2), P, NT * RH, RV),
                                        ALU.mult).then_inc(y_ready, 1)
                dve.wait_ge(wo_ps, i + 1)
                dve.wait_ge(stored, i * 16)
                nc.vector.tensor_tensor(xn[:, :, :], ps[:, 6, :].rearrange("p (n d) -> p n d", n=NT), xt[:, :, :],
                                        ALU.add).then_inc(xn_ready, 1)
                link.end()

        @block.tensor
        def _(pe):
            pe.wait_ge(weights_in, 3 * 16)
            pe.wait_ge(consts_ready, 1)
            with pe.Fori(0, B) as i:
                pe.wait_ge(loaded, (i * NL + NL) * 16)
                pe.wait_ge(eg_ready, i)
                for tb in range(NT):
                    last = nc.tensor.matmul(ps[:, tb, :], zT[:, tb * P:(tb + 1) * P], wg[:, :], start=True, stop=True)
                last.then_inc(g_ps, 1)
                pe.wait_ge(y_ready, i + 1)
                for tb in range(NT):
                    if tb >= 2:
                        pe.wait_ge(oT_ready, i * NT + tb - 1)
                    for c in range(NVT):
                        last = nc.tensor.transpose(ps[:, 4 + tb % 2, c * P:(c + 1) * P], o[:, tb, c * P:(c + 1) * P], ident[:, :])
                    last.then_inc(oT_ps, 1)
                    pe.wait_ge(oT_ready, i * NT + tb + 1)
                    for c in range(NVT):
                        last = nc.tensor.matmul(ps[:, 6, tb * P:(tb + 1) * P], oT[:, tb % 2, c * P:(c + 1) * P],
                                                wo[:, c, :], start=(c == 0), stop=(c == NVT - 1))
                last.then_inc(wo_ps, 1)


def hybrid(nc, ins, out):
    def scratch(name, shape):
        return nc.dram_tensor(name, shape, F32).ap()

    def layer(prefix):
        return {name[len(prefix):]: ap for name, ap in ins.items() if name.startswith(prefix)}
    x1, x2, x3 = (scratch(f"x{n}", [B, T, DM]) for n in (1, 2, 3))
    zt_d = scratch("zt_d", [P, B, PAD + T])
    chunks = T // TCH + 2
    k_d, q_d, d_d = (scratch(n, [chunks, P, G * TCH]) for n in ("k_d", "q_d", "d_d"))
    v_d = scratch("v_d", [HH, T + 2 * TCH, B * J, RV])
    sq_d = scratch("sq_d", [P, T, RV])
    a, b, f = layer("L0_attn_a_"), layer("L0_attn_b_"), layer("L0_ffn_")
    state_space(nc, a["x"], x1, a)
    feed_forward(nc, "f1_", x1, x2, f)
    normalised_columns(nc, x2, zt_d)
    projections(nc, zt_d, k_d, q_d, d_d, v_d, b)
    recurrence(nc, k_d, q_d, d_d, v_d, sq_d)
    outputs(nc, x2, x3, zt_d, sq_d, b)
    feed_forward(nc, "f2_", x3, out, f)


def kernel(**inputs):
    import numpy as _np
    import concourse.bacc as _bacc
    from concourse import mybir as _mybir
    from concourse.bass_utils import run_bass_kernel_spmd as _run

    column = {"L0_attn_a_conv_b", "L0_attn_a_b_dt", "L0_attn_a_D", "L0_ffn_gamma1", "L0_ffn_gamma2"}
    row = {"L0_ffn_bq", "L0_ffn_bup", "L0_ffn_bo", "L0_ffn_bg", "L0_attn_b_o_norm_w"}
    turned = {"L0_attn_b_" + n for n in ("Wq", "Wk", "Wv", "Wa", "Wg", "Wo")}
    taps = {"L0_attn_b_" + n for n in ("q_conv_w", "k_conv_w", "v_conv_w")}
    by_half = {"L0_attn_b_A_log", "L0_attn_b_dt_bias"}
    nc = _bacc.Bacc("TRN2", target_bir_lowering=False, num_devices=1)
    arrays, ins = {}, {}
    for name, value in inputs.items():
        a = _np.asarray(value)
        if name in column:
            a = a.reshape(-1, 128).T
        elif name in row:
            a = a.reshape(1, -1)
        elif name == "L0_ffn_bdown":
            a = a.reshape(-1, 1)
        elif name in turned:
            a = a.T
        elif name in taps:
            a = a[:, 0, :].T
        elif name in by_half:
            a = a.reshape(2, 4).T
        a = _np.ascontiguousarray(a)
        arrays[f"in_{name}"] = a
        ins[name] = nc.dram_tensor(f"in_{name}", a.shape, _mybir.dt.from_np(a.dtype), kind="ExternalInput").ap()
    out = nc.dram_tensor("out_x", (16, 512, 128), _mybir.dt.float32, kind="ExternalOutput").ap()
    hybrid(nc, ins, out)
    r = _run(nc, [arrays], core_ids=[0])
    return r.results[0]["out_x"]
```

```python
import concourse.bass as bass
from concourse import mybir
from contextlib import ExitStack, contextmanager

F32 = mybir.dt.float32
BF16 = mybir.dt.bfloat16
ALU = mybir.AluOpType
ACT = mybir.ActivationFunctionType
AXX = mybir.AxisListType.X

P = 128
B = 16
T = 512
DM = 128
NT = T // P
LN_EPS = 1e-5

CH = 256
CT = CH // P
ST = 16
RK = 64
TAPS = 4
PAD = TAPS - 1

FH = 16
HD = DM // FH
LAT = 64
EX = 8
RMS_EPS = 1e-6

RH = 8
RN = 32
RV = 64
HH = 2
J = RH // HH
G = HH * B
NC = 4
CG = G // NC
CW = CG * RV
TCH = 16
PCH = 32
PARTS = 3
BLK = 8
GRP = 4


class Batch:

    def __init__(self, i, c):
        self.i, self.c, self.slot = i, c, c % 2

    def index(self):
        return self.i * 2 + self.c

    def count(self, per=1, k=None):
        return self.i * (2 * per) + self.c * per + (per if k is None else k)

    def slot_count(self, per):
        return self.i * per + (self.c // 2 + 1) * per

    def near(self, d):
        return Batch(self.i, self.c + d)


class Chain:

    def __init__(self, eng, sem, per=0):
        self.eng, self.sem, self.per, self.i, self.n = eng, sem, per, 0, 0

    def round(self, i):
        self.i, self.n = i, 0

    def __call__(self, ins):
        self.n += 1
        ins.then_inc(self.sem, 1)
        self.eng.wait_ge(self.sem, self.i.count(self.per, self.n) if isinstance(self.i, Batch) else self.i * self.per + self.n)

    def end(self):
        assert self.n == self.per, self.n


def alloc(nc, ctx, tag=""):
    def sb(name, shape, dt=F32):
        return ctx.enter_context(nc.sbuf_tensor(tag + name, shape, dt))

    def sem(name):
        return nc.alloc_semaphore(tag + name)
    return sb, sem


@contextmanager
def layer_scope(nc):
    with nc.cleanup_on_exit(), ExitStack() as ctx:
        yield ctx


def bc(ap, *shape):
    return ap.broadcast_to(list(shape))


def diagonal(pool, chain, m, base=0, pattern=None, fill=1.0):
    chain(pool.affine_select(out=m, in_=m, compare_op=ALU.not_equal, fill=fill, base=base,
                             pattern=pattern, channel_multiplier=1))


def norm_statistics(nc, link, src, stats, mv):
    for tb in range(NT):
        last = nc.vector.bn_stats(stats[:, tb, :], src[:, tb, :])
    link(last)
    nc.vector.memset(stats[:, NT, :], 0.0)
    for tb in range(NT):
        last = nc.vector.bn_aggr(mv[:, tb, :], stats[:, tb, :])
    link(last)


def power(pool, dst, src, exponent):
    return pool.tensor_tensor(dst, src, exponent, ALU.pow)


def normalise(nc, src, dst, mv, rstd):
    for tb in range(NT):
        last = nc.vector.tensor_scalar(dst[:, tb, :], src[:, tb, :], mv[:, tb, 0:1], rstd[:, tb:tb + 1],
                                       ALU.subtract, ALU.mult)
    return last


def rows(x, b):
    return x[b].rearrange("(n p) d -> p n d", p=P)


def pipelined(eng, body):
    first = Batch(0, 0)
    body(None, None, first)
    body(None, first, first.near(1))
    with eng.Fori(0, B // 2 - 1) as i:
        for c in (1, 2):
            n = Batch(i, c)
            body(n.near(-1), n, n.near(1))
    last = Batch(0, B - 1)
    body(last.near(-1), last, None)
    body(last, None, None)


def batch_traffic(sp, load, store, slot_free):
    n = Batch(0, 0)
    slot_free(n)
    load(n.near(2))
    with sp.Fori(0, B // 2 - 2) as i:
        for c in (1, 2):
            n = Batch(i, c)
            slot_free(n)
            load(n.near(2))
            store(n.near(-1))
    n = Batch(0, B - 3)
    slot_free(n)
    load(n.near(2))
    for c in range(B - 4, B):
        store(Batch(0, c))


def state_space(nc, x_in, x_out, w):
    RA, RB, RS, RP, RC = 8, 4, 8, 16, 4
    LAG, LEFT = 4, 3
    AHEAD = 2
    NK = ST * CT
    Y0, BB, CB, EVEN, ODD = 0, 2, 5, 6, 7
    NBB = 3
    with layer_scope(nc) as ctx:
        sb, sem = alloc(nc, ctx)
        w_in = sb("ss_w_in", [P, 2 * CH])
        conv_w = sb("ss_conv_w", [P, TAPS, CH])
        w_tap = sb("ss_w_tap", [P, TAPS, CH])
        conv_b = sb("ss_conv_b", [P, CT])
        w_x = sb("ss_w_x", [P, CT, RK + 2 * ST])
        w_bc = sb("ss_w_bc", [P, CT, 3, 2 * ST])
        w_dt = sb("ss_w_dt", [RK, CH])
        b_dt = sb("ss_b_dt", [P, CT])
        a_log = sb("ss_a_log", [P, CT, ST])
        a_neg = sb("ss_a_neg", [P, CT, ST])
        d_skip = sb("ss_d", [P, CT])
        w_out = sb("ss_w_out", [P, CT, DM])
        ident = sb("ss_ident", [P, P])
        pick = sb("ss_pick", [96, 2 * ST, P], BF16)
        xt, xc = sb("ss_xt", [P, 2, NT, DM]), sb("ss_xc", [P, 2, NT, DM])
        xn, z = sb("ss_xn", [P, NT, DM]), sb("ss_z", [P, NT, DM])
        stats, mv = sb("ss_stats", [P, NT + 1, 6]), sb("ss_mv", [P, NT, 2])
        rstd, var, minus_half = sb("ss_rstd", [P, NT]), sb("ss_var", [P, NT]), sb("ss_minus_half", [P, NT])
        zT = sb("ss_zT", [P, PAD + T])
        sig = sb("ss_sig", [P, CT, T])
        h, gate = sb("ss_h", [P, 2, CT, T]), sb("ss_gate", [P, 2, CT, T])
        ts = sb("ss_ts", [RK, T])
        u, e = sb("ss_u", [P, CT, T]), sb("ss_e", [P, CT, T])
        dt, dth = sb("ss_dt", [P, 2, CT, T]), sb("ss_dth", [P, 2, CT, T])
        bc_hi, bc_mid = sb("ss_bc_hi", [96, T], BF16), sb("ss_bc_mid", [96, T], BF16)
        bc_r1, bc3 = sb("ss_bc_r1", [96, T]), sb("ss_bc3", [96, 2, T], BF16)
        dA, dBu = sb("ss_dA", [P, RA, T]), sb("ss_dBu", [P, RB, T])
        state, c_all, prod = sb("ss_state", [P, RS, T]), sb("ss_c_all", [P, RC, T]), sb("ss_prod", [P, RP, T])
        y, yT = sb("ss_y", [P, CT, T]), sb("ss_yT", [P, CT, T])
        ps = ctx.enter_context(nc.psum_tensor("ss_ps", [P, 8, 512], F32))

        weights_in, ident_ready, taps_ready = sem("ss_weights_in"), sem("ss_ident_ready"), sem("ss_taps_ready")
        a_exp, pool_step, pre_step = sem("ss_a_exp"), sem("ss_pool_step"), sem("ss_pre_step")
        x_loaded = [sem("ss_x_loaded0"), sem("ss_x_loaded1")]
        xc_ready, z_ready, zT_ps, zT_ready = sem("ss_xc_ready"), sem("ss_z_ready"), sem("ss_zT_ps"), sem("ss_zT_ready")
        var_ready, rstd_ready = sem("ss_var_ready"), sem("ss_rstd_ready")
        h_ps, h_sig, h_ready = sem("ss_h_ps"), sem("ss_h_sig"), sem("ss_h_ready")
        gate_ps, gate_sig, gate_ready = sem("ss_gate_ps"), sem("ss_gate_sig"), sem("ss_gate_ready")
        ts_ps, bc_ps, ts_ready, bc_ready = sem("ss_ts_ps"), sem("ss_bc_ps"), sem("ss_ts_ready"), sem("ss_bc_ready")
        dt_ps, u_ready, abs_ready, dte_ready, ln_ready = sem("ss_dt_ps"), sem("ss_u_ready"), sem("ss_abs_ready"), sem("ss_dte_ready"), sem("ss_ln_ready")
        dt_ready, dth_ready = sem("ss_dt_ready"), sem("ss_dth_ready")
        b_ps, c_ps, c_copied, dA_ready = sem("ss_b_ps"), sem("ss_c_ps"), sem("ss_c_copied"), sem("ss_dA_ready")
        dBu_done, scan_done, prod_ready, y_acc = sem("ss_dBu_done"), sem("ss_scan_done"), sem("ss_prod_ready"), sem("ss_y_acc")
        y_ready, yT_ready, out_ps, xn_ready, stored = sem("ss_y_ready"), sem("ss_yT_ready"), sem("ss_out_ps"), sem("ss_xn_ready"), sem("ss_stored")
        NW = 9

        block = ctx.enter_context(nc.Block())

        def ring_wait(eng, sem, n, per, k):
            if k > 0 or n.c > 0:
                eng.wait_ge(sem, n.count(per, k))

        @block.sync
        def _(sp):
            def load(n):
                sp.dma_start(xt[:, n.slot, :, :], rows(x_in, n.index())).then_inc(x_loaded[n.slot], 16)

            def store(n):
                sp.wait_ge(xn_ready, n.count())
                sp.dma_start(rows(x_out, n.index()), xn[:, :, :]).then_inc(stored, 16)

            def slot_free(n):
                sp.wait_ge(z_ready, n.count())
                sp.wait_ge(xc_ready, n.count())

            sp.sem_inc(stored, 16)
            load(Batch(0, 0))
            load(Batch(0, 1))
            for dst, src in ((w_in[:, :], w["W_in"]),
                             (conv_w[:, :, :], bc(w["conv_w"].rearrange("k a c -> a k c"), P, TAPS, CH)),
                             (conv_b[:, :], w["conv_b"]),
                             (w_x[:, :, :], w["W_x"].rearrange("(c p) n -> p c n", p=P)),
                             (w_dt[:, :], w["W_dt"]),
                             (b_dt[:, :], w["b_dt"]),
                             (a_log[:, :, :], w["A_log"].rearrange("(c p) n -> p c n", p=P)),
                             (d_skip[:, :], w["D"]),
                             (w_out[:, :, :], w["W_out"].rearrange("(c p) n -> p c n", p=P))):
                sp.dma_start(dst, src).then_inc(weights_in, 16)

            batch_traffic(sp, load, store, slot_free)
            sp.wait_ge(stored, B * 16 + 16)

        @block.gpsimd
        def _(pool):
            link = Chain(pool, pool_step)
            link(pool.memset(ident[:, :], 0.0))
            diagonal(pool, link, ident[:, :], 0, [[-1, P]])
            link(pool.memset(pick[:, :, :], 0.0))
            for part in range(3):
                diagonal(pool, link, pick[:, :, :], -2 * ST * part, [[-1, 2 * ST], [0, P]])
            link(pool.memset(minus_half[:, :], -0.5))
            pool.memset(zT[:, 0:PAD], 0.0).then_inc(ident_ready, 1)

            def body(post, mid, pre):
                if pre:
                    pool.wait_ge(var_ready, pre.count())
                    power(pool, rstd[:, :], var[:, :], minus_half[:, :]).then_inc(rstd_ready, 1)
                for n in range(ST if mid else 0):
                    for ct in range(CT):
                        k = n * CT + ct
                        pool.wait_ge(scan_done, mid.count(NK, k + 1))
                        pool.wait_ge(c_copied, mid.count(ST, n + 1))
                        ring_wait(pool, y_acc, mid, NK, k - RP + 1)
                        pool.tensor_tensor(prod[:, k % RP, :], state[:, k % RS, :], c_all[:, n % RC, :],
                                           ALU.mult).then_inc(prod_ready, 1)

            pipelined(pool, body)

        @block.scalar
        def _(act):
            act.wait_ge(weights_in, NW * 16)
            act.activation(a_neg[:, :, :], a_log[:, :, :], ACT.Exp).then_inc(a_exp, 1)
            act.wait_ge(taps_ready, 1)

            def decays(mid, n):
                if n == 0:
                    act.wait_ge(dt_ready, mid.count())
                for ct in range(CT):
                    k = n * CT + ct
                    ring_wait(act, scan_done, mid, NK, k - RA + 1)
                    act.activation(dA[:, k % RA, :], dt[:, mid.slot, ct, :], ACT.Exp,
                                   scale=a_neg[:, ct, n:n + 1]).then_inc(dA_ready, 1)

            def c_rows(mid, n):
                act.wait_ge(c_ps, mid.count(ST, n + 1))
                ring_wait(act, prod_ready, mid, NK, (n - RC + 1) * CT)
                act.activation(c_all[:, n % RC, :], ps[:, CB, :], ACT.Copy).then_inc(c_copied, 1)

            def prepare(pre, n):
                if n == 1:
                    act.wait_ge(zT_ps, pre.count())
                    act.activation(zT[:, PAD:PAD + T], ps[:, ODD, :], ACT.Copy).then_inc(zT_ready, 1)
                if n == 5:
                    for ct in range(CT):
                        act.wait_ge(h_ps, pre.count(CT, ct + 1))
                        act.activation(sig[:, ct, :], ps[:, EVEN + ct, :], ACT.Sigmoid, bias=conv_b[:, ct:ct + 1]).then_inc(h_sig, 1)
                if n == 7:
                    act.wait_ge(h_ready, pre.count(CT))
                    for ct in range(CT):
                        act.wait_ge(gate_ps, pre.count(CT, ct + 1))
                        act.activation(sig[:, ct, :], ps[:, EVEN + ct, :], ACT.Sigmoid).then_inc(gate_sig, 1)
                if n == 9:
                    act.wait_ge(ts_ps, pre.count())
                    act.activation(ts[:, :], ps[0:RK, EVEN, :], ACT.Copy).then_inc(ts_ready, 1)
                if n == 12:
                    for ct in range(CT):
                        act.wait_ge(dt_ps, pre.count(CT, ct + 1))
                        act.activation(u[:, ct, :], ps[:, EVEN + ct, :], ACT.Identity, bias=b_dt[:, ct:ct + 1]).then_inc(u_ready, 1)
                if n == 14:
                    act.wait_ge(abs_ready, pre.count())
                    act.activation(e[:, :, :], e[:, :, :], ACT.Exp, scale=-1.0).then_inc(dte_ready, 1)
                    act.wait_ge(dte_ready, pre.count())
                    act.activation(e[:, :, :], e[:, :, :], ACT.Ln, bias=1.0).then_inc(ln_ready, 1)

            def body(post, mid, pre):
                for n in range(ST):
                    if mid:
                        if n == 0:
                            decays(mid, 0)
                        elif n + AHEAD < ST:
                            decays(mid, n + AHEAD)
                        c_rows(mid, n)
                        for ahead in range(1, AHEAD + 1 if n == 0 else 1):
                            decays(mid, ahead)
                    if mid and n == 3:
                        act.wait_ge(x_loaded[mid.slot], mid.slot_count(16))
                        act.activation(xc[:, mid.slot, :, :], xt[:, mid.slot, :, :], ACT.Copy).then_inc(xc_ready, 1)
                    if pre:
                        prepare(pre, n)

            pipelined(act, body)

        @block.vector
        def _(dve):
            dve.wait_ge(weights_in, NW * 16)
            nc.vector.tensor_tensor(w_tap[:, :, :], bc(w_in[:, 0:CH].unsqueeze(1), P, TAPS, CH), conv_w[:, :, :], ALU.mult)
            for rep in range(3):
                nc.vector.tensor_copy(w_bc[:, :, rep, :], w_x[:, :, RK:RK + 2 * ST])
            dve.wait_ge(a_exp, 1)
            nc.vector.tensor_scalar(a_neg[:, :, :], a_neg[:, :, :], -1.0, None, ALU.mult).then_inc(taps_ready, 1)
            pre_link = Chain(dve, pre_step, 5)

            def inflow(mid, k):
                n, ct = k // CT, k % CT
                if k == 0:
                    dve.wait_ge(dth_ready, mid.count())
                dve.wait_ge(b_ps, mid.count(ST, n + 1))
                ring_wait(dve, scan_done, mid, NK, k - RB + 1)
                nc.vector.tensor_tensor(dBu[:, k % RB, :], dth[:, mid.slot, ct, :], ps[:, BB + n % NBB, :],
                                        ALU.mult).then_inc(dBu_done, 1)

            def scans(mid, n):
                if n == 0:
                    inflow(mid, 0)
                for k in range(n * CT, (n + 1) * CT):
                    if k + 1 < NK:
                        inflow(mid, k + 1)
                    dve.wait_ge(dBu_done, mid.count(NK, k + 1))
                    dve.wait_ge(dA_ready, mid.count(NK, k + 1))
                    ring_wait(dve, prod_ready, mid, NK, k - RS + 1)
                    nc.vector.tensor_tensor_scan(state[:, k % RS, :], dA[:, k % RA, :], dBu[:, k % RB, :], 0.0,
                                                 ALU.mult, ALU.add).then_inc(scan_done, 1)

            def finish(post, n):
                if n == 2:
                    dve.wait_ge(y_acc, post.count(NK))
                    for ct in range(CT):
                        last = nc.vector.scalar_tensor_tensor(out=y[:, ct, :], in0=h[:, post.slot, ct, :], scalar=d_skip[:, ct:ct + 1],
                                                              in1=ps[:, Y0 + ct, :], op0=ALU.mult, op1=ALU.add)
                    last.then_inc(y_ready, 1)
                    dve.wait_ge(y_ready, post.count())
                    nc.vector.tensor_tensor(yT[:, :, :], y[:, :, :], gate[:, post.slot, :, :], ALU.mult).then_inc(yT_ready, 1)
                if n == 15:
                    dve.wait_ge(out_ps, post.count())
                    dve.wait_ge(xc_ready, post.count())
                    dve.wait_ge(stored, post.count(16))
                    nc.vector.tensor_tensor(xn[:, :, :], xc[:, post.slot, :, :],
                                            ps[:, EVEN, :].rearrange("p (n d) -> p n d", n=NT), ALU.add).then_inc(xn_ready, 1)

            def statistics(pre):
                link = pre_link
                link.round(pre)
                dve.wait_ge(x_loaded[pre.slot], pre.slot_count(16))
                norm_statistics(nc, link, xt[:, pre.slot, :, :], stats, mv)
                nc.vector.tensor_scalar(var[:, :], mv[:, :, 1], LN_EPS, None, ALU.add).then_inc(var_ready, 1)

            def prepare(pre, n):
                link = pre_link
                if n == 0:
                    dve.wait_ge(rstd_ready, pre.count())
                    normalise(nc, xt[:, pre.slot, :, :], z, mv, rstd).then_inc(z_ready, 1)
                if n == 6:
                    for ct in range(CT):
                        dve.wait_ge(h_sig, pre.count(CT, ct + 1))
                        nc.vector.scalar_tensor_tensor(out=h[:, pre.slot, ct, :], in0=ps[:, EVEN + ct, :], scalar=conv_b[:, ct:ct + 1],
                                                       in1=sig[:, ct, :], op0=ALU.add, op1=ALU.mult).then_inc(h_ready, 1)
                if n == 8:
                    for ct in range(CT):
                        dve.wait_ge(gate_sig, pre.count(CT, ct + 1))
                        nc.vector.tensor_tensor(gate[:, pre.slot, ct, :], sig[:, ct, :], ps[:, EVEN + ct, :],
                                                ALU.mult).then_inc(gate_ready, 1)
                if n == 11:
                    dve.wait_ge(bc_ps, pre.count())
                    link(nc.vector.tensor_copy(bc_hi[:, :], ps[0:96, ODD, :]))
                    link(nc.vector.tensor_tensor(bc_r1[:, :], ps[0:96, ODD, :], bc_hi[:, :], ALU.subtract))
                    link(nc.vector.tensor_copy(bc_mid[:, :], bc_r1[:, :]))
                    nc.vector.tensor_copy(bc3[0:32, pre.slot, :], bc_hi[0:32, :])
                    nc.vector.tensor_copy(bc3[32:64, pre.slot, :], bc_mid[32:64, :])
                    nc.vector.tensor_tensor(bc3[64:96, pre.slot, :], bc_r1[64:96, :], bc_mid[64:96, :],
                                            ALU.subtract).then_inc(bc_ready, 1)
                if n == 13:
                    dve.wait_ge(u_ready, pre.count(CT))
                    nc.vector.scalar_tensor_tensor(out=e[:, :, :], in0=u[:, :, :], scalar=-1.0, in1=u[:, :, :],
                                                   op0=ALU.mult, op1=ALU.max).then_inc(abs_ready, 1)
                if n == 15:
                    dve.wait_ge(ln_ready, pre.count())
                    nc.vector.scalar_tensor_tensor(out=dt[:, pre.slot, :, :], in0=u[:, :, :], scalar=0.0, in1=e[:, :, :],
                                                   op0=ALU.max, op1=ALU.add).then_inc(dt_ready, 1)
                    dve.wait_ge(dt_ready, pre.count())
                    dve.wait_ge(h_ready, pre.count(CT))
                    nc.vector.tensor_tensor(dth[:, pre.slot, :, :], dt[:, pre.slot, :, :], h[:, pre.slot, :, :], ALU.mult).then_inc(dth_ready, 1)
                    link.end()

            def body(post, mid, pre):
                if pre:
                    statistics(pre)
                for n in range(ST):
                    if mid:
                        scans(mid, n)
                    if pre:
                        prepare(pre, n)
                    if post:
                        finish(post, n)

            pipelined(dve, body)

        @block.tensor
        def _(pe):
            pe.wait_ge(ident_ready, 1)
            pe.wait_ge(taps_ready, 1)
            pe.wait_ge(weights_in, NW * 16)

            def add_state(mid, n):
                for ct in range(CT):
                    k = n * CT + ct
                    pe.wait_ge(prod_ready, mid.count(NK, k + 1))
                    nc.tensor.matmul(ps[:, Y0 + ct, :], ident[:, :], prod[:, k % RP, :],
                                     start=(n == 0), stop=(n == ST - 1)).then_inc(y_acc, 1)

            def rows(mid, n):
                if n == 0:
                    pe.wait_ge(bc_ready, mid.count())
                ring_wait(pe, dBu_done, mid, NK, (n - NBB + 1) * CT if n else 0)
                nc.tensor.matmul(ps[:, BB + n % NBB, :], pick[:, n, :], bc3[:, mid.slot, :],
                                 start=True, stop=True).then_inc(b_ps, 1)

            def sums(post, mid, n):
                ring_wait(pe, c_copied, mid, ST, n)
                nc.tensor.matmul(ps[:, CB, :], pick[:, ST + n, :], bc3[:, mid.slot, :],
                                 start=True, stop=True).then_inc(c_ps, 1)
                if n == LAG and post:
                    pe.wait_ge(y_ready, post.count())
                for summed in range(n - LAG, n - LAG + 1) if n < ST - 1 else range(ST - 1 - LAG, ST - LEFT):
                    if summed >= 0:
                        add_state(mid, summed)

            def finish(post, pre, n):
                if n < LEFT:
                    add_state(post, ST - LEFT + n)
                if n == 14:
                    pe.wait_ge(yT_ready, post.count())
                    if pre:
                        pe.wait_ge(u_ready, pre.count(CT))
                    for tb in range(NT):
                        for ct in range(CT):
                            last = nc.tensor.matmul(ps[:, EVEN, tb * P:(tb + 1) * P], yT[:, ct, tb * P:(tb + 1) * P],
                                                    w_out[:, ct, :], start=(ct == 0), stop=(ct == CT - 1))
                    last.then_inc(out_ps, 1)

            def convolution(ct, taps):
                for tap in taps:
                    last = nc.tensor.matmul(ps[:, EVEN + ct, :], w_tap[:, tap, ct * P:(ct + 1) * P],
                                            zT[:, tap:tap + T], start=(tap == 0), stop=(tap == TAPS - 1))
                return last

            def prepare(mid, pre, n):
                if n == 1:
                    pe.wait_ge(z_ready, pre.count())
                    if mid:
                        pe.wait_ge(u_ready, mid.count(CT))
                    for tb in range(NT):
                        last = nc.tensor.transpose(ps[:, ODD, tb * P:(tb + 1) * P], z[:, tb, :], ident[:, :])
                    last.then_inc(zT_ps, 1)
                if n == 2:
                    pe.wait_ge(zT_ready, pre.count())
                    convolution(0, (0, 1))
                if n == 3:
                    convolution(0, (2, 3)).then_inc(h_ps, 1)
                if n == 4:
                    convolution(1, (0, 1))
                if n == 5:
                    convolution(1, (2, 3)).then_inc(h_ps, 1)
                if n == 7:
                    for ct in range(CT):
                        pe.wait_ge(h_ready, pre.count(CT, ct + 1))
                        nc.tensor.matmul(ps[:, EVEN + ct, :], w_in[:, CH + ct * P:CH + (ct + 1) * P],
                                         zT[:, PAD:PAD + T], start=True, stop=True).then_inc(gate_ps, 1)
                if n == 9:
                    pe.wait_ge(gate_ready, pre.count(CT))
                    for ct in range(CT):
                        last = nc.tensor.matmul(ps[0:RK, EVEN, :], w_x[:, ct, 0:RK], h[:, pre.slot, ct, :],
                                                start=(ct == 0), stop=(ct == CT - 1))
                    last.then_inc(ts_ps, 1)
                if n == 10:
                    for ct in range(CT):
                        last = nc.tensor.matmul(ps[0:96, ODD, :], w_bc[:, ct, :, :].rearrange("p r n -> p (r n)"),
                                                h[:, pre.slot, ct, :], start=(ct == 0), stop=(ct == CT - 1))
                    last.then_inc(bc_ps, 1)
                if n in (11, 12):
                    ct = n - 11
                    pe.wait_ge(ts_ready, pre.count())
                    if ct == 1:
                        pe.wait_ge(bc_ready, pre.count())
                    nc.tensor.matmul(ps[:, EVEN + ct, :], w_dt[:, ct * P:(ct + 1) * P], ts[:, :],
                                     start=True, stop=True).then_inc(dt_ps, 1)

            def body(post, mid, pre):
                if mid:
                    rows(mid, 0)
                for n in range(ST):
                    if mid:
                        if n + 1 < ST:
                            rows(mid, n + 1)
                        sums(post, mid, n)
                    if post:
                        finish(post, pre, n)
                    if pre:
                        prepare(mid, pre, n)

            pipelined(pe, body)


def feed_forward(nc, tag, x_in, x_out, w):
    SCALE = 1.0 / float(HD) ** 0.5
    S0, EX0, TURN, WIDE, KV0 = 0, 2, 4, 5, 6
    HE = EX // 2
    with layer_scope(nc) as ctx:
        sb, sem = alloc(nc, ctx, tag)
        ident = sb("ident", [P, P])
        wq, wdown = sb("wq", [P, DM]), sb("wdown", [P, LAT])
        wup = sb("wup", [LAT, 2 * DM])
        wo, wg, we = sb("wo", [P, DM]), sb("wg", [P, EX]), sb("we", [P, EX, DM])
        g1, g2, bdown = sb("g1", [P, 1]), sb("g2", [P, 1]), sb("bdown", [LAT, 1])
        b_q, b_up, bo, bg = sb("b_q", [P, DM]), sb("b_up", [P, 2 * DM]), sb("bo", [P, DM]), sb("bg", [P, EX])
        minus_half = sb("minus_half", [P, NT])
        xt, xc, z, zb = sb("xt", [P, 2, NT, DM]), sb("xc", [P, 2, NT, DM]), sb("z", [P, NT, DM]), sb("zb", [P, 2, NT, DM])
        stats, mv, stats2, mv2 = sb("stats", [P, NT + 1, 6]), sb("mv", [P, NT, 2]), sb("stats2", [P, NT + 1, 6]), sb("mv2", [P, NT, 2])
        var, rstd, ms, r1 = sb("var", [P, NT]), sb("rstd", [P, NT]), sb("ms", [P, NT]), sb("r1", [P, NT])
        ms2, r2 = sb("ms2", [P, NT]), sb("r2", [P, NT])
        hn, hT, down = sb("hn", [P, NT, DM]), sb("hT", [P, T]), sb("down", [LAT, T])
        q, kk, v = sb("q", [P, NT, DM]), sb("k", [P, NT, DM]), sb("v", [P, 2, NT, DM])
        qk = sb("qk", [P, 2, HD, FH * FH])
        pv = sb("pv", [P, 2, FH, DM])
        top, s, tot = sb("top", [P, NT, FH]), sb("s", [P, NT, FH, FH]), sb("tot", [P, NT, FH])
        attn, attnT = sb("attn", [P, NT, DM]), sb("attnT", [P, T])
        x1, xr, h2, h2T = sb("x1", [P, NT, DM]), sb("xr", [P, NT, DM]), sb("h2", [P, NT, DM]), sb("h2T", [P, T])
        lg, lmax, gsum = sb("lg", [P, NT, EX]), sb("lmax", [P, NT]), sb("gsum", [P, NT])
        mix, comb, xn = sb("mix", [P, 2, EX, DM]), sb("comb", [P, NT, DM]), sb("xn", [P, NT, DM])
        ps = ctx.enter_context(nc.psum_tensor(tag + "ps", [P, 8, 512], F32))

        weights_in, pool_step, consts_ready = sem("weights_in"), sem("pool_step"), sem("consts_ready")
        pre_step, mid_step, post_step = sem("pre_step"), sem("mid_step"), sem("post_step")
        x_loaded = [sem("x_loaded0"), sem("x_loaded1")]
        xc_ready, var_ready, rstd_ready, z_ready = sem("xc_ready"), sem("var_ready"), sem("rstd_ready"), sem("z_ready")
        ms_ready, r1_ready, h_ready, zb_ready = sem("ms_ready"), sem("r1_ready"), sem("h_ready"), sem("zb_ready")
        hT_ps, hT_ready, qd_ps, down_ready, kv_ps, qkv_ready = sem("hT_ps"), sem("hT_ready"), sem("qd_ps"), sem("down_ready"), sem("kv_ps"), sem("qkv_ready")
        qk_ready, s_ps, s_ready, p_ready, pv_ready = sem("qk_ready"), sem("s_ps"), sem("s_ready"), sem("p_ready"), sem("pv_ready")
        o_done, attn_ready, attnT_ps, attnT_ready = sem("o_done"), sem("attn_ready"), sem("attnT_ps"), sem("attnT_ready")
        wo_ps, ms2_ready, r2_ready, xr_ready = sem("wo_ps"), sem("ms2_ready"), sem("r2_ready"), sem("xr_ready")
        h2_ready, h2T_ps, h2T_ready, lg_ps, lg_ready, eg_ready = sem("h2_ready"), sem("h2T_ps"), sem("h2T_ready"), sem("lg_ps"), sem("lg_ready"), sem("eg_ready")
        gates_ready, ex_ps, mixed, summed, xn_ready, stored = sem("gates_ready"), sem("ex_ps"), sem("mixed"), sem("summed"), sem("xn_ready"), sem("stored")

        block = ctx.enter_context(nc.Block())
        loads = [(wq[:, :], w["Wq"]), (wdown[:, :], w["Wdown"]), (wup[:, :], w["Wup"]), (wo[:, :], w["Wo"]),
                 (wg[:, :], w["Wg"]), (we[:, :, :], w["We"].rearrange("e d f -> d e f")),
                 (g1[:, :], w["gamma1"]), (g2[:, :], w["gamma2"]), (bdown[:, :], w["bdown"]),
                 (b_q[:, :], bc(w["bq"], P, DM)), (b_up[:, :], bc(w["bup"], P, 2 * DM)),
                 (bo[:, :], bc(w["bo"], P, DM)), (bg[:, :], bc(w["bg"], P, EX))]
        NW = len(loads)

        def heads(ap):
            return ap.rearrange("p (h d) -> p h d", d=HD)

        @block.sync
        def _(sp):
            def load(n):
                sp.dma_start(xt[:, n.slot, :, :], rows(x_in, n.index())).then_inc(x_loaded[n.slot], 16)

            def store(n):
                sp.wait_ge(xn_ready, n.count())
                sp.dma_start(rows(x_out, n.index()), xn[:, :, :]).then_inc(stored, 16)

            def slot_free(n):
                sp.wait_ge(z_ready, n.count())
                sp.wait_ge(xc_ready, n.count())

            sp.sem_inc(stored, 16)
            load(Batch(0, 0))
            load(Batch(0, 1))
            for dst, src in loads:
                sp.dma_start(dst, src).then_inc(weights_in, 16)
            batch_traffic(sp, load, store, slot_free)
            sp.wait_ge(stored, B * 16 + 16)

        @block.gpsimd
        def _(pool):
            link = Chain(pool, pool_step)
            link(pool.memset(ident[:, :], 0.0))
            diagonal(pool, link, ident[:, :], 0, [[-1, P]])
            pool.memset(minus_half[:, :], -0.5).then_inc(consts_ready, 1)
            pool.wait_ge(consts_ready, 1)
            pool.wait_ge(weights_in, NW * 16)

            def values(n, tb):
                if tb == 0:
                    pool.wait_ge(qkv_ready, n.count())
                pool.wait_ge(p_ready, n.count(NT, tb + 1))
                if tb >= 2:
                    pool.wait_ge(o_done, n.count(NT, tb - 1))
                pool.tensor_tensor(pv[:, tb % 2, :, :].rearrange("p g (h d) -> p g h d", d=HD),
                                   bc(s[:, tb, :, :].rearrange("p h g -> p g h").unsqueeze(3), P, FH, FH, HD),
                                   bc(heads(v[:, n.slot, tb, :]).unsqueeze(2), P, FH, FH, HD),
                                   ALU.mult).then_inc(pv_ready, 1)

            def body(post, mid, pre):
                if pre:
                    pool.wait_ge(var_ready, pre.count())
                    power(pool, rstd[:, :], var[:, :], minus_half[:, :]).then_inc(rstd_ready, 1)
                if post:
                    pool.wait_ge(ms2_ready, post.count())
                    power(pool, r2[:, :], ms2[:, :], minus_half[:, :]).then_inc(r2_ready, 1)
                if pre:
                    pool.wait_ge(ms_ready, pre.count())
                    power(pool, r1[:, :], ms[:, :], minus_half[:, :]).then_inc(r1_ready, 1)
                if mid:
                    values(mid, 0)
                if pre:
                    pool.wait_ge(z_ready, pre.count())
                    pool.wait_ge(r1_ready, pre.count())
                    pool.tensor_tensor(hn[:, :, :], z[:, :, :], bc(r1[:, :].unsqueeze(2), P, NT, DM),
                                       ALU.mult).then_inc(h_ready, 1)
                if mid:
                    values(mid, 1)
                if post:
                    pool.wait_ge(xc_ready, post.count())
                    pool.tensor_tensor(xr[:, :, :], x1[:, :, :], xc[:, post.slot, :, :], ALU.add).then_inc(xr_ready, 1)
                if pre:
                    pool.tensor_tensor(zb[:, pre.slot, :, :], z[:, :, :], bc(bo[:, :].unsqueeze(1), P, NT, DM),
                                       ALU.add).then_inc(zb_ready, 1)
                if mid:
                    values(mid, 2)
                    values(mid, 3)

            pipelined(pool, body)

        @block.scalar
        def _(act):
            act.wait_ge(weights_in, NW * 16)

            def exponentials(n, tb):
                act.wait_ge(s_ready, n.count(NT, tb + 1))
                act.activation(s[:, tb, :, :], s[:, tb, :, :], ACT.Exp, scale=SCALE).then_inc(p_ready, 1)

            def body(post, mid, pre):
                if post:
                    act.wait_ge(attnT_ps, post.count())
                    act.activation(attnT[:, :], ps[:, TURN, :], ACT.Copy).then_inc(attnT_ready, 1)
                if mid:
                    exponentials(mid, 0)
                    exponentials(mid, 1)
                if post:
                    act.wait_ge(h2T_ps, post.count())
                    act.activation(h2T[:, :], ps[:, TURN, :], ACT.Copy, scale=g2[:, :]).then_inc(h2T_ready, 1)
                    act.wait_ge(lg_ready, post.count())
                    act.activation(lg[:, :, :], lg[:, :, :], ACT.Exp).then_inc(eg_ready, 1)
                if mid:
                    exponentials(mid, 2)
                if pre:
                    act.wait_ge(hT_ps, pre.count())
                    act.activation(hT[:, :], ps[:, KV0, :], ACT.Copy, scale=g1[:, :]).then_inc(hT_ready, 1)
                    if post:
                        act.wait_ge(xr_ready, post.count())
                    act.wait_ge(x_loaded[pre.slot], pre.slot_count(16))
                    act.activation(xc[:, pre.slot, :, :], xt[:, pre.slot, :, :], ACT.Copy).then_inc(xc_ready, 1)
                    act.wait_ge(qd_ps, pre.count())
                    act.activation(down[:, :], ps[0:LAT, KV0 + 1, :], ACT.Identity, bias=bdown[:, :]).then_inc(down_ready, 1)
                if mid:
                    exponentials(mid, 3)
                if post:
                    act.wait_ge(gates_ready, post.count())
                    for tb in range(NT):
                        if tb >= 2:
                            act.wait_ge(summed, post.count(NT, tb - 1))
                        for half in range(2):
                            act.wait_ge(ex_ps, post.count(2 * NT, 2 * tb + half + 1))
                            for e in range(half * HE, (half + 1) * HE):
                                last = act.activation(mix[:, tb % 2, e, :],
                                                      ps[:, EX0 + half, (e % HE) * DM:(e % HE + 1) * DM],
                                                      ACT.Copy, scale=lg[:, tb, e:e + 1])
                            last.then_inc(mixed, 1)

            pipelined(act, body)

        @block.vector
        def _(dve):
            dve.wait_ge(weights_in, NW * 16)
            pre_link, mid_link, post_link = Chain(dve, pre_step, 4), Chain(dve, mid_step, 12), Chain(dve, post_step, 9)

            def statistics(n):
                pre_link.round(n)
                dve.wait_ge(x_loaded[n.slot], n.slot_count(16))
                norm_statistics(nc, pre_link, xt[:, n.slot, :, :], stats, mv)
                nc.vector.tensor_scalar(var[:, :], mv[:, :, 1], LN_EPS, None, ALU.add).then_inc(var_ready, 1)

            def normalised(n, mid):
                if mid:
                    dve.wait_ge(zb_ready, mid.count())
                dve.wait_ge(rstd_ready, n.count())
                link = pre_link
                normalise(nc, xt[:, n.slot, :, :], z, mv, rstd).then_inc(z_ready, 1)
                link(nc.vector.tensor_tensor(ms[:, :], rstd[:, :], rstd[:, :], ALU.mult))
                link(nc.vector.tensor_tensor(ms[:, :], ms[:, :], mv[:, :, 1], ALU.mult))
                nc.vector.tensor_scalar(ms[:, :], ms[:, :], RMS_EPS, None, ALU.add).then_inc(ms_ready, 1)

            def projected(n):
                dve.wait_ge(qd_ps, n.count())
                nc.vector.tensor_tensor(q[:, :, :], ps[:, TURN, :].rearrange("p (n d) -> p n d", n=NT),
                                        bc(b_q[:, :].unsqueeze(1), P, NT, DM), ALU.add)
                dve.wait_ge(kv_ps, n.count())
                for a, dst in enumerate((kk[:, :, :], v[:, n.slot, :, :])):
                    last = nc.vector.tensor_tensor(
                        dst.rearrange("p n (h d) -> p n h d", d=HD),
                        ps[:, KV0:KV0 + 2, :].rearrange("p a (m h e d) -> p (a m) h e d", h=FH, e=2, d=HD)[:, :, :, a, :],
                        bc(b_up[:, :].rearrange("p (h e d) -> p h e d", e=2, d=HD)[:, :, a, :].unsqueeze(1), P, NT, FH, HD),
                        ALU.add)
                last.then_inc(qkv_ready, 1)
                pre_link.end()

            def scores(n, tb):
                if tb == 0:
                    mid_link.round(n)
                    dve.wait_ge(qkv_ready, n.count())
                if tb >= 2:
                    dve.wait_ge(s_ps, n.count(NT, tb - 1))
                nc.vector.tensor_tensor(qk[:, tb % 2, :, :].rearrange("p d (h g) -> p d h g", g=FH),
                                        bc(heads(q[:, tb, :]).rearrange("p h d -> p d h").unsqueeze(3), P, HD, FH, FH),
                                        bc(heads(kk[:, tb, :]).rearrange("p g d -> p d g").unsqueeze(2), P, HD, FH, FH),
                                        ALU.mult).then_inc(qk_ready, 1)

            def less_maximum(n, tb):
                dve.wait_ge(s_ps, n.count(NT, tb + 1))
                sc = ps[:, S0 + tb % 2, 0:256].rearrange("p (h g) -> p h g", g=FH)
                mid_link(nc.vector.tensor_reduce(out=top[:, tb, :], in_=sc, op=ALU.max, axis=AXX))
                nc.vector.tensor_tensor(s[:, tb, :, :], sc, bc(top[:, tb, :].unsqueeze(2), P, FH, FH),
                                        ALU.subtract).then_inc(s_ready, 1)

            def weighted(n, tb):
                dve.wait_ge(p_ready, n.count(NT, tb + 1))
                mid_link(nc.vector.tensor_reduce(out=tot[:, tb, :], in_=s[:, tb, :, :], op=ALU.add, axis=AXX))
                mid_link(nc.vector.reciprocal(tot[:, tb, :], tot[:, tb, :]))
                dve.wait_ge(pv_ready, n.count(NT, tb + 1))
                nc.vector.tensor_reduce(out=attn[:, tb, :], in_=pv[:, tb % 2, :, :].rearrange("p g c -> p c g"),
                                        op=ALU.add, axis=AXX).then_inc(o_done, 1)
                dve.wait_ge(o_done, n.count(NT, tb + 1))
                nc.vector.tensor_tensor(heads(attn[:, tb, :]), heads(attn[:, tb, :]),
                                        bc(tot[:, tb, :].unsqueeze(2), P, FH, HD), ALU.mult).then_inc(attn_ready, 1)
                if tb == NT - 1:
                    mid_link.end()

            def attended(n):
                link = post_link
                link.round(n)
                dve.wait_ge(wo_ps, n.count())
                dve.wait_ge(zb_ready, n.count())
                link(nc.vector.tensor_tensor(x1[:, :, :], ps[:, WIDE, :].rearrange("p (n d) -> p n d", n=NT),
                                             zb[:, n.slot, :, :], ALU.add))
                norm_statistics(nc, link, x1, stats2, mv2)
                link(nc.vector.tensor_tensor(ms2[:, :], mv2[:, :, 0], mv2[:, :, 0], ALU.mult))
                link(nc.vector.tensor_tensor(ms2[:, :], ms2[:, :], mv2[:, :, 1], ALU.add))
                nc.vector.tensor_scalar(ms2[:, :], ms2[:, :], RMS_EPS, None, ALU.add).then_inc(ms2_ready, 1)

            def scaled(n):
                dve.wait_ge(r2_ready, n.count())
                nc.vector.tensor_tensor(h2[:, :, :], x1[:, :, :], bc(r2[:, :].unsqueeze(2), P, NT, DM),
                                        ALU.mult).then_inc(h2_ready, 1)

            def logits(n):
                dve.wait_ge(lg_ps, n.count())
                post_link(nc.vector.tensor_tensor(lg[:, :, :], ps[:, WIDE, 0:NT * EX].rearrange("p (n e) -> p n e", n=NT),
                                                  bc(bg[:, :].unsqueeze(1), P, NT, EX), ALU.add))
                post_link(nc.vector.tensor_reduce(out=lmax[:, :], in_=lg[:, :, :], op=ALU.max, axis=AXX))
                nc.vector.tensor_tensor(lg[:, :, :], lg[:, :, :], bc(lmax[:, :].unsqueeze(2), P, NT, EX),
                                        ALU.subtract).then_inc(lg_ready, 1)

            def gates(n):
                dve.wait_ge(eg_ready, n.count())
                post_link(nc.vector.tensor_reduce(out=gsum[:, :], in_=lg[:, :, :], op=ALU.add, axis=AXX))
                post_link(nc.vector.reciprocal(gsum[:, :], gsum[:, :]))
                nc.vector.tensor_tensor(lg[:, :, :], lg[:, :, :], bc(gsum[:, :].unsqueeze(2), P, NT, EX),
                                        ALU.mult).then_inc(gates_ready, 1)

            def experts(n, tb):
                dve.wait_ge(mixed, n.count(2 * NT, 2 * tb + 2))
                nc.vector.tensor_reduce(out=comb[:, tb, :], in_=mix[:, tb % 2, :, :].rearrange("p e f -> p f e"),
                                        op=ALU.add, axis=AXX).then_inc(summed, 1)
                if tb == NT - 1:
                    dve.wait_ge(summed, n.count(NT))
                    dve.wait_ge(xr_ready, n.count())
                    dve.wait_ge(stored, n.count(16))
                    nc.vector.tensor_tensor(xn[:, :, :], xr[:, :, :], comb[:, :, :], ALU.add).then_inc(xn_ready, 1)
                    post_link.end()

            def body(post, mid, pre):
                if mid:
                    scores(mid, 0)
                    scores(mid, 1)
                if post:
                    attended(post)
                if pre:
                    statistics(pre)
                if mid:
                    less_maximum(mid, 0)
                    scores(mid, 2)
                if pre:
                    normalised(pre, mid)
                if mid:
                    less_maximum(mid, 1)
                if post:
                    scaled(post)
                if mid:
                    scores(mid, 3)
                    weighted(mid, 0)
                if post:
                    logits(post)
                if mid:
                    less_maximum(mid, 2)
                    weighted(mid, 1)
                    less_maximum(mid, 3)
                if post:
                    gates(post)
                if pre:
                    projected(pre)
                if mid:
                    weighted(mid, 2)
                if post:
                    experts(post, 0)
                    experts(post, 1)
                if mid:
                    weighted(mid, 3)
                if post:
                    experts(post, 2)
                    experts(post, 3)

            pipelined(dve, body)

        @block.tensor
        def _(pe):
            pe.wait_ge(weights_in, NW * 16)
            pe.wait_ge(consts_ready, 1)

            def scores(n, tb):
                pe.wait_ge(qk_ready, n.count(NT, tb + 1))
                if tb >= 2:
                    pe.wait_ge(s_ready, n.count(NT, tb - 1))
                for d in range(HD):
                    last = nc.tensor.matmul(ps[:, S0 + tb % 2, 0:256], ident[:, :],
                                            qk[:, tb % 2, d, :], start=(d == 0), stop=(d == HD - 1))
                last.then_inc(s_ps, 1)

            def turn(bank, src, done):
                for tb in range(NT):
                    last = nc.tensor.transpose(ps[:, bank, tb * P:(tb + 1) * P], src[:, tb, :], ident[:, :])
                last.then_inc(done, 1)

            def body(post, mid, pre):
                if post:
                    pe.wait_ge(attn_ready, post.count(NT))
                    if mid:
                        pe.wait_ge(qkv_ready, mid.count())
                    turn(TURN, attn, attnT_ps)
                    pe.wait_ge(attnT_ready, post.count())
                    for tb in range(NT):
                        last = nc.tensor.matmul(ps[:, WIDE, tb * P:(tb + 1) * P], attnT[:, tb * P:(tb + 1) * P], wo[:, :],
                                                start=True, stop=True)
                    last.then_inc(wo_ps, 1)
                if mid:
                    scores(mid, 0)
                    scores(mid, 1)
                    scores(mid, 2)
                if post:
                    pe.wait_ge(h2_ready, post.count())
                    turn(TURN, h2, h2T_ps)
                    pe.wait_ge(h2T_ready, post.count())
                    for tb in range(NT):
                        last = nc.tensor.matmul(ps[:, WIDE, tb * EX:(tb + 1) * EX], h2T[:, tb * P:(tb + 1) * P], wg[:, :],
                                                start=True, stop=True)
                    last.then_inc(lg_ps, 1)
                if mid:
                    scores(mid, 3)
                if pre:
                    pe.wait_ge(h_ready, pre.count())
                    if mid:
                        pe.wait_ge(qkv_ready, mid.count())
                    turn(KV0, hn, hT_ps)
                    pe.wait_ge(hT_ready, pre.count())
                    nc.tensor.matmul(ps[0:LAT, KV0 + 1, :], wdown[:, :], hT[:, :], start=True, stop=True)
                    for tb in range(NT):
                        last = nc.tensor.matmul(ps[:, TURN, tb * P:(tb + 1) * P], hT[:, tb * P:(tb + 1) * P], wq[:, :],
                                                start=True, stop=True)
                    last.then_inc(qd_ps, 1)
                    pe.wait_ge(down_ready, pre.count())
                    for tb in range(NT):
                        last = nc.tensor.matmul(ps[:, KV0 + tb // 2, (tb % 2) * 256:(tb % 2) * 256 + 256],
                                                down[:, tb * P:(tb + 1) * P], wup[:, :], start=True, stop=True)
                    last.then_inc(kv_ps, 1)
                if post:
                    for tb in range(NT):
                        for half in range(2):
                            if tb >= 1:
                                pe.wait_ge(mixed, post.count(2 * NT, 2 * tb - 1 + half))
                            nc.tensor.matmul(ps[:, EX0 + half, :], h2T[:, tb * P:(tb + 1) * P],
                                             we[:, half * HE:(half + 1) * HE, :].rearrange("p e f -> p (e f)"),
                                             start=True, stop=True).then_inc(ex_ps, 1)

            pipelined(pe, body)


def normalised_columns(nc, x_in, zt_d):
    with layer_scope(nc) as ctx:
        sb, sem = alloc(nc, ctx)
        ident, minus_half = sb("nz_ident", [P, P]), sb("nz_minus_half", [P, NT])
        xt, z, zT = sb("nz_xt", [P, 2, NT, DM]), sb("nz_z", [P, NT, DM]), sb("nz_zT", [P, 2, PAD + T])
        stats, mv = sb("nz_stats", [P, NT + 1, 6]), sb("nz_mv", [P, NT, 2])
        var, rstd = sb("nz_var", [P, NT]), sb("nz_rstd", [P, NT])
        ps = ctx.enter_context(nc.psum_tensor("nz_ps", [P, 2, 512], F32))
        pool_step, consts_ready, dve_step = sem("nz_pool_step"), sem("nz_consts_ready"), sem("nz_dve_step")
        x_loaded = [sem("nz_x_loaded0"), sem("nz_x_loaded1")]
        stored = [sem("nz_stored0"), sem("nz_stored1")]
        var_ready, rstd_ready, z_ready = sem("nz_var_ready"), sem("nz_rstd_ready"), sem("nz_z_ready")
        zT_ps, zT_ready = sem("nz_zT_ps"), sem("nz_zT_ready")
        block = ctx.enter_context(nc.Block())

        @block.sync
        def _(sp):
            for a in range(2):
                sp.dma_start(xt[:, a, :, :], rows(x_in, a)).then_inc(x_loaded[a], 16)
            with sp.Fori(0, B // 2 - 1) as i:
                for a in range(2):
                    sp.wait_ge(z_ready, i * 2 + a + 1)
                    sp.dma_start(xt[:, a, :, :], rows(x_in, i * 2 + 2 + a)).then_inc(x_loaded[a], 16)

        @block.gpsimd
        def _(pool):
            link = Chain(pool, pool_step)
            link(pool.memset(ident[:, :], 0.0))
            diagonal(pool, link, ident[:, :], 0, [[-1, P]])
            link(pool.memset(zT[:, :, 0:PAD], 0.0))
            pool.memset(minus_half[:, :], -0.5).then_inc(consts_ready, 1)
            pool.wait_ge(consts_ready, 1)
            with pool.Fori(0, B) as i:
                pool.wait_ge(var_ready, i + 1)
                power(pool, rstd[:, :], var[:, :], minus_half[:, :]).then_inc(rstd_ready, 1)

        @block.vector
        def _(dve):
            link = Chain(dve, dve_step, 4)
            with dve.Fori(0, B // 2) as i:
                link.round(i)
                for a in range(2):
                    dve.wait_ge(x_loaded[a], i * 16 + 16)
                    norm_statistics(nc, link, xt[:, a, :, :], stats, mv)
                    nc.vector.tensor_scalar(var[:, :], mv[:, :, 1], LN_EPS, None, ALU.add).then_inc(var_ready, 1)
                    dve.wait_ge(rstd_ready, i * 2 + a + 1)
                    dve.wait_ge(zT_ps, i * 2 + a + 1)
                    normalise(nc, xt[:, a, :, :], z, mv, rstd).then_inc(z_ready, 1)
                link.end()

        @block.tensor
        def _(pe):
            pe.sem_inc(zT_ps, 1)
            pe.wait_ge(consts_ready, 1)
            with pe.Fori(0, B // 2) as i:
                for a in range(2):
                    pe.wait_ge(z_ready, i * 2 + a + 1)
                    pe.wait_ge(zT_ready, i * 2 + a + 1)
                    for tb in range(NT):
                        last = nc.tensor.transpose(ps[:, 0, tb * P:(tb + 1) * P], z[:, tb, :], ident[:, :])
                    last.then_inc(zT_ps, 1)

        @block.scalar
        def _(act):
            act.sem_inc(zT_ready, 1)
            for a in range(2):
                act.sem_inc(stored[a], 16)
            act.wait_ge(consts_ready, 1)
            with act.Fori(0, B // 2) as i:
                for a in range(2):
                    act.wait_ge(zT_ps, i * 2 + a + 2)
                    act.wait_ge(stored[a], i * 16 + 16)
                    act.activation(zT[:, a, PAD:PAD + T], ps[:, 0, :], ACT.Copy).then_inc(zT_ready, 1)
                    act.wait_ge(zT_ready, i * 2 + a + 2)
                    act.dma_start(zt_d[:, i * 2 + a, :], zT[:, a, :]).then_inc(stored[a], 16)
            for a in range(2):
                act.wait_ge(stored[a], B // 2 * 16 + 16)


def projections(nc, zt_d, k_d, q_d, d_d, v_d, w):
    NP = T // PCH
    assert NP == B
    KD, VD = RH * RN, RH * RV
    VT = P // B
    NV = PCH // VT
    REP = RN // J
    V0, D0, SS = 4, 6, 6
    with layer_scope(nc) as ctx:
        sb, sem = alloc(nc, ctx)
        wq, wk, wv = sb("pr_wq", [P, KD]), sb("pr_wk", [P, KD]), sb("pr_wv", [P, VD])
        cq, ck, cv = sb("pr_cq", [P, TAPS, KD]), sb("pr_ck", [P, TAPS, KD]), sb("pr_cv", [P, TAPS, VD])
        wa, wa_rep = sb("pr_wa", [P, RH]), sb("pr_wa_rep", [P, HH, J, RN])
        a_log, dt_b, a_exp = sb("pr_a_log", [P, HH]), sb("pr_dt_b", [P, HH]), sb("pr_a_exp", [P, HH])
        head_sum, spread = sb("pr_head_sum", [P, J, REP]), sb("pr_spread", [P, 4, J, RN])
        zb = sb("pr_zb", [P, B, PAD + PCH])
        zc = sb("pr_zc", [P, 2, (PAD + PCH) * B])
        sg = sb("pr_sg", [P, 4, 512])
        act_kq = sb("pr_act_kq", [P, 4, 512])
        sq = sb("pr_sq", [P, 4, 512])
        root, inv = sb("pr_root", [P, 512]), sb("pr_inv", [P, 512])
        kq = sb("pr_kq", [P, 2, 2, HH, B, TCH])
        du, de = sb("pr_du", [P, HH, 512]), sb("pr_de", [P, HH, 512])
        dec = sb("pr_dec", [P, 2, HH, B, TCH])
        vv, vs = sb("pr_vv", [P, NV, VD]), sb("pr_vs", [P, 2, VD])
        rest, parts = sb("pr_rest", [P, NV, VD]), sb("pr_parts", [P, PARTS, NV, VD], BF16)
        ps = ctx.enter_context(nc.psum_tensor("pr_ps", [P, 8, 512], F32))

        weights_in, pool_step, consts_ready, a_ready, taps_ready = sem("pr_weights_in"), sem("pr_pool_step"), sem("pr_consts_ready"), sem("pr_a_ready"), sem("pr_taps_ready")
        dve_step, root_ready = sem("pr_dve_step"), sem("pr_root_ready")
        z_in, z_ready = sem("pr_z_in"), sem("pr_z_ready")
        kq_ps, kq_sig, kq_silu, kq_sq, ss_ps, inv_ready, inv_ps, kq_ready = sem("pr_kq_ps"), sem("pr_kq_sig"), sem("pr_kq_silu"), sem("pr_kq_sq"), sem("pr_ss_ps"), sem("pr_inv_ready"), sem("pr_inv_ps"), sem("pr_kq_ready")
        d_ps, du_ready, de_ready, ln_ready, dl_ready, d_ready = sem("pr_d_ps"), sem("pr_du_ready"), sem("pr_de_ready"), sem("pr_ln_ready"), sem("pr_dl_ready"), sem("pr_d_ready")
        v_ps, v_sig, v_ready = sem("pr_v_ps"), sem("pr_v_sig"), sem("pr_v_ready")
        hi_ready, rest_ready, mid_ready, lo_ready = sem("pr_hi_ready"), sem("pr_rest_ready"), sem("pr_mid_ready"), sem("pr_lo_ready")
        d_stored, kq_stored, v_stored = sem("pr_d_stored"), sem("pr_kq_stored"), sem("pr_v_stored")
        block = ctx.enter_context(nc.Block())
        NW = 7 + 2 * J

        @block.sync
        def _(sp):
            for dst, src in ((wq[:, :], w["Wq"]), (wk[:, :], w["Wk"]), (wv[:, :], w["Wv"]), (wa[:, :], w["Wa"])):
                sp.dma_start(dst, src).then_inc(weights_in, 16)
            for dst, src, n in ((cq, w["q_conv_w"], KD), (ck, w["k_conv_w"], KD), (cv, w["v_conv_w"], VD)):
                sp.dma_start(dst[:, :, :], bc(src.unsqueeze(0), P, TAPS, n)).then_inc(weights_in, 16)
            for j in range(J):
                sp.dma_start(a_log[RN * j:RN * (j + 1), :], bc(w["A_log"][j:j + 1, :], RN, HH)).then_inc(weights_in, 16)
                sp.dma_start(dt_b[RN * j:RN * (j + 1), :], bc(w["dt_bias"][j:j + 1, :], RN, HH)).then_inc(weights_in, 16)

            def body(post, mid, pre):
                if pre:
                    if mid:
                        sp.wait_ge(z_ready, mid.count())
                    sp.dma_start(zb[:, :, :], zt_d[:, :, bass.ds(pre.index() * PCH, PAD + PCH)]).then_inc(z_in, 16)
                if mid:
                    sp.wait_ge(lo_ready, mid.count(NV))
                    for part in range(PARTS):
                        for m in range(NV):
                            for h in range(HH):
                                sp.dma_start(v_d[part * HH + h, bass.ds(mid.index() * PCH + m * VT, VT)].rearrange("t (b j) v -> (t b) (j v)", j=J),
                                             parts[:, part, m, h * J * RV:(h + 1) * J * RV]).then_inc(v_stored, 16)
                    sp.wait_ge(kq_ready, mid.count(4))
                    for c in range(2):
                        for a, dst in enumerate((q_d, k_d)):
                            sp.dma_start(dst[mid.index() * 2 + c], kq[:, a, c, :, :, :].rearrange("p h b t -> p (h b t)")).then_inc(kq_stored, 16)
                    sp.wait_ge(d_ready, mid.count())
                    for c in range(2):
                        sp.dma_start(d_d[mid.index() * 2 + c], dec[:, c, :, :, :].rearrange("p h b t -> p (h b t)")).then_inc(d_stored, 16)

            pipelined(sp, body)
            sp.wait_ge(v_stored, NP * PARTS * NV * HH * 16)
            sp.wait_ge(kq_stored, NP * 4 * 16)
            sp.wait_ge(d_stored, NP * 2 * 16)
            for dst in (k_d, q_d, d_d):
                sp.dma_start(dst[2 * NP:2 * NP + 2], dst[0:2]).then_inc(d_stored, 16)
            sp.dma_start(v_d[:, T:T + PCH], v_d[:, 0:PCH]).then_inc(v_stored, 16)
            sp.wait_ge(d_stored, (NP * 2 + 3) * 16)
            sp.wait_ge(v_stored, (NP * PARTS * NV * HH + 1) * 16)

        @block.gpsimd
        def _(pool):
            link = Chain(pool, pool_step)
            link(pool.memset(head_sum[:, :, :], 1.0))
            link(pool.affine_select(out=head_sum[:, :, :], in_=head_sum[:, :, :], compare_op=ALU.is_ge, fill=0.0, base=0,
                                    pattern=[[-RN, J], [0, REP]], channel_multiplier=1))
            link(pool.affine_select(out=head_sum[:, :, :], in_=head_sum[:, :, :], compare_op=ALU.is_ge, fill=0.0, base=RN - 1,
                                    pattern=[[RN, J], [0, REP]], channel_multiplier=-1))
            link(pool.memset(spread[:, :, :, :], 0.0))
            for n in range(4):
                diagonal(pool, link, spread[:, n, :, :], -RN * n, [[-REP, J], [0, RN]])
            pool.drain().then_inc(consts_ready, 1)

            def body(post, mid, pre):
                for m in range(NV if mid else 0):
                    pool.wait_ge(hi_ready, mid.count(NV, m + 1))
                    pool.tensor_tensor(rest[:, m, :], vv[:, m, :], parts[:, 0, m, :], ALU.subtract).then_inc(rest_ready, 1)
                    pool.wait_ge(mid_ready, mid.count(NV, m + 1))
                    pool.tensor_tensor(parts[:, 2, m, :], rest[:, m, :], parts[:, 1, m, :], ALU.subtract).then_inc(lo_ready, 1)

            pipelined(pool, body)

        @block.scalar
        def _(act):
            act.wait_ge(weights_in, NW * 16)
            act.activation(a_exp[:, :], a_log[:, :], ACT.Exp).then_inc(a_ready, 1)

            def value_sigmoid(n, m):
                act.wait_ge(v_ps, n.count(NV, m + 1))
                if m >= 2:
                    act.wait_ge(v_ready, n.count(NV, m - 1))
                act.activation(vs[:, m % 2, :], ps[:, V0 + m % 2, :], ACT.Sigmoid).then_inc(v_sig, 1)

            def upper_parts(n, m):
                act.wait_ge(v_ready, n.count(NV, m + 1))
                act.activation(parts[:, 0, m, :], vv[:, m, :], ACT.Copy).then_inc(hi_ready, 1)
                act.wait_ge(rest_ready, n.count(NV, m + 1))
                act.activation(parts[:, 1, m, :], rest[:, m, :], ACT.Copy).then_inc(mid_ready, 1)

            def body(post, mid, pre):
                if mid:
                    act.wait_ge(kq_ps, mid.count())
                    act.activation(sg[:, :, :], ps[:, 0:4, :], ACT.Sigmoid).then_inc(kq_sig, 1)
                    value_sigmoid(mid, 0)
                    act.wait_ge(kq_silu, mid.count())
                    act.activation(sq[:, :, :], act_kq[:, :, :], ACT.Square).then_inc(kq_sq, 1)
                    value_sigmoid(mid, 1)
                    if post:
                        act.wait_ge(v_stored, post.count(PARTS * NV * HH * 16))
                    upper_parts(mid, 0)
                if pre:
                    act.wait_ge(z_in, pre.count(16))
                    act.activation(zc[:, pre.slot, :].rearrange("p (t b) -> p b t", b=B), zb[:, :, :], ACT.Copy).then_inc(z_ready, 1)
                if mid:
                    act.wait_ge(ss_ps, mid.count())
                    act.activation(root[:, :], ps[:, SS, :], ACT.Sqrt).then_inc(root_ready, 1)
                    value_sigmoid(mid, 2)
                    upper_parts(mid, 1)
                    value_sigmoid(mid, 3)
                    upper_parts(mid, 2)
                    act.wait_ge(du_ready, mid.count())
                    act.activation(de[:, :, :], de[:, :, :], ACT.Exp, scale=-1.0).then_inc(de_ready, 1)
                    act.wait_ge(de_ready, mid.count())
                    act.activation(de[:, :, :], de[:, :, :], ACT.Ln, bias=1.0).then_inc(ln_ready, 1)
                    upper_parts(mid, 3)
                    act.wait_ge(dl_ready, mid.count())
                    if post:
                        act.wait_ge(d_stored, post.count(2 * 16))
                    for h in range(HH):
                        last = act.activation(dec[:, :, h, :, :].rearrange("p c b t -> p c t b"),
                                              du[:, h, :].rearrange("p (c t b) -> p c t b", b=B, c=2), ACT.Exp,
                                              scale=-1.0)
                    last.then_inc(d_ready, 1)

            pipelined(act, body)

        @block.vector
        def _(dve):
            dve.wait_ge(weights_in, NW * 16)
            for c, m, n in ((cq, wq, KD), (ck, wk, KD), (cv, wv, VD)):
                nc.vector.tensor_tensor(c[:, :, :], c[:, :, :], bc(m[:, :].unsqueeze(1), P, TAPS, n), ALU.mult)
            nc.vector.tensor_copy(wa_rep[:, :, :, :], bc(wa[:, :].rearrange("p (h j) -> p h j", h=HH).unsqueeze(3), P, HH, J, RN)).then_inc(taps_ready, 1)
            dve.wait_ge(a_ready, 1)
            link = Chain(dve, dve_step, 3)

            def values(n, m):
                dve.wait_ge(v_sig, n.count(NV, m + 1))
                nc.vector.tensor_tensor(vv[:, m, :], vs[:, m % 2, :], ps[:, V0 + m % 2, :], ALU.mult).then_inc(v_ready, 1)

            def body(post, mid, pre):
                if mid:
                    link.round(mid)
                    dve.wait_ge(kq_sig, mid.count())
                    nc.vector.tensor_tensor(act_kq[:, :, :], sg[:, :, :], ps[:, 0:4, :], ALU.mult).then_inc(kq_silu, 1)
                    dve.wait_ge(d_ps, mid.count())
                    if post:
                        dve.wait_ge(d_ready, post.count())
                    for h in range(HH):
                        last = nc.vector.tensor_scalar(du[:, h, :], ps[:, D0 + h, :], dt_b[:, h:h + 1], None, ALU.add)
                    link(last)
                    nc.vector.scalar_tensor_tensor(out=de[:, :, :], in0=du[:, :, :], scalar=-1.0, in1=du[:, :, :],
                                                   op0=ALU.mult, op1=ALU.max).then_inc(du_ready, 1)
                    if post:
                        dve.wait_ge(lo_ready, post.count(NV))
                    values(mid, 0)
                    values(mid, 1)
                    dve.wait_ge(root_ready, mid.count())
                    link(nc.vector.tensor_scalar(inv[:, :], root[:, :], 1e-6, None, ALU.add))
                    nc.vector.reciprocal(inv[:, :], inv[:, :]).then_inc(inv_ready, 1)
                    values(mid, 2)
                    values(mid, 3)
                    if post:
                        dve.wait_ge(kq_stored, post.count(4 * 16))
                    for a in range(2):
                        for h in range(HH):
                            n = a * HH + h
                            dve.wait_ge(inv_ps, mid.count(4, n + 1))
                            nc.vector.tensor_tensor(kq[:, a, :, h, :, :].rearrange("p c b t -> p c t b"),
                                                    act_kq[:, n, :].rearrange("p (c t b) -> p c t b", b=B, c=2),
                                                    ps[:, SS + (n + 1) % 2, :].rearrange("p (c t b) -> p c t b", b=B, c=2),
                                                    ALU.mult).then_inc(kq_ready, 1)
                    dve.wait_ge(ln_ready, mid.count())
                    link(nc.vector.scalar_tensor_tensor(out=du[:, :, :], in0=du[:, :, :], scalar=0.0, in1=de[:, :, :],
                                                        op0=ALU.max, op1=ALU.add))
                    for h in range(HH):
                        last = nc.vector.tensor_scalar(du[:, h, :], du[:, h, :], a_exp[:, h:h + 1], None, ALU.mult)
                    last.then_inc(dl_ready, 1)
                    link.end()

            pipelined(dve, body)

        @block.tensor
        def _(pe):
            pe.wait_ge(taps_ready, 1)
            pe.wait_ge(consts_ready, 1)
            pe.wait_ge(weights_in, NW * 16)

            def values(n, m):
                if m >= 2:
                    pe.wait_ge(v_ready, n.count(NV, m - 1))
                for tap in range(TAPS):
                    last = nc.tensor.matmul(ps[:, V0 + m % 2, :], zc[:, n.slot, (tap + VT * m) * B:(tap + VT * (m + 1)) * B],
                                            cv[:, tap, :], start=(tap == 0), stop=(tap == TAPS - 1))
                last.then_inc(v_ps, 1)

            def body(post, mid, pre):
                if mid:
                    pe.wait_ge(z_ready, mid.count())
                    for n, (c, h) in enumerate(((cq, 0), (cq, 1), (ck, 0), (ck, 1))):
                        for tap in range(TAPS):
                            last = nc.tensor.matmul(ps[:, n, :], c[:, tap, h * P:(h + 1) * P],
                                                    zc[:, mid.slot, tap * B:(tap + PCH) * B],
                                                    start=(tap == 0), stop=(tap == TAPS - 1))
                    last.then_inc(kq_ps, 1)
                    if post:
                        pe.wait_ge(kq_ready, post.count(4))
                    for h in range(HH):
                        last = nc.tensor.matmul(ps[:, D0 + h, :], wa_rep[:, h, :, :].rearrange("p j n -> p (j n)"),
                                                zc[:, mid.slot, PAD * B:(PAD + PCH) * B], start=True, stop=True)
                    last.then_inc(d_ps, 1)
                    values(mid, 0)
                    values(mid, 1)
                    pe.wait_ge(kq_sq, mid.count())
                    pe.wait_ge(du_ready, mid.count())
                    for n in range(4):
                        last = nc.tensor.matmul(ps[RN * n:RN * (n + 1), SS, :], head_sum[:, :, :].rearrange("p j r -> p (j r)"),
                                                sq[:, n, :], start=True, stop=True)
                    last.then_inc(ss_ps, 1)
                    values(mid, 2)
                    values(mid, 3)
                    pe.wait_ge(inv_ready, mid.count())
                    for n in range(4):
                        if n >= 2:
                            pe.wait_ge(kq_ready, mid.count(4, n - 1))
                        nc.tensor.matmul(ps[:, SS + (n + 1) % 2, :], spread[:, n, :, :].rearrange("p j r -> p (j r)"),
                                         inv[:, :], start=True, stop=True).then_inc(inv_ps, 1)

            pipelined(pe, body)


def recurrence(nc, k_d, q_d, d_d, v_d, sq_d):
    SR = 2 * TCH
    NB = SR // BLK
    LD = 16 * (3 + PARTS * NC)
    PC = P // NC
    PIECES = [(c * CW, CW, c) for c in range(2)]
    for c in range(2, NC):
        PIECES += [(c * CW, CW // 2, c), (c * CW + CW // 2, CW // 2, c - 2)]
    NPC = len(PIECES)
    LAST = [1, 2, 4, 6]
    with layer_scope(nc) as ctx:
        sb, sem = alloc(nc, ctx)
        kc, qc, dc = sb("rc_kc", [P, 2, G, TCH]), sb("rc_qc", [P, 2, G, TCH]), sb("rc_dc", [P, 2, G, TCH])
        vc = sb("rc_vc", [PARTS * PC, 2, NC, TCH, RV], BF16)
        sum_parts = sb("rc_sum_parts", [PARTS * PC, PC], BF16)
        kb, qb = sb("rc_kb", [P, 2, BLK, P]), sb("rc_qb", [P, 2, BLK, P])
        kt = sb("rc_kt", [P, 2, GRP, NC, P])
        state = sb("rc_state", [P, 2, G * RV])
        faded, arg = sb("rc_faded", [P, G * RV]), sb("rc_arg", [P, G * RV])
        delta = sb("rc_delta", [P, 2, CW])
        ring = sb("rc_ring", [P, 2, BLK, CW])
        ident = sb("rc_ident", [P, P])
        neg_head, one_head = sb("rc_neg_head", [P, J]), sb("rc_one_head", [P, J])
        own4, neg_own = sb("rc_own4", [P, NC, CG]), sb("rc_neg_own", [P, CG])
        ps = ctx.enter_context(nc.psum_tensor("rc_ps", [P, 8, 512], F32))
        RB, QB, TB = 4, 6, 7

        pool_step, consts_ready, own_ready = sem("rc_pool_step"), sem("rc_consts_ready"), sem("rc_own_ready")
        chunk_in = [sem("rc_chunk_in0"), sem("rc_chunk_in1")]
        k_built, q_built = sem("rc_k_built"), sem("rc_q_built")
        kt_ps, kt_copied = sem("rc_kt_ps"), sem("rc_kt_copied")
        state_ready = sem("rc_state_ready")
        r_ps, delta_ready, up_ps, faded_ready, arg_ready = sem("rc_r_ps"), sem("rc_delta_ready"), sem("rc_up_ps"), sem("rc_faded_ready"), sem("rc_arg_ready")
        q_ps, q_copied = sem("rc_q_ps"), sem("rc_q_copied")
        ring_out = [sem("rc_ring_out0"), sem("rc_ring_out1")]
        block = ctx.enter_context(nc.Block())

        def cols(c):
            return slice(c * CW, (c + 1) * CW)

        @block.sync
        def _(sp):
            def load(par, chunk, t0):
                for dst, src in ((kc, k_d), (qc, q_d), (dc, d_d)):
                    sp.dma_start(dst[:, par, :, :].rearrange("p g t -> p (g t)"), src[chunk]).then_inc(chunk_in[par], 16)
                for part in range(PARTS):
                    for c in range(NC):
                        r0 = c % (NC // HH) * PC
                        sp.dma_start(vc[part * PC:(part + 1) * PC, par, c, :, :],
                                     v_d[part * HH + c * HH // NC, bass.ds(t0, TCH), r0:r0 + PC].rearrange("t r v -> r t v")).then_inc(chunk_in[par], 16)

            for par in range(2):
                sp.sem_inc(ring_out[par], 16)
                load(par, par, par * TCH)
            with sp.Fori(0, T // SR) as i:
                for blk in range(NB):
                    sp.wait_ge(q_copied, i * SR + (blk + 1) * BLK + 1)
                    for c in range(NC):
                        for g in range(CG):
                            p0 = 32 * c + J * g
                            sp.dma_start(sq_d[p0:p0 + J, bass.ds(i * SR + blk * BLK, BLK), :],
                                         ring[p0:p0 + J, blk % 2, :, g * RV:(g + 1) * RV]).then_inc(ring_out[blk % 2], 16)
                    if blk % 2 == 1:
                        par = blk // 2
                        sp.wait_ge(arg_ready, i * SR * NPC + NPC * TCH * (par + 1))
                        load(par, i * 2 + 2 + par, i * SR + SR + par * TCH)
            for par in range(2):
                sp.wait_ge(ring_out[par], T // SR * NB // 2 * 32 * 16 + 16)
                sp.wait_ge(chunk_in[par], (T // SR + 1) * LD)

        @block.gpsimd
        def _(pool):
            link = Chain(pool, pool_step)
            link(pool.memset(ident[:, :], 0.0))
            diagonal(pool, link, ident[:, :], 0, [[-1, P]])
            link(pool.memset(sum_parts[:, :], 0.0))
            for part in range(PARTS):
                diagonal(pool, link, sum_parts[:, :], -PC * part, [[-1, PC]])
            for m, value in ((neg_head, -1.0), (one_head, 1.0)):
                link(pool.memset(m[:, :], value))
                link(pool.affine_select(out=m[:, :], in_=m[:, :], compare_op=ALU.is_ge, fill=0.0, base=0,
                                        pattern=[[-RN, J]], channel_multiplier=1))
                link(pool.affine_select(out=m[:, :], in_=m[:, :], compare_op=ALU.is_ge, fill=0.0, base=RN - 1,
                                        pattern=[[RN, J]], channel_multiplier=-1))
            link(pool.memset(own4[:, :, :], -1.0))
            link(pool.affine_select(out=own4[:, :, :], in_=own4[:, :, :], compare_op=ALU.is_ge, fill=0.0, base=0,
                                    pattern=[[-32, NC], [-J, CG]], channel_multiplier=1))
            link(pool.affine_select(out=own4[:, :, :], in_=own4[:, :, :], compare_op=ALU.is_ge, fill=0.0, base=J - 1,
                                    pattern=[[32, NC], [J, CG]], channel_multiplier=-1))
            pool.memset(kt[:, :, :, :, :], 0.0).then_inc(consts_ready, 1)
            with pool.Fori(0, T // SR) as i:
                for s in range(SR):
                    par = s // TCH
                    if s % TCH == 0:
                        pool.wait_ge(chunk_in[par], i * LD + LD)
                    for n, (c0, width, _) in enumerate(PIECES):
                        pool.wait_ge(state_ready, i * SR * NPC + NPC * s + n + 1)
                        pool.tensor_tensor(faded[:, c0:c0 + width].rearrange("p (g v) -> p g v", v=RV),
                                           state[:, (s + 1) % 2, c0:c0 + width].rearrange("p (g v) -> p g v", v=RV),
                                           bc(dc[:, par, c0 // RV:(c0 + width) // RV, s % TCH].unsqueeze(2), P, width // RV, RV),
                                           ALU.mult).then_inc(faded_ready, 1)

        @block.vector
        def _(dve):
            dve.wait_ge(consts_ready, 1)
            nc.vector.tensor_reduce(out=neg_own[:, :], in_=own4[:, :, :].rearrange("p c g -> p g c"), op=ALU.add,
                                    axis=AXX).then_inc(own_ready, 1)
            for c0, width, _ in PIECES:
                nc.vector.memset(state[:, 1, c0:c0 + width], 0.0).then_inc(state_ready, 1)
            dve.wait_ge(own_ready, 1)

            HB = BLK // 2

            def build(dst, slot, src, half, par, head, part):
                t0 = half * BLK + part * HB
                return nc.vector.tensor_tensor(
                    dst[:, slot, part * HB:(part + 1) * HB, :].rearrange("p t (g j) -> p t g j", j=J),
                    bc(src[:, par, :, t0:t0 + HB].rearrange("p g t -> p t g").unsqueeze(3), P, HB, G, J),
                    bc(head[:, :].unsqueeze(1).unsqueeze(1), P, HB, G, J), ALU.mult)

            dve.wait_ge(chunk_in[0], LD)
            for part in range(2):
                last = build(kb, 0, kc, 0, 0, neg_head, part)
            last.then_inc(k_built, 1)
            for part in range(2):
                last = build(qb, 0, qc, 0, 0, one_head, part)
            last.then_inc(q_built, 1)
            with dve.Fori(0, T // SR) as i:
                for s in range(SR):
                    dve.wait_ge(r_ps, i * SR + s + 1)
                    nc.vector.tensor_tensor(delta[:, s % 2, :].rearrange("p (g v) -> p g v", v=RV),
                                            ps[:, RB + s % 2, :].rearrange("p (g v) -> p g v", v=RV),
                                            bc(neg_own[:, :].unsqueeze(2), P, CG, RV), ALU.mult).then_inc(delta_ready, 1)
                    nb = s // BLK + 1
                    par = nb // 2 % 2
                    if s % BLK == 1:
                        dve.wait_ge(q_ps, i * SR + s + 1)
                        if nb % 2 == 0:
                            dve.wait_ge(chunk_in[par], i * LD + (2 * LD if nb == NB else LD))
                    if s % BLK in (1, 2):
                        last = build(kb, nb % 2, kc, nb % 2, par, neg_head, s % BLK - 1)
                        if s % BLK == 2:
                            last.then_inc(k_built, 1)
                    if s % BLK in (3, 4):
                        last = build(qb, nb % 2, qc, nb % 2, par, one_head, s % BLK - 3)
                        if s % BLK == 4:
                            last.then_inc(q_built, 1)
                    for n, (c0, width, bank) in enumerate(PIECES):
                        dve.wait_ge(up_ps, i * SR * NPC + NPC * s + n + 1)
                        dve.wait_ge(faded_ready, i * SR * NPC + NPC * s + n + 1)
                        nc.vector.tensor_tensor(arg[:, c0:c0 + width], faded[:, c0:c0 + width], ps[:, bank, 0:width],
                                                ALU.add).then_inc(arg_ready, 1)

        @block.scalar
        def _(act):
            def copy_turned(slot, c0, n):
                for c in range(c0, c0 + n):
                    act.activation(kt[32 * c:32 * c + 32, slot, :, c, :],
                                   ps[32 * c:32 * c + 32, TB, :].rearrange("p (t m) -> p t m", t=GRP),
                                   ACT.Copy).then_inc(kt_copied, 1)

            def copy_answer(i, s):
                act.wait_ge(q_ps, i * SR + s + 2)
                if s % BLK == 0:
                    act.wait_ge(ring_out[s // BLK % 2], (i * (NB // 2) + s // BLK // 2) * 512 + 16)
                act.activation(ring[:, s // BLK % 2, s % BLK, :], ps[:, QB, :], ACT.Copy).then_inc(q_copied, 1)

            act.sem_inc(q_copied, 1)
            act.wait_ge(consts_ready, 1)
            act.wait_ge(kt_ps, 1)
            copy_turned(0, 0, NC)
            with act.Fori(0, T // SR) as i:
                for s in range(SR):
                    if s > 0:
                        copy_answer(i, s - 1)
                    for n, (c0, width, _) in enumerate(PIECES):
                        act.wait_ge(arg_ready, i * SR * NPC + NPC * s + n + 1)
                        if s == 0 and n == 0:
                            act.wait_ge(q_ps, i * SR + 1)
                        act.activation(state[:, s % 2, c0:c0 + width], arg[:, c0:c0 + width], ACT.Tanh).then_inc(state_ready, 1)
                    grp = s // GRP
                    if s % GRP == 1:
                        act.wait_ge(kt_ps, i * (SR // GRP) + grp + 2)
                        copy_turned((grp + 1) % 2, 0, 2)
                    if s % GRP == 2:
                        copy_turned((grp + 1) % 2, 2, 2)
                copy_answer(i, SR - 1)

        @block.tensor
        def _(pe):
            def place_values(bank, par, t):
                for c in range(NC):
                    last = nc.tensor.matmul(ps[32 * c:32 * c + 32, bank, :].rearrange("p (g v) -> p g v", v=RV),
                                            sum_parts[:, :], bc(vc[:, par, c, t, :].unsqueeze(1), PARTS * PC, CG, RV),
                                            start=True, stop=False, skip_group_check=True)

            def turn_keys(slot, first):
                for t in range(GRP):
                    last = nc.tensor.transpose(ps[:, TB, t * P:(t + 1) * P], kb[:, slot, first + t, :], ident[:, :])
                last.then_inc(kt_ps, 1)

            def answer(i, s):
                for c in range(NC):
                    pe.wait_ge(state_ready, i * SR * NPC + NPC * (s + 1) + LAST[c])
                    if c == 0:
                        pe.wait_ge(q_copied, i * SR + s + 1)
                    last = nc.tensor.matmul(ps[32 * c:32 * c + 32, QB, :], qb[:, s // BLK % 2, s % BLK, 32 * c:32 * c + 32],
                                            state[:, s % 2, cols(c)], start=True, stop=True)
                last.then_inc(q_ps, 1)

            pe.sem_inc(q_ps, 1)
            pe.wait_ge(consts_ready, 1)
            pe.wait_ge(k_built, 1)
            turn_keys(0, 0)
            pe.wait_ge(chunk_in[0], LD)
            place_values(RB, 0, 0)
            with pe.Fori(0, T // SR) as i:
                for s in range(SR):
                    blk, grp = s // BLK, s // GRP
                    if s % BLK == 0:
                        pe.wait_ge(k_built, i * NB + blk + 1)
                        pe.wait_ge(q_built, i * NB + blk + 1)
                    for c in range(NC):
                        if c == NC - 1:
                            if (s + 1) % TCH == 0:
                                par = (s + 1) // TCH % 2
                                pe.wait_ge(chunk_in[par], i * LD + (2 * LD if par == 0 else LD))
                            place_values(RB + (s + 1) % 2, (s + 1) // TCH % 2, (s + 1) % TCH)
                            if s % GRP == 0:
                                n = grp + 1
                                pe.wait_ge(kt_copied, (i * (SR // GRP) + grp + 1) * NC)
                                if n % 2 == 0:
                                    pe.wait_ge(k_built, i * NB + n // 2 + 1)
                                turn_keys(n // 2 % 2, (n % 2) * GRP)
                        pe.wait_ge(state_ready, i * SR * NPC + NPC * s + LAST[c])
                        last = nc.tensor.matmul(ps[32 * c:32 * c + 32, RB + s % 2, :],
                                                kb[:, blk % 2, s % BLK, 32 * c:32 * c + 32],
                                                state[:, (s + 1) % 2, cols(c)], start=False, stop=True,
                                                skip_group_check=True)
                    last.then_inc(r_ps, 1)
                    if s > 0:
                        answer(i, s - 1)
                    pe.wait_ge(delta_ready, i * SR + s + 1)
                    for n, (c0, width, bank) in enumerate(PIECES):
                        if n >= 2 and bank < 2:
                            pe.wait_ge(arg_ready, i * SR * NPC + NPC * s + bank + 1)
                        nc.tensor.matmul(ps[:, bank, 0:width], kt[:, grp % 2, s % GRP, c0 // CW, :],
                                         delta[:, s % 2, c0 % CW:c0 % CW + width], start=True, stop=True).then_inc(up_ps, 1)
                answer(i, SR - 1)


def outputs(nc, x_in, x_out, zt_d, sq_d, w):
    VD = RH * RV
    NVT = VD // P
    OT, WO = 4, 6
    with layer_scope(nc) as ctx:
        sb, sem = alloc(nc, ctx)
        ident, minus_half = sb("po_ident", [P, P]), sb("po_minus_half", [P, NT, RH])
        wg, wo, onorm = sb("po_wg", [P, VD]), sb("po_wo", [P, NVT, DM]), sb("po_onorm", [P, 1])
        xt, xn, zT = sb("po_xt", [P, NT, DM]), sb("po_xn", [P, NT, DM]), sb("po_zT", [P, 2, T])
        s, e, o2 = sb("po_s", [P, 2, NT, VD]), sb("po_e", [P, NT, VD]), sb("po_o2", [P, NT, VD])
        o, eg, y = sb("po_o", [P, NT, VD]), sb("po_eg", [P, NT, VD]), sb("po_y", [P, 2, NT, VD])
        ssum, rms = sb("po_ssum", [P, NT, RH]), sb("po_rms", [P, NT, RH])
        oT = sb("po_oT", [P, 2, VD])
        ps = ctx.enter_context(nc.psum_tensor("po_ps", [P, 8, 512], F32))
        weights_in, pool_step, consts_ready, dve_step = sem("po_weights_in"), sem("po_pool_step"), sem("po_consts_ready"), sem("po_dve_step")
        loaded = [sem("po_loaded0"), sem("po_loaded1")]
        xt_loaded, wo_ready = sem("po_xt_loaded"), sem("po_wo_ready")
        g_ps, eg_ready, s_ready, sq_ready = sem("po_g_ps"), sem("po_eg_ready"), sem("po_s_ready"), sem("po_sq_ready")
        o_ready, o2_ready, oe_ready, ss_ready, rms_ready, y_ready = sem("po_o_ready"), sem("po_o2_ready"), sem("po_oe_ready"), sem("po_ss_ready"), sem("po_rms_ready"), sem("po_y_ready")
        oT_ps, oT_ready, wo_ps, xn_ready, stored = sem("po_oT_ps"), sem("po_oT_ready"), sem("po_wo_ps"), sem("po_xn_ready"), sem("po_stored")
        block = ctx.enter_context(nc.Block())
        NL = 1 + NT * HH
        sq_v = sq_d.rearrange("(h b j) t v -> b h t j v", h=HH, j=J)

        @block.sync
        def _(sp):
            for dst, src in ((wg[:, :], w["Wg"]), (wo[:, :, :], w["Wo"].rearrange("(c p) n -> p c n", p=P)),
                             (onorm[0:RV, :], w["o_norm_w"]), (onorm[RV:P, :], w["o_norm_w"])):
                sp.dma_start(dst, src).then_inc(weights_in, 16)
            sp.sem_inc(stored, 16)

            def body(post, mid, pre):
                if pre:
                    if post:
                        sp.wait_ge(o_ready, post.count())
                        sp.wait_ge(g_ps, post.count())
                    sp.dma_start(zT[:, pre.slot, :], zt_d[:, pre.index(), PAD:PAD + T]).then_inc(loaded[pre.slot], 16)
                    for tb in range(NT):
                        for h in range(HH):
                            sp.dma_start(s[:, pre.slot, tb, h * J * RV:(h + 1) * J * RV].rearrange("p (j v) -> p j v", j=J),
                                         sq_v[pre.index(), h, tb * P:(tb + 1) * P]).then_inc(loaded[pre.slot], 16)
                if post:
                    sp.wait_ge(xn_ready, post.count())
                    sp.dma_start(rows(x_out, post.index()), xn[:, :, :]).then_inc(stored, 16)
                if mid:
                    sp.dma_start(xt[:, :, :], rows(x_in, mid.index())).then_inc(xt_loaded, 16)

            pipelined(sp, body)
            sp.wait_ge(stored, B * 16 + 16)

        @block.gpsimd
        def _(pool):
            link = Chain(pool, pool_step)
            link(pool.memset(ident[:, :], 0.0))
            diagonal(pool, link, ident[:, :], 0, [[-1, P]])
            pool.memset(minus_half[:, :, :], -0.5).then_inc(consts_ready, 1)
            pool.wait_ge(consts_ready, 1)

            def body(post, mid, pre):
                if mid:
                    pool.wait_ge(ss_ready, mid.count())
                    power(pool, rms[:, :, :], ssum[:, :, :], minus_half[:, :, :]).then_inc(rms_ready, 1)
                    pool.wait_ge(rms_ready, mid.count())
                    pool.wait_ge(oe_ready, mid.count())
                    pool.tensor_tensor(y[:, mid.slot, :, :].rearrange("p n (h v) -> p (n h) v", v=RV),
                                       o[:, :, :].rearrange("p n (h v) -> p (n h) v", v=RV),
                                       bc(rms[:, :, :].rearrange("p n h -> p (n h)").unsqueeze(2), P, NT * RH, RV),
                                       ALU.mult).then_inc(y_ready, 1)

            pipelined(pool, body)

        @block.scalar
        def _(act):
            def body(post, mid, pre):
                if mid:
                    act.wait_ge(loaded[mid.slot], mid.slot_count(NL * 16))
                    act.activation(e[:, :, :], s[:, mid.slot, :, :], ACT.Sigmoid).then_inc(s_ready, 1)
                    act.activation(s[:, mid.slot, :, :], s[:, mid.slot, :, :], ACT.Square).then_inc(sq_ready, 1)
                    act.wait_ge(g_ps, mid.count())
                    if post:
                        act.wait_ge(oe_ready, post.count())
                    act.activation(eg[:, :, :], ps[:, 0:NT, :], ACT.Sigmoid).then_inc(eg_ready, 1)
                    act.wait_ge(o_ready, mid.count())
                    act.activation(o2[:, :, :], o[:, :, :], ACT.Square).then_inc(o2_ready, 1)
                if post:
                    for tb in range(NT):
                        act.wait_ge(oT_ps, post.count(NT, tb + 1))
                        act.activation(oT[:, tb % 2, :], ps[:, OT + tb % 2, :], ACT.Copy).then_inc(oT_ready, 1)

            pipelined(act, body)

        @block.vector
        def _(dve):
            dve.wait_ge(weights_in, 4 * 16)
            nc.vector.tensor_tensor(wo[:, :, :], wo[:, :, :], bc(onorm[:, :].unsqueeze(2), P, NVT, DM),
                                    ALU.mult).then_inc(wo_ready, 1)
            link = Chain(dve, dve_step, 1)

            def body(post, mid, pre):
                if mid:
                    link.round(mid)
                    dve.wait_ge(sq_ready, mid.count())
                    if post:
                        dve.wait_ge(y_ready, post.count())
                    nc.vector.tensor_tensor(o[:, :, :], s[:, mid.slot, :, :], e[:, :, :], ALU.mult).then_inc(o_ready, 1)
                    dve.wait_ge(o2_ready, mid.count())
                    link(nc.vector.tensor_reduce(out=ssum[:, :, :], in_=o2[:, :, :].rearrange("p n (h v) -> p n h v", v=RV),
                                                 op=ALU.add, axis=AXX))
                    nc.vector.tensor_scalar(ssum[:, :, :], ssum[:, :, :], 1.0 / RV, 1e-5, ALU.mult, ALU.add).then_inc(ss_ready, 1)
                    dve.wait_ge(eg_ready, mid.count())
                    nc.vector.tensor_tensor(o[:, :, :], o[:, :, :], eg[:, :, :], ALU.mult).then_inc(oe_ready, 1)
                    link.end()
                if post:
                    dve.wait_ge(wo_ps, post.count())
                    dve.wait_ge(xt_loaded, post.count(16))
                    dve.wait_ge(stored, post.count(16))
                    nc.vector.tensor_tensor(xn[:, :, :], ps[:, WO + post.slot, :].rearrange("p (n d) -> p n d", n=NT), xt[:, :, :],
                                            ALU.add).then_inc(xn_ready, 1)

            pipelined(dve, body)

        @block.tensor
        def _(pe):
            pe.wait_ge(wo_ready, 1)
            pe.wait_ge(consts_ready, 1)

            def body(post, mid, pre):
                if mid:
                    pe.wait_ge(loaded[mid.slot], mid.slot_count(NL * 16))
                    if post:
                        pe.wait_ge(eg_ready, post.count())
                    for tb in range(NT):
                        last = nc.tensor.matmul(ps[:, tb, :], zT[:, mid.slot, tb * P:(tb + 1) * P], wg[:, :], start=True, stop=True)
                    last.then_inc(g_ps, 1)
                if post:
                    pe.wait_ge(y_ready, post.count())
                    for tb in range(NT):
                        if tb >= 2:
                            pe.wait_ge(oT_ready, post.count(NT, tb - 1))
                        for c in range(NVT):
                            last = nc.tensor.transpose(ps[:, OT + tb % 2, c * P:(c + 1) * P],
                                                       y[:, post.slot, tb, c * P:(c + 1) * P], ident[:, :])
                        last.then_inc(oT_ps, 1)
                        pe.wait_ge(oT_ready, post.count(NT, tb + 1))
                        for c in range(NVT):
                            last = nc.tensor.matmul(ps[:, WO + post.slot, tb * P:(tb + 1) * P], oT[:, tb % 2, c * P:(c + 1) * P],
                                                    wo[:, c, :], start=(c == 0), stop=(c == NVT - 1))
                    last.then_inc(wo_ps, 1)

            pipelined(pe, body)


def hybrid(nc, ins, out):
    def scratch(name, shape, dt=F32):
        return nc.dram_tensor(name, shape, dt).ap()

    def layer(prefix):
        return {name[len(prefix):]: ap for name, ap in ins.items() if name.startswith(prefix)}
    x1, x2, x3 = (scratch(f"x{n}", [B, T, DM]) for n in (1, 2, 3))
    zt_d = scratch("zt_d", [P, B, PAD + T])
    chunks = T // TCH + 2
    k_d, q_d, d_d = (scratch(n, [chunks, P, G * TCH]) for n in ("k_d", "q_d", "d_d"))
    v_d = scratch("v_d", [PARTS * HH, T + 2 * TCH, B * J, RV], BF16)
    sq_d = scratch("sq_d", [P, T, RV])
    a, b, f = layer("L0_attn_a_"), layer("L0_attn_b_"), layer("L0_ffn_")
    state_space(nc, a["x"], x1, a)
    feed_forward(nc, "f1_", x1, x2, f)
    normalised_columns(nc, x2, zt_d)
    projections(nc, zt_d, k_d, q_d, d_d, v_d, b)
    recurrence(nc, k_d, q_d, d_d, v_d, sq_d)
    outputs(nc, x2, x3, zt_d, sq_d, b)
    feed_forward(nc, "f2_", x3, out, f)


def kernel(**inputs):
    import numpy as _np
    import concourse.bacc as _bacc
    from concourse import mybir as _mybir
    from concourse.bass_utils import run_bass_kernel_spmd as _run

    column = {"L0_attn_a_conv_b", "L0_attn_a_b_dt", "L0_attn_a_D", "L0_ffn_gamma1", "L0_ffn_gamma2"}
    row = {"L0_ffn_bq", "L0_ffn_bup", "L0_ffn_bo", "L0_ffn_bg"}
    turned = {"L0_attn_b_" + n for n in ("Wq", "Wk", "Wv", "Wa", "Wg", "Wo")}
    taps = {"L0_attn_b_" + n for n in ("q_conv_w", "k_conv_w", "v_conv_w")}
    by_half = {"L0_attn_b_A_log", "L0_attn_b_dt_bias"}
    nc = _bacc.Bacc("TRN2", target_bir_lowering=False, num_devices=1)
    arrays, ins = {}, {}
    for name, value in inputs.items():
        a = _np.asarray(value)
        if name in column:
            a = a.reshape(-1, 128).T
        elif name in row:
            a = a.reshape(1, -1)
        elif name in ("L0_ffn_bdown", "L0_attn_b_o_norm_w"):
            a = a.reshape(-1, 1)
        elif name in turned:
            a = a.T
        elif name in taps:
            a = a[:, 0, :].T
        elif name in by_half:
            a = a.reshape(2, 4).T
        a = _np.ascontiguousarray(a)
        arrays[f"in_{name}"] = a
        ins[name] = nc.dram_tensor(f"in_{name}", a.shape, _mybir.dt.from_np(a.dtype), kind="ExternalInput").ap()
    out = nc.dram_tensor("out_x", (16, 512, 128), _mybir.dt.float32, kind="ExternalOutput").ap()
    hybrid(nc, ins, out)
    r = _run(nc, [arrays], core_ids=[0])
    return r.results[0]["out_x"]
```
